# Optimizing a Trainium2 kernel written in Bass

```python
import numpy as np
import jax
import jax.numpy as jnp

def _softmax(x, axis=-1):
    return jax.nn.softmax(x, axis=axis)

def _gelu(x):
    return jax.nn.gelu(x, approximate=True)

def _silu(x):
    return jax.nn.silu(x)

def _sigmoid(x):
    return jax.nn.sigmoid(x)

def _layernorm(x, axis=-1, eps=1e-05):
    m = jnp.mean(x, axis=axis, keepdims=True)
    v = jnp.var(x, axis=axis, keepdims=True)
    return (x - m) / jnp.sqrt(v + eps)

def _scatter_add(tgt, idx, src, axis=0):
    return tgt.at[idx].add(src)

def _segment_sum(src, seg, n):
    return jax.ops.segment_sum(src, seg, n)
kernel_name = 'mk_seq_preln_d1_jaxref_r8_666251'

def setup_inputs(seed: int=0):
    np.random.seed(seed)
    _w = jnp.asarray

    def _L0_attn_setup():
        import jax, jax.numpy as jnp
        import numpy as np
        B, S, E = (4, 256, 128)
        H, KVH = (16, 4)
        D = E // H
        QL, KVL = (64, 32)
        ROPE_BASE = 10000.0

        def _rope(x):
            d = x.shape[-1]
            inv_freq = 1.0 / ROPE_BASE ** (jnp.arange(0, d, 2, dtype=jnp.float32) / d)
            t = jnp.arange(x.shape[1], dtype=jnp.float32)
            freqs = jnp.outer(t, inv_freq)
            cos = jnp.cos(freqs)[None, :, None, :].astype(x.dtype)
            sin = jnp.sin(freqs)[None, :, None, :].astype(x.dtype)
            x1, x2 = (x[..., ::2], x[..., 1::2])
            r1 = x1 * cos - x2 * sin
            r2 = x1 * sin + x2 * cos
            return jnp.stack([r1, r2], axis=-1).reshape(x.shape)
        key = jax.random.key(seed)
        ks = jax.random.split(key, 7)
        s = 0.02
        return {'x': jax.random.normal(ks[0], (B, S, E), dtype=jnp.float32), 'Wqa': jax.random.normal(ks[1], (E, QL), dtype=jnp.float32) * s, 'Wqb': jax.random.normal(ks[2], (QL, E), dtype=jnp.float32) * s, 'Wkva': jax.random.normal(ks[3], (E, KVL), dtype=jnp.float32) * s, 'Wkvb': jax.random.normal(ks[4], (KVL, KVH * D * 2), dtype=jnp.float32) * s, 'Wout': jax.random.normal(ks[5], (E, E), dtype=jnp.float32) * s, 'bout': jax.random.normal(ks[6], (E,), dtype=jnp.float32) * s}
    _L0_attn_in = _L0_attn_setup()

    def _L0_ffn_setup():
        import jax, jax.numpy as jnp
        import numpy as np
        B, S, D_MODEL, D_FF, E, R, TOP_K = (4, 256, 128, 512, 8, 16, 2)
        key = jax.random.key(seed)
        ks = jax.random.split(key, 9)
        sd = 1.0 / np.sqrt(D_MODEL)
        return {'hidden_states': jax.random.normal(ks[0], (B, S, D_MODEL), jnp.float32), 'wi': jax.random.normal(ks[1], (D_FF, D_MODEL), jnp.float32) * sd, 'bi': jax.random.normal(ks[2], (D_FF,), jnp.float32) * 0.01, 'wo': jax.random.normal(ks[3], (D_MODEL, D_FF), jnp.float32) * (1.0 / np.sqrt(D_FF)), 'bo': jax.random.normal(ks[4], (D_MODEL,), jnp.float32) * 0.01, 'lora_A': jax.random.normal(ks[5], (E, R, D_MODEL), jnp.float32) * sd, 'lora_B': jax.random.normal(ks[6], (E, D_FF, R), jnp.float32) * 0.02, 'gate_w': jax.random.normal(ks[7], (E, D_MODEL), jnp.float32) * sd, 'gate_b': jax.random.normal(ks[8], (E,), jnp.float32) * 0.01}
    _L0_ffn_in = _L0_ffn_setup()
    _d = {'L0_attn_x': _L0_attn_in['x'], 'L0_attn_Wqa': _L0_attn_in['Wqa'], 'L0_attn_Wqb': _L0_attn_in['Wqb'], 'L0_attn_Wkva': _L0_attn_in['Wkva'], 'L0_attn_Wkvb': _L0_attn_in['Wkvb'], 'L0_attn_Wout': _L0_attn_in['Wout'], 'L0_attn_bout': _L0_attn_in['bout'], 'L0_ffn_wi': _L0_ffn_in['wi'], 'L0_ffn_bi': _L0_ffn_in['bi'], 'L0_ffn_wo': _L0_ffn_in['wo'], 'L0_ffn_bo': _L0_ffn_in['bo'], 'L0_ffn_lora_A': _L0_ffn_in['lora_A'], 'L0_ffn_lora_B': _L0_ffn_in['lora_B'], 'L0_ffn_gate_w': _L0_ffn_in['gate_w'], 'L0_ffn_gate_b': _L0_ffn_in['gate_b']}
    _x0 = _d['L0_attn_x']
    _d['L0_attn_x'] = jax.random.normal(jax.random.fold_in(jax.random.key(seed), 1), (4, 512, 128), dtype=_x0.dtype)
    del _x0
    return _d

def reference(L0_attn_x, L0_attn_Wqa, L0_attn_Wqb, L0_attn_Wkva, L0_attn_Wkvb, L0_attn_Wout, L0_attn_bout, L0_ffn_wi, L0_ffn_bi, L0_ffn_wo, L0_ffn_bo, L0_ffn_lora_A, L0_ffn_lora_B, L0_ffn_gate_w, L0_ffn_gate_b):

    def _L0_attn_ref(x, Wqa, Wqb, Wkva, Wkvb, Wout, bout):
        import jax, jax.numpy as jnp
        import numpy as np
        B, S, E = (4, 256, 128)
        H, KVH = (16, 4)
        D = E // H
        QL, KVL = (64, 32)
        ROPE_BASE = 10000.0

        def _rope(x):
            d = x.shape[-1]
            inv_freq = 1.0 / ROPE_BASE ** (jnp.arange(0, d, 2, dtype=jnp.float32) / d)
            t = jnp.arange(x.shape[1], dtype=jnp.float32)
            freqs = jnp.outer(t, inv_freq)
            cos = jnp.cos(freqs)[None, :, None, :].astype(x.dtype)
            sin = jnp.sin(freqs)[None, :, None, :].astype(x.dtype)
            x1, x2 = (x[..., ::2], x[..., 1::2])
            r1 = x1 * cos - x2 * sin
            r2 = x1 * sin + x2 * cos
            return jnp.stack([r1, r2], axis=-1).reshape(x.shape)
        b, s, _ = x.shape
        scale = D ** (-0.5)
        q = (x @ Wqa @ Wqb).reshape(b, s, H, D)
        kv = (x @ Wkva @ Wkvb).reshape(b, s, KVH, D, 2)
        k, v = (kv[..., 0], kv[..., 1])
        q = _rope(q)
        k = _rope(k)
        g = H // KVH
        k = jnp.repeat(k, g, axis=2)
        v = jnp.repeat(v, g, axis=2)
        scores = jnp.einsum('bqhd,bkhd->bhqk', q, k) * scale
        causal = jnp.triu(jnp.ones((s, s), dtype=bool), k=1)
        scores = jnp.where(causal[None, None], -jnp.inf, scores)
        w = jax.nn.softmax(scores, axis=-1)
        out = jnp.einsum('bhqk,bkhd->bqhd', w, v).reshape(b, s, E)
        return out @ Wout + bout

    def _L0_ffn_ref(hidden_states, wi, bi, wo, bo, lora_A, lora_B, gate_w, gate_b):
        import jax, jax.numpy as jnp
        import numpy as np
        B, S, D_MODEL, D_FF, E, R, TOP_K = (4, 256, 128, 512, 8, 16, 2)
        logits = jnp.einsum('bsd,ed->bse', hidden_states, gate_w) + gate_b
        scores = jax.nn.softmax(logits, axis=-1)
        top_v, top_i = jax.lax.top_k(scores, TOP_K)
        val_sum = top_v.sum(axis=-1)
        out = jnp.zeros_like(hidden_states)
        for e in range(E):
            count = (top_i == e).sum(axis=-1).astype(hidden_states.dtype)
            gate = count * val_sum
            inter = jnp.einsum('bsd,fd->bsf', hidden_states, wi) + bi + jnp.einsum('bsr,fr->bsf', jnp.einsum('bsd,rd->bsr', hidden_states, lora_A[e]), lora_B[e])
            h = jax.nn.relu(inter)
            expert_out = jnp.einsum('bsf,df->bsd', h, wo) + bo
            out = out + gate[..., None] * expert_out
        return out
    x = L0_attn_x
    x = x + _L0_attn_ref(_layernorm(x, axis=-1), L0_attn_Wqa, L0_attn_Wqb, L0_attn_Wkva, L0_attn_Wkvb, L0_attn_Wout, L0_attn_bout)
    x = x + _L0_ffn_ref(_layernorm(x, axis=-1), L0_ffn_wi, L0_ffn_bi, L0_ffn_wo, L0_ffn_bo, L0_ffn_lora_A, L0_ffn_lora_B, L0_ffn_gate_w, L0_ffn_gate_b)
    return x

_drawn_inputs = setup_inputs


def setup_inputs(seed=0):
    import zlib

    import numpy as np

    out = dict(_drawn_inputs(seed))
    spreads = {}
    factors = {'L0_attn_Wqa': 8.0,
     'L0_attn_Wqb': 8.0,
     'L0_attn_Wkva': 8.0,
     'L0_attn_Wkvb': 8.0,
     'L0_attn_Wout': 8.0,
     'L0_ffn_bi': 8.0,
     'L0_ffn_bo': 6.452,
     'L0_ffn_gate_b': 29.636,
     'L0_attn_bout': 5.313}
    for name, (base, spread) in spreads.items():
        noise = np.random.default_rng([zlib.crc32(name.encode()), seed]).standard_normal(out[name].shape)
        drawn = base * np.exp(spread * noise) if base else spread * noise
        out[name] = jnp.asarray(drawn.astype(out[name].dtype))
    for name, factor in factors.items():
        out[name] = (out[name] * factor).astype(out[name].dtype)
    return out
```

```python
from contextlib import ExitStack

import concourse.bass as bass
from concourse import mybir

ALU = mybir.AluOpType
ACT = mybir.ActivationFunctionType
AX = mybir.AxisListType
F32 = mybir.dt.float32
BF16 = mybir.dt.bfloat16

P = 128
LN_EPS = 1e-5
MASKED = -1e30

SLOTS = 8
MAX_ROW = 48

NPOS = 11
MAX_AT = [(0, 1), (2, 3), (4,), (5, 6), (7,), (8, 9), (10,), (), (), (), ()]
MAX_UNITS = 11
EXP_UNITS = 10
RELU_AT = [(2, 1), (2, 3), (2, 7), (2, 9)]
HIDDEN_AT = [(2, 4), (2, 6), (2, 10), (3, 1)]
SETUP = 13


def max_place(k):
    if k == 0:
        return 0, 0, 4, P
    if k < 3:
        return 1, 2 * (k - 1), 2, 2 * P
    if k < 7:
        return 2, k - 3, 1, 3 * P
    return 3, k - 7, 1, 4 * P


def exp_place(k):
    if k < 4:
        return [(k, 0, 0)]
    if k < 8:
        return [(k - 4, 1, 0), (k - 4, 3, 3 * P)]
    return [(2 * (k - 8), 2, 0), (2 * (k - 8) + 1, 2, 2 * P)]


def bass_preln_attention_moe_lora(nc: bass.Bass, x, w_q, w_kv, w_big, rows, tables, y):
    B, _, T, E = x.shape
    S = T * P
    D = 8
    H = E // D
    G = 4
    HG = H // G
    HK = H + G
    QL = w_q.shape[0]
    KVL = w_kv.shape[0]
    NE = 8
    R = P // NE
    FC = 4
    QKV = (HK + G) * D
    SCALE = float(D) ** -0.5
    assert S == 512 and E == P and HG == 4 and T == 4

    with ExitStack() as ctx:
        def sb(name, shape, dt=F32):
            return ctx.enter_context(nc.sbuf_tensor(name, shape, dt))

        def sem(name):
            return ctx.enter_context(nc.semaphore(name))

        wq_in = sb("wq_in", [QL, 2 * P])
        wkv_in = sb("wkv_in", [KVL, P + 2 * G * D])
        wbig = sb("wbig", [P, w_big.shape[1]])
        o = 0
        wi_t = wbig[:, o:o + FC * P].rearrange("p (c f) -> p c f", c=FC); o += FC * P
        lb_t = wbig[:, o:o + FC * P].rearrange("p (c f) -> p c f", c=FC); o += FC * P
        wo_t = wbig[:, o:o + FC * P].rearrange("p (c d) -> p c d", c=FC); o += FC * P
        la_t = wbig[:, o:o + P]; o += P
        gate_t = wbig[:, o:o + NE]; o += NE
        wout = wbig[:, o:o + P]; o += P
        bi = wbig[:, o:o + FC]; o += FC
        row_sb = sb("row_sb", [P, 2 * E + NE])
        bout_row, bo_row, gate_b_row = row_sb[:, 0:E], row_sb[:, E:2 * E], row_sb[:, 2 * E:2 * E + NE]
        tab_sb = sb("tab_sb", [P, 2 * T * D + NE])
        cos_t = tab_sb[:, 0:T * D].rearrange("p (t o d) -> p t o d", t=T, o=1)
        sin_t = tab_sb[:, T * D:2 * T * D].rearrange("p (t o d) -> p t o d", t=T, o=1)
        rank_row = tab_sb[:, 2 * T * D:2 * T * D + NE]
        wqkv = sb("wqkv", [P, QKV])
        neg_bi = sb("neg_bi", [P, FC])
        out_const = sb("out_const", [P, E])
        ident_f = sb("ident_f", [P, P])
        ident_b = sb("ident_b", [P, P], BF16)
        mask_b = sb("mask_b", [P, HG, P], BF16)
        neg_half = sb("neg_half", [P, T])

        x_sb = sb("x_sb", [P, T, E])
        st1 = sb("st1", [P, T, 6])
        mv1 = sb("mv1", [P, T, 2])
        ve1 = sb("ve1", [P, T])
        rstd1 = sb("rstd1", [P, T])
        xn1 = sb("xn1", [P, T, E])
        xn1_t = sb("xn1_t", [P, S])
        raw = sb("raw", [P, T, QKV])
        rot_a = sb("rot_a", [P, T, HK, D])
        rot_b = sb("rot_b", [P, T, HK, D])
        rq = sb("rq", [P, T * H, D])
        rk = sb("rk", [P, T * G, D])
        rest_q = sb("rest_q", [P, T * H, D])
        rest_k = sb("rest_k", [P, T * G, D])
        q_parts = sb("q_parts", [P, T * H, SLOTS * D], BF16)
        k_parts = sb("k_parts", [P, T * G, 2, SLOTS * D], BF16)

        q_t = sb("q_t", [P, G, 2, S], BF16)
        k_t = sb("k_t", [P, G, 2, S], BF16)
        v_aug = sb("v_aug", [P, T, G, 32])
        neg_max = sb("neg_max", [P, T, HG])
        max_rest = sb("max_rest", [P, T, HG])
        max_parts = sb("max_parts", [P, T, HG, 3], BF16)
        max_t = sb("max_t", [6, 2, S], BF16)
        probs = sb("probs", [P, 2, EXP_UNITS, S])
        o_sb = sb("o_sb", [P, S])
        rcp = sb("rcp", [P, T, HG])
        att = sb("att", [P, T, H, D])

        x_res = sb("x_res", [P, T, E])
        x_bias = sb("x_bias", [P, T, E])
        att_t = sb("att_t", [P, S])
        x1 = sb("x1", [P, T, E])
        st2 = sb("st2", [P, T, 6])
        mv2 = sb("mv2", [P, T, 2])
        ve2 = sb("ve2", [P, T])
        rstd2 = sb("rstd2", [P, T])
        xn2 = sb("xn2", [P, T, E])
        xn2_t = sb("xn2_t", [P, S])
        logit = sb("logit", [P, T, NE])
        lmax = sb("lmax", [P, T])
        ex = sb("ex", [P, T, NE])
        esum = sb("esum", [P, T])
        ersum = sb("ersum", [P, T])
        top1 = sb("top1", [P, T])
        top2 = sb("top2", [P, T])
        tsum = sb("tsum", [P, T])
        gate = sb("gate", [P, T])
        tie = sb("tie", [P, T, NE])
        tmax = sb("tmax", [P, T])
        hot1 = sb("hot1", [P, T, NE])
        hot2 = sb("hot2", [P, T, NE])
        hot_d = sb("hot_d", [P, T, NE])
        u1 = sb("u1", [P, T, NE, R])
        ud = sb("ud", [P, T, NE, R])
        u1_t = sb("u1_t", [P, S])
        ud_t = sb("ud_t", [P, S])
        relu1 = sb("relu1", [P, FC, S])
        hid = sb("hid", [P, FC, S])
        ffn = sb("ffn", [P, T, E])
        gated = sb("gated", [P, T, E])
        y_sb = sb("y_sb", [P, T, E])

        max_ps = ctx.enter_context(nc.psum_tensor("max_ps", [P, 2, S], F32))
        sc_ps = ctx.enter_context(nc.psum_tensor("sc_ps", [P, 2, S], F32))
        pv_ps = ctx.enter_context(nc.psum_tensor("pv_ps", [P, S], F32))
        a_ps = ctx.enter_context(nc.psum_tensor("a_ps", [P, S], F32))
        f_ps = ctx.enter_context(nc.psum_tensor("f_ps", [P, 2, S], F32))
        a_bf = a_ps[:, :].bitcast(BF16)

        small_in = sem("small_in")
        big_in = sem("big_in")
        x_in = sem("x_in")
        xres_in = sem("xres_in")
        y_out = sem("y_out")
        setup = sem("setup")
        wqkv_ps = sem("wqkv_ps")
        wqkv_done = sem("wqkv_done")
        const_ps = sem("const_ps")
        const_done = sem("const_done")
        a_full = sem("a_full")
        f_full = [sem("f_full0"), sem("f_full1")]
        passed = sem("passed")
        x1_done = sem("x1_done")
        logit_read = sem("logit_read")
        max_full = sem("max_full")
        max_done = sem("max_done")
        sc_full = sem("sc_full")
        exp_done = sem("exp_done")
        masked = sem("masked")
        pv_full = sem("pv_full")
        o_copied = sem("o_copied")
        att_done = sem("att_done")
        stats1 = sem("stats1")
        rstd1_done = sem("rstd1_done")
        xn1_done = sem("xn1_done")
        xn1t_done = sem("xn1t_done")
        raw_done = sem("raw_done")
        rope_done = sem("rope_done")
        v_done = sem("v_done")
        parts_done = sem("parts_done")
        qt_done = sem("qt_done")
        kt_done = sem("kt_done")
        max_parts_done = sem("max_parts_done")
        maxt_done = sem("maxt_done")
        max_rows_in = sem("max_rows_in")
        bias_added = sem("bias_added")
        att_t_done = sem("att_t_done")
        stats2 = sem("stats2")
        rstd2_done = sem("rstd2_done")
        xn2_done = sem("xn2_done")
        xn2t_done = sem("xn2t_done")
        logit_done = sem("logit_done")
        ex_done = sem("ex_done")
        u_done = sem("u_done")
        ut_done = sem("ut_done")
        relu_done = sem("relu_done")
        hid_done = sem("hid_done")
        ffn_done = sem("ffn_done")
        y_done = sem("y_done")
        c_prep = sem("c_prep")
        c_max = sem("c_max")
        c_att = sem("c_att")
        c_ffn = sem("c_ffn")
        c_pool = sem("c_pool")
        c_pool2 = sem("c_pool2")

        HEAD_START = [(stats2, 1), (hid_done, FC), (ffn_done, 1), (y_done, 1), (y_out, 16)]

        block = ctx.enter_context(nc.Block())

        def a_jobs(first, last):
            jobs = []
            for g in range(G):
                if not (last and g >= 2):
                    jobs += [("q_t", g), ("k_t", g)]
                if not (first and g == 0):
                    jobs.append(("out_t", g))
                if g == 0 and not last:
                    jobs += [("xn1_t", 0), ("qkv", 0)]
                if not (last and g == 3):
                    jobs.append(("max_t", g))
                if g == 0 and not last:
                    jobs.append(("qkv", 1))
            return jobs

        PRO_JOBS = [("xn1_t", 0), ("qkv", 0), ("qkv", 1), ("q_t", 0), ("k_t", 0), ("q_t", 1), ("k_t", 1), ("max_t", 0)]

        def a_index(b, name, g=0):
            if isinstance(b, int) and b < 0:
                return PRO_JOBS.index((name, g))
            if isinstance(b, int) and b == B:
                return (len(PRO_JOBS) + len(a_jobs(True, False)) + (B - 2) * len(a_jobs(False, False))
                        + len(a_jobs(False, True)))
            first, last = isinstance(b, int) and b == 0, isinstance(b, int) and b == B - 1
            k = a_jobs(first, last).index((name, g))
            if first:
                return len(PRO_JOBS) + k
            return (b - 1) * len(a_jobs(False, False)) + (len(PRO_JOBS) + len(a_jobs(True, False)) + k)

        def a_previous(b, name, g=0):
            if isinstance(b, int) and b < 0:
                k = PRO_JOBS.index((name, g))
                if k == 0:
                    return wqkv_done, 0
                before, at = PRO_JOBS[k - 1]
                group = {"q_t": at, "k_t": at, "max_t": 0}.get(before)
                return a_reader(before, group, 0, at)
            if isinstance(b, int) and b == B:
                return a_reader("out_t", 4 * B - 2, b, 0)
            jobs = a_jobs(isinstance(b, int) and b == 0, isinstance(b, int) and b == B - 1)
            k = jobs.index((name, g))
            if k == 0:
                return a_reader("max_t", 4 * b, b, 0)
            before, at = jobs[k - 1]
            group = 4 * b + at + {"q_t": 2, "k_t": 2, "out_t": -1, "max_t": 1}.get(before, 0)
            return a_reader(before, group, b + 1, at)

        def a_reader(name, group, batch, j):
            return {"q_t": (qt_done, group), "k_t": (kt_done, group), "out_t": (att_done, group),
                    "max_t": (maxt_done, group), "xn1_t": (xn1t_done, batch),
                    "qkv": (raw_done, batch)}[name][0], \
                   {"xn1_t": batch + 1, "qkv": 2 * batch + j + 1}.get(name, None if group is None else group + 1)

        F_USES = [["att_t", "xn2_t", "logit", "ud_t", "c1", "c1+", "c3", "c3+"],
                  ["x1", "u", "u1_t", "c0", "c0+", "c2", "c2+", "ffn"]]

        def f_use(b, name):
            bank = 0 if name in F_USES[0] else 1
            return bank, len(F_USES[bank]) * b + F_USES[bank].index(name)

        def f_previous(b, name):
            uses = F_USES[f_use(b, name)[0]]
            k = uses.index(name)
            if k == 0:
                b = b - 1
            before = uses[k - 1]
            if before[0] == "c":
                if before[-1] == "+":
                    return hid_done, FC * (b + 1) + int(before[1]) + 1
                return relu_done, FC * b + int(before[1]) + 1
            return {"att_t": (att_t_done, b + 1), "x1": (x1_done, b + 1), "xn2_t": (xn2t_done, b + 1),
                    "u": (u_done, b + 1), "logit": (logit_read, b + 1), "u1_t": (ut_done, 2 * b + 1),
                    "ud_t": (ut_done, 2 * b + 2), "ffn": (ffn_done, b + 2)}[before]

        def wait_from(eng, semaphore, value):
            if not (isinstance(value, int) and value <= 0):
                eng.wait_ge(semaphore, value)

        def wait_apart(eng, semaphore, value):
            eng.wait_ge(semaphore, value)
            if not isinstance(value, int):
                eng.sem_inc(passed, 1)

        @block.sync
        def _(sp):
            sp.dma_start(x_sb[:, :, :], x[0]).then_inc(x_in, 16)
            sp.dma_start(wq_in[:, :], w_q).then_inc(small_in, 16)
            sp.dma_start(wkv_in[:, :], w_kv).then_inc(small_in, 16)
            sp.dma_start(tab_sb[:, :], tables).then_inc(big_in, 16)
            sp.dma_start(wbig[:, :], w_big).then_inc(big_in, 16)
            sp.dma_start(row_sb[:, :], rows.to_broadcast([P, 2 * E + NE])).then_inc(big_in, 16)

            def load_x(b):
                wait_from(sp, xn1_done, b)
                sp.dma_start(x_sb[:, :, :], x[b]).then_inc(x_in, 16)

            def load_residual(b):
                wait_from(sp, bias_added, b)
                sp.dma_start(x_res[:, :, :], x[b]).then_inc(xres_in, 16)

            def max_rows(n, g):
                sp.wait_ge(maxt_done, n + 1)
                for c in range(2):
                    r = 64 * c + MAX_ROW
                    sp.dma_start(q_t[r:r + 3, g, :, :], max_t[3 * c:3 * c + 3, :, :]).then_inc(max_rows_in, 16)

            def store(b):
                sp.wait_ge(y_done, b + 2)
                sp.dma_start(y[b], y_sb[:, :, :]).then_inc(y_out, 16)

            def step(b, first=False, last=False):
                for g in range(G):
                    if g == 0 and not last:
                        load_x(b + 1)
                    if g == 1:
                        load_residual(b)
                    if not (last and g == 3):
                        max_rows(4 * b + g + 1, (g + 1) % G)
                    if g == 3 and not first:
                        store(b - 1)

            max_rows(0, 0)
            step(0, first=True)
            with sp.Fori(1, B - 1) as b:
                step(b)
            step(B - 1, last=True)
            store(B - 1)
            sp.wait_ge(y_out, 16 * (B + 1))

        @block.gpsimd
        def _(pool):
            n_setup = 0
            for semaphore, count in HEAD_START:
                pool.sem_inc(semaphore, count)

            def done(ins):
                nonlocal n_setup
                ins.then_inc(setup, 1)
                n_setup += 1

            done(nc.gpsimd.memset(ident_f[:, :], 0.0))
            done(nc.gpsimd.memset(ident_b[:, :], 0.0))
            done(nc.gpsimd.memset(mask_b[:, :, :], 0.0))
            done(nc.gpsimd.memset(neg_half[:, :], -0.5))
            done(nc.gpsimd.memset(q_parts[:, :, :], 0.0))
            done(nc.gpsimd.memset(k_parts[:, :, :, :], 0.0))
            done(nc.gpsimd.memset(k_t[:, :, :, :], 0.0))
            done(nc.gpsimd.memset(v_aug[:, :, :, :], 0.0))
            pool.wait_ge(setup, n_setup)
            for m in (ident_f, ident_b):
                done(nc.gpsimd.affine_select(out=m[:, :], in_=m[:, :], compare_op=ALU.not_equal, fill=1.0,
                                             base=0, pattern=[[-1, P]], channel_multiplier=1))
            done(nc.gpsimd.affine_select(out=mask_b[:, :, :], in_=mask_b[:, :, :], compare_op=ALU.is_ge, fill=MASKED,
                                         base=0, pattern=[[0, HG], [-1, P]], channel_multiplier=1))
            done(nc.gpsimd.memset(k_parts[:, :, :, MAX_ROW:MAX_ROW + 3], 1.0))
            done(nc.gpsimd.memset(v_aug[:, :, :, D:D + 1], 1.0))
            pool.wait_ge(setup, n_setup)
            assert n_setup == SETUP

            def rstd(stats, n, var, ve, out, chain, k, ready):
                wait_apart(pool, stats, n)
                nc.gpsimd.tensor_scalar(ve[:, :], var[:, :, 1], LN_EPS, None, ALU.add).then_inc(chain, 1)
                pool.wait_ge(chain, k)
                nc.gpsimd.tensor_tensor(out[:, :], ve[:, :], neg_half[:, :], ALU.pow).then_inc(ready, 1)

            def rstd1_of(b):
                rstd(stats1, b + 1, mv1, ve1, rstd1, c_pool, 2 * b + 1, rstd1_done)

            def rope(b):
                pool.wait_ge(raw_done, 2 * b + 2)
                wait_from(pool, parts_done, b)
                both = raw[:, :, 0:HK * D].rearrange("p t (h d) -> p t h d", d=D)
                nc.gpsimd.tensor_tensor(rot_a[:, :, :, :], both, cos_t.to_broadcast([P, T, HK, D]), ALU.mult)
                h = D // 2
                nc.gpsimd.tensor_tensor(rot_b[:, :, :, 0:h], both[:, :, :, h:D],
                                        sin_t[:, :, :, 0:h].to_broadcast([P, T, HK, h]), ALU.mult)
                nc.gpsimd.tensor_tensor(rot_b[:, :, :, h:D], both[:, :, :, 0:h],
                                        sin_t[:, :, :, h:D].to_broadcast([P, T, HK, h]), ALU.mult).then_inc(c_pool, 1)
                pool.wait_ge(c_pool, 2 * b + 2)
                nc.gpsimd.tensor_tensor(rq[:, :, :].rearrange("p (t h) d -> p t h d", t=T), rot_a[:, :, 0:H, :],
                                        rot_b[:, :, 0:H, :], ALU.add)
                nc.gpsimd.tensor_tensor(rk[:, :, :].rearrange("p (t h) d -> p t h d", t=T), rot_a[:, :, H:HK, :],
                                        rot_b[:, :, H:HK, :], ALU.add).then_inc(rope_done, 1)

            def values(b, g0, g1):
                wait_from(pool, pv_full, 4 * b + g1 - 4)
                wait_apart(pool, raw_done, 2 * b + 2)
                v = raw[:, :, HK * D:QKV].rearrange("p t (g d) -> p t g d", d=D)
                nc.gpsimd.tensor_copy(v_aug[:, :, g0:g1, 0:D], v[:, :, g0:g1, :]).then_inc(v_done, 1)

            def clear_later_keys(n, g, k):
                pr = probs[:, g % 2]
                units = [(4, 0, 4, 0), (8, 4, 8, 0), (8, 4, 8, 384), (10, 8, 10, None)]
                after, u0, u1_, col = units[k]
                wait_apart(pool, exp_done, EXP_UNITS * n + after)
                if col is None:
                    v = pr[:, u0:u1_, :].rearrange("p u (i q) -> p (u i) q", i=2)[:, :, 0:P]
                else:
                    v = pr[:, u0:u1_, col:col + P]
                nc.gpsimd.affine_select(out=v, in_=v, compare_op=ALU.is_ge, fill=0.0, base=0,
                                        pattern=[[0, 4], [1, P]], channel_multiplier=-1).then_inc(masked, 1)

            def add_out_bias(b):
                pool.wait_ge(xres_in, 16 * (b + 1))
                pool.wait_ge(stats2, b + 1)
                nc.gpsimd.tensor_tensor(x_bias[:, :, :], x_res[:, :, :],
                                        bout_row.rearrange("p (o d) -> p o d", o=1).to_broadcast([P, T, E]),
                                        ALU.add).then_inc(bias_added, 1)

            def finish(b):
                pool.wait_ge(ffn_done, b + 2)
                nc.gpsimd.tensor_tensor(gated[:, :, :], ffn[:, :, :],
                                        gate[:, :].rearrange("p (t o) -> p t o", o=1).to_broadcast([P, T, E]),
                                        ALU.mult).then_inc(c_pool2, 1)
                pool.wait_ge(c_pool2, 2 * b + 2)
                pool.wait_ge(y_out, 16 * (b + 1))
                nc.gpsimd.tensor_tensor(y_sb[:, :, :], gated[:, :, :], x1[:, :, :], ALU.add).then_inc(y_done, 1)

            def rstd2_of(b):
                rstd(stats2, b + 2, mv2, ve2, rstd2, c_pool2, 2 * b + 1, rstd2_done)

            def step(b, first=False, last=False):
                for g in range(G):
                    n = 4 * b + g
                    if g == 0 and not first:
                        add_out_bias(b - 1)
                    if g == 0 and not last:
                        rstd1_of(b + 1)
                    clear_later_keys(n, g, 0)
                    if g == 0 and not first:
                        values(b, 3, 4)
                    clear_later_keys(n, g, 1)
                    clear_later_keys(n, g, 2)
                    clear_later_keys(n, g, 3)
                    if g == 0 and not first:
                        rstd2_of(b - 1)
                    if g == 0 and not last:
                        rope(b + 1)
                    if g == 3 and not last:
                        values(b + 1, 0, 3)
                    if g == 3 and not first:
                        finish(b - 1)

            pool.wait_ge(big_in, 48)
            rstd1_of(0)
            rope(0)
            values(0, 0, 3)
            values(0, 3, 4)
            step(0, first=True)
            with pool.Fori(1, B - 1) as b:
                step(b)
            step(B - 1, last=True)
            add_out_bias(B - 1)
            rstd2_of(B - 1)
            finish(B - 1)

        @block.scalar
        def _(act):
            def a_read(b, name, g=0):
                act.wait_ge(a_full, a_index(b, name, g) + 1)

            def xn1_t_copy(b, step):
                a_read(step, "xn1_t")
                nc.scalar.activation(xn1_t[:, :], a_ps[:, :], ACT.Copy).then_inc(xn1t_done, 1)

            def raw_copy(b, step, j):
                a_read(step, "qkv", j)
                if j == 0:
                    wait_from(act, rope_done, b)
                    wait_from(act, v_done, 2 * b)
                nc.scalar.activation(raw[:, 2 * j:2 * j + 2, :],
                                     a_ps[:, 0:2 * QKV].rearrange("p (t c) -> p t c", t=2), ACT.Copy)\
                  .then_inc(raw_done, 1)

            def k_t_copy(n, step, slot, g):
                a_read(step, "k_t", slot)
                wait_from(act, sc_full, EXP_UNITS * (n - 3))
                nc.scalar.activation(k_t[0:64, g, 0, :], a_bf[0:64, 0:S], ACT.Copy)
                nc.scalar.activation(k_t[64:P, g, 1, :], a_bf[64:P, 0:S], ACT.Copy).then_inc(kt_done, 1)

            def max_t_copy(n, step, slot):
                a_read(step, "max_t", slot)
                wait_from(act, max_rows_in, 32 * n)
                nc.scalar.activation(max_t[:, :, :], a_bf[0:6, :].rearrange("p (a q) -> p a q", a=2), ACT.Copy)\
                  .then_inc(maxt_done, 1)

            def exp_unit(n, g, k):
                if k == 0:
                    wait_from(act, pv_full, n - 1)
                act.wait_ge(sc_full, EXP_UNITS * n + k + 1)
                nc.scalar.activation(probs[:, g % 2, k, :], sc_ps[:, k % 2, :], ACT.Exp, scale=SCALE)\
                  .then_inc(exp_done, 1)

            def o_copy(n):
                act.wait_ge(pv_full, n + 1)
                wait_from(act, att_done, n)
                nc.scalar.activation(o_sb[:, :], pv_ps[:, :], ACT.Copy).then_inc(o_copied, 1)

            def f_copy(b, name, out, ready):
                bank, k = f_use(b, name)
                act.wait_ge(f_full[bank], k + 1)
                nc.scalar.activation(out[:, :], f_ps[:, bank, :], ACT.Copy).then_inc(ready, 1)

            def router_exp(b):
                act.wait_ge(logit_done, b + 1)
                nc.scalar.activation(ex[:, :, :], logit[:, :, :], ACT.Exp).then_inc(ex_done, 1)

            def relu(b, c):
                bank, k = f_use(b, f"c{c}")
                act.wait_ge(f_full[bank], k + 1)
                act.wait_ge(hid_done, FC * (b + 1))
                nc.scalar.activation(relu1[:, c, :], f_ps[:, bank, :], ACT.Relu, bias=bi[:, c:c + 1])\
                  .then_inc(relu_done, 1)

            def ffn_task(b, g, p):
                if (g, p) == (0, 7):
                    f_copy(b, "att_t", att_t, att_t_done)
                if (g, p) == (1, 2):
                    f_copy(b, "xn2_t", xn2_t, xn2t_done)
                if (g, p) == (1, 4):
                    router_exp(b)
                if (g, p) == (1, 9):
                    f_copy(b, "u1_t", u1_t, ut_done)
                if (g, p) == (1, 10):
                    f_copy(b, "ud_t", ud_t, ut_done)
                if (g, p) in RELU_AT:
                    relu(b, RELU_AT.index((g, p)))

            def step(b, first=False, last=False):
                for g in range(G):
                    n = 4 * b + g
                    for p in range(NPOS):
                        if p < EXP_UNITS:
                            exp_unit(n, g, p)
                        if p == 1 and not (last and g >= 2):
                            k_t_copy(n + 2, b, g, (g + 2) % G)
                        if p == 4 and not (first and g == 0):
                            o_copy(n - 1)
                        if p == 6 and g == 0 and not last:
                            xn1_t_copy(b + 1, b)
                        if p == 7 and g == 0 and not last:
                            raw_copy(b + 1, b, 0)
                        if p == 8 and not (last and g == 3):
                            max_t_copy(n + 1, b, g)
                        if p == 9 and g == 0 and not last:
                            raw_copy(b + 1, b, 1)
                        if not first:
                            ffn_task(b - 1, g, p)

            act.wait_ge(big_in, 48)
            act.wait_ge(wqkv_ps, 1)
            nc.scalar.activation(wqkv[:, :], f_ps[:, 0, 0:QKV], ACT.Copy).then_inc(wqkv_done, 1)
            act.wait_ge(setup, SETUP)
            xn1_t_copy(0, -1)
            raw_copy(0, -1, 0)
            raw_copy(0, -1, 1)
            k_t_copy(0, -1, 0, 0)
            k_t_copy(1, -1, 1, 1)
            max_t_copy(0, -1, 0)
            step(0, first=True)
            with act.Fori(1, B - 1) as b:
                step(b)
            step(B - 1, last=True)
            o_copy(4 * B - 1)
            for g in range(G):
                for p in range(NPOS):
                    ffn_task(B - 1, g, p)

        @block.vector
        def _(dve):
            def norm_stats(xs, st, mv, chain, k, ready):
                for t in range(T):
                    last = nc.vector.bn_stats(st[:, t, :], xs[:, t, :])
                last.then_inc(chain, 1)
                wait_apart(dve, chain, k)
                for t in range(T):
                    last = nc.vector.bn_aggr(mv[:, t, :], st[:, t, :])
                last.then_inc(ready, 1)

            def normalise(xs, mv, rs, out, ready):
                for t in range(T):
                    last = nc.vector.tensor_scalar(out[:, t, :], xs[:, t, :], mv[:, t, 0:1], rs[:, t:t + 1],
                                                   ALU.subtract, ALU.mult)
                last.then_inc(ready, 1)

            PREP_CHAIN = 7

            def stats1_of(b):
                dve.wait_ge(x_in, 16 * (b + 1))
                norm_stats(x_sb, st1, mv1, c_prep, PREP_CHAIN * b + 1, stats1)

            def normalise1(b):
                dve.wait_ge(rstd1_done, b + 1)
                wait_from(dve, xn1t_done, b)
                normalise(x_sb, mv1, rstd1, xn1, xn1_done)

            def split(src, rest, parts_of, chain, k):
                h_out, m_out, l_out, h_one, m_one = parts_of
                nc.vector.tensor_copy(*h_out).then_inc(chain, 1)
                dve.wait_ge(chain, k + 1)
                nc.vector.tensor_tensor(rest, src, h_one, ALU.subtract).then_inc(chain, 1)
                dve.wait_ge(chain, k + 2)
                nc.vector.tensor_copy(*m_out).then_inc(chain, 1)
                dve.wait_ge(chain, k + 3)
                return nc.vector.tensor_tensor(l_out, rest, m_one, ALU.subtract)

            def split_q(b):
                dve.wait_ge(rope_done, b + 1)
                wait_from(dve, qt_done, 4 * b)
                s = q_parts[:, :, :].rearrange("p r (s d) -> p r s d", d=D)
                n = T * H
                q3 = rq[:, :, :].rearrange("p r (o d) -> p r o d", o=1)
                r3 = rest_q[:, :, :].rearrange("p r (o d) -> p r o d", o=1)
                split(rq[:, :, :], rest_q[:, :, :],
                      ((s[:, :, 0:3, :], q3.to_broadcast([P, n, 3, D])),
                       (s[:, :, 3:6:2, :], r3.to_broadcast([P, n, 2, D])),
                       s[:, :, 4, :], s[:, :, 0, :], s[:, :, 3, :]), c_prep, PREP_CHAIN * b + 1)

            def split_k(b):
                wait_from(dve, kt_done, 4 * b)
                n = T * G
                s = k_parts[:, :, :, :].rearrange("p r e (s d) -> p r e s d", d=D)
                k3 = rk[:, :, :].rearrange("p r (o d) -> p r o d", o=1)
                r3 = rest_k[:, :, :].rearrange("p r (o d) -> p r o d", o=1)
                k = PREP_CHAIN * b + 4
                for e in range(2):
                    last = nc.vector.tensor_copy(s[:, :, e, 2:5, :], k3.to_broadcast([P, n, 3, D]))
                last.then_inc(c_prep, 1)
                dve.wait_ge(c_prep, k + 1)
                nc.vector.tensor_tensor(rest_k[:, :, :], rk[:, :, :], s[:, :, 0, 2, :], ALU.subtract).then_inc(c_prep, 1)
                dve.wait_ge(c_prep, k + 2)
                for e in range(2):
                    last = nc.vector.tensor_copy(s[:, :, e, 0:6:5, :], r3.to_broadcast([P, n, 2, D]))
                last.then_inc(c_prep, 1)
                dve.wait_ge(c_prep, k + 3)
                for e in range(2):
                    last = nc.vector.tensor_tensor(s[:, :, e, 1, :], rest_k[:, :, :], s[:, :, e, 0, :], ALU.subtract)
                last.then_inc(parts_done, 1)

            def q_t_copy(n, step, slot, g):
                dve.wait_ge(a_full, a_index(step, "q_t", slot) + 1)
                wait_from(dve, sc_full, EXP_UNITS * (n - 3))
                nc.vector.tensor_copy(q_t[:, g, :, :].rearrange("p a q -> p (a q)"), a_bf[:, :])\
                  .then_inc(qt_done, 1)

            def max_unit(n, g, k):
                t, h0, nh, width = max_place(k)
                dve.wait_ge(max_full, MAX_UNITS * n + k + 1)
                if k == 0:
                    wait_from(dve, max_parts_done, n)
                src = max_ps[:, (g + k) % 2, 0:nh * width].rearrange("p (h k) -> p h k", h=nh)
                nc.vector.tensor_reduce(neg_max[:, t, h0:h0 + nh], src, AX.X, ALU.max, negate=True)\
                  .then_inc(max_done, 1)

            def split_max(n):
                dve.wait_ge(max_done, MAX_UNITS * (n + 1))
                wait_from(dve, maxt_done, n)
                nc.vector.tensor_copy(max_parts[:, :, :, 0], neg_max[:, :, :]).then_inc(c_max, 1)
                dve.wait_ge(c_max, 3 * n + 1)
                nc.vector.tensor_tensor(max_rest[:, :, :], neg_max[:, :, :], max_parts[:, :, :, 0], ALU.subtract)\
                  .then_inc(c_max, 1)
                dve.wait_ge(c_max, 3 * n + 2)
                nc.vector.tensor_copy(max_parts[:, :, :, 1], max_rest[:, :, :]).then_inc(c_max, 1)
                dve.wait_ge(c_max, 3 * n + 3)
                nc.vector.tensor_tensor(max_parts[:, :, :, 2], max_rest[:, :, :], max_parts[:, :, :, 1], ALU.subtract)\
                  .then_inc(max_parts_done, 1)

            def normalise_att(n, b, step, slot, g):
                dve.wait_ge(a_full, a_index(step, "out_t", slot) + 1)
                v = a_ps[:, :].rearrange("p (t h d) -> p t h d", t=T, h=HG)
                nc.vector.reciprocal(rcp[:, :, :], v[:, :, :, D]).then_inc(c_att, 1)
                dve.wait_ge(c_att, n + 1)
                if g == 0:
                    wait_from(dve, att_t_done, b)
                nc.vector.tensor_tensor(att[:, :, HG * g:HG * g + HG, :], v[:, :, :, 0:D],
                                        rcp[:, :, :].rearrange("p t (h o) -> p t h o", o=1)
                                        .to_broadcast([P, T, HG, D]), ALU.mult).then_inc(att_done, 1)

            FFN_CHAIN = 14

            def residual(b):
                bank, k = f_use(b, "x1")
                dve.wait_ge(f_full[bank], k + 1)
                dve.wait_ge(bias_added, b + 1)
                dve.wait_ge(y_done, b + 1)
                nc.vector.tensor_tensor(x1[:, :, :], f_ps[:, bank, :].rearrange("p (t d) -> p t d", t=T),
                                        x_bias[:, :, :], ALU.add).then_inc(x1_done, 1)
                dve.wait_ge(x1_done, b + 1)
                norm_stats(x1, st2, mv2, c_ffn, FFN_CHAIN * b + 1, stats2)

            def normalise2(b):
                dve.wait_ge(rstd2_done, b + 1)
                normalise(x1, mv2, rstd2, xn2, xn2_done)

            def over(a):
                return a[:, :].rearrange("p (t o) -> p t o", o=1).to_broadcast([P, T, NE])

            def router(b, stage):
                chain = FFN_CHAIN * b + stage

                def link(ins):
                    nonlocal chain
                    ins.then_inc(c_ffn, 1)
                    chain = chain + 1
                    dve.wait_ge(c_ffn, chain)

                rank = rank_row.rearrange("p (o e) -> p o e", o=1).to_broadcast([P, T, NE])
                if stage == 1:
                    bank, k = f_use(b, "logit")
                    dve.wait_ge(f_full[bank], k + 1)
                    nc.vector.tensor_tensor(logit[:, :, :], f_ps[:, bank, 0:T * NE].rearrange("p (t e) -> p t e", t=T),
                                            gate_b_row.rearrange("p (o e) -> p o e", o=1).to_broadcast([P, T, NE]),
                                            ALU.add).then_inc(logit_read, 1)
                    dve.wait_ge(logit_read, b + 1)
                    link(nc.vector.tensor_reduce(lmax[:, :], logit[:, :, :], AX.X, ALU.max))
                    nc.vector.tensor_tensor(logit[:, :, :], logit[:, :, :], over(lmax), ALU.subtract)\
                      .then_inc(logit_done, 1)
                if stage == 2:
                    dve.wait_ge(ex_done, b + 1)
                    nc.vector.tensor_reduce(esum[:, :], ex[:, :, :], AX.X, ALU.add)
                    link(nc.vector.tensor_reduce(top1[:, :], ex[:, :, :], AX.X, ALU.max))
                    nc.vector.reciprocal(ersum[:, :], esum[:, :])
                    link(nc.vector.tensor_tensor(tie[:, :, :], ex[:, :, :], over(top1), ALU.is_equal))
                    link(nc.vector.tensor_tensor(tie[:, :, :], tie[:, :, :], rank, ALU.mult))
                    link(nc.vector.tensor_reduce(tmax[:, :], tie[:, :, :], AX.X, ALU.max))
                    link(nc.vector.tensor_tensor(hot1[:, :, :], tie[:, :, :], over(tmax), ALU.is_equal))
                    link(nc.vector.scalar_tensor_tensor(out=ex[:, :, :], in0=hot1[:, :, :], scalar=-2.0,
                                                        in1=ex[:, :, :], op0=ALU.mult, op1=ALU.add))
                    link(nc.vector.tensor_reduce(top2[:, :], ex[:, :, :], AX.X, ALU.max))
                    link(nc.vector.tensor_tensor(tie[:, :, :], ex[:, :, :], over(top2), ALU.is_equal))
                    nc.vector.tensor_tensor(tsum[:, :], top1[:, :], top2[:, :], ALU.add)
                    link(nc.vector.tensor_tensor(tie[:, :, :], tie[:, :, :], rank, ALU.mult))
                    link(nc.vector.tensor_reduce(tmax[:, :], tie[:, :, :], AX.X, ALU.max))
                    dve.wait_ge(y_done, b + 1)
                    nc.vector.tensor_tensor(gate[:, :], tsum[:, :], ersum[:, :], ALU.mult)
                    link(nc.vector.tensor_tensor(hot2[:, :, :], tie[:, :, :], over(tmax), ALU.is_equal))
                    link(nc.vector.tensor_tensor(hot_d[:, :, :], hot2[:, :, :], hot1[:, :, :], ALU.subtract))
                    bank, k = f_use(b, "u")
                    dve.wait_ge(f_full[bank], k + 1)
                    u = f_ps[:, bank, :].rearrange("p (t e r) -> p t e r", t=T, e=NE)
                    for hot, out in ((hot1, u1), (hot_d, ud)):
                        last = nc.vector.tensor_tensor(out[:, :, :, :], u, hot[:, :, :].rearrange("p t (e o) -> p t e o", o=1)
                                                       .to_broadcast([P, T, NE, R]), ALU.mult)
                    last.then_inc(u_done, 1)

            def hidden(b, c):
                bank, k = f_use(b, f"c{c}+")
                dve.wait_ge(f_full[bank], k + 1)
                nc.vector.scalar_tensor_tensor(out=hid[:, c, :], in0=f_ps[:, bank, :], scalar=neg_bi[:, c:c + 1],
                                               in1=relu1[:, c, :], op0=ALU.max, op1=ALU.add).then_inc(hid_done, 1)

            def ffn_out(b):
                bank, k = f_use(b, "ffn")
                dve.wait_ge(f_full[bank], k + 1)
                dve.wait_ge(y_done, b + 1)
                nc.vector.tensor_tensor(ffn[:, :, :], f_ps[:, bank, :].rearrange("p (t d) -> p t d", t=T),
                                        out_const[:, :].rearrange("p (o d) -> p o d", o=1).to_broadcast([P, T, E]),
                                        ALU.add).then_inc(ffn_done, 1)

            def ffn_task(b, g, p):
                if (g, p) == (0, 9):
                    residual(b)
                if (g, p) == (1, 0):
                    normalise2(b)
                if (g, p) == (1, 4):
                    router(b, 1)
                if (g, p) == (1, 7):
                    router(b, 2)
                if (g, p) in HIDDEN_AT:
                    hidden(b, HIDDEN_AT.index((g, p)))
                if (g, p) == (3, 7):
                    ffn_out(b)

            def step(b, first=False, last=False):
                for g in range(G):
                    n = 4 * b + g
                    for p in range(NPOS):
                        if not (last and g == 3):
                            for k in MAX_AT[p]:
                                max_unit(n + 1, (g + 1) % G, k)
                        if p == 0 and not (last and g >= 2):
                            q_t_copy(n + 2, b, g, (g + 2) % G)
                        if g == 0 and not last:
                            if p == 2:
                                stats1_of(b + 1)
                            if p == 4:
                                normalise1(b + 1)
                        if p == 5 and not (first and g == 0):
                            normalise_att(n - 1, b if g else b - 1, b, g, (g - 1) % G)
                        if p == 7 and not (last and g == 3):
                            split_max(n + 1)
                        if g == 1 and not last:
                            if p == 9:
                                split_q(b + 1)
                            if p == 10:
                                split_k(b + 1)
                        if not first:
                            ffn_task(b - 1, g, p)

            dve.wait_ge(setup, SETUP)
            dve.wait_ge(big_in, 48)
            nc.vector.tensor_scalar(neg_bi[:, :], bi, -1.0, None, ALU.mult)
            stats1_of(0)
            normalise1(0)
            dve.wait_ge(const_ps, 1)
            nc.vector.scalar_tensor_tensor(out=out_const[:, :], in0=bo_row, scalar=2.0, in1=f_ps[:, 1, 0:E],
                                           op0=ALU.mult, op1=ALU.add).then_inc(const_done, 1)
            split_q(0)
            split_k(0)
            q_t_copy(0, -1, 0, 0)
            q_t_copy(1, -1, 1, 1)
            for k in range(MAX_UNITS):
                max_unit(0, 0, k)
            split_max(0)
            step(0, first=True)
            with dve.Fori(1, B - 1) as b:
                step(b)
            step(B - 1, last=True)
            normalise_att(4 * B - 1, B - 1, B, 0, 3)
            for g in range(G):
                for p in range(NPOS):
                    ffn_task(B - 1, g, p)

        @block.tensor
        def _(pe):
            def a_write(step, name, g=0):
                wait_from(pe, *a_previous(step, name, g))

            def xn1_transpose(b, step):
                a_write(step, "xn1_t")
                pe.wait_ge(xn1_done, b + 1)
                for t in range(T):
                    last = nc.tensor.transpose(a_ps[:, t * P:(t + 1) * P], xn1[:, t, :], ident_f[:, :])
                last.then_inc(a_full, 1)

            def project(b, step, j):
                a_write(step, "qkv", j)
                pe.wait_ge(xn1t_done, b + 1)
                for i in range(2):
                    t = 2 * j + i
                    last = nc.tensor.matmul(a_ps[:, i * QKV:(i + 1) * QKV], xn1_t[:, t * P:(t + 1) * P], wqkv[:, :],
                                            start=True, stop=True)
                last.then_inc(a_full, 1)

            def q_transpose(b, step, slot, g):
                a_write(step, "q_t", slot)
                pe.wait_ge(parts_done, b + 1)
                for pp in range(2):
                    for t in range(T):
                        h = t * H + HG * g + 2 * pp
                        last = nc.tensor.transpose(a_bf[:, pp * S + t * P:pp * S + (t + 1) * P],
                                                   q_parts[:, h:h + 2, :].rearrange("p h r -> p (h r)"), ident_b[:, :])
                last.then_inc(a_full, 1)

            def k_transpose(b, step, slot, g):
                a_write(step, "k_t", slot)
                for t in range(T):
                    last = nc.tensor.transpose(a_bf[:, t * P:(t + 1) * P],
                                               k_parts[:, t * G + g, :, :].rearrange("p e r -> p (e r)"), ident_b[:, :])
                last.then_inc(a_full, 1)

            def max_unit(n, g, k):
                t, h0, nh, width = max_place(k)
                if k == 0:
                    pe.wait_ge(qt_done, n + 1)
                    pe.wait_ge(kt_done, n + 1)
                wait_from(pe, max_done, MAX_UNITS * n + k - 1)
                bank = max_ps[:, (g + k) % 2, 0:nh * width].rearrange("p (h k) -> p h k", h=nh)
                for i in range(nh):
                    h = h0 + i
                    nc.tensor.matmul(bank[:, i, :], q_t[:, g, h // 2, t * P:(t + 1) * P], k_t[:, g, h % 2, 0:width],
                                     start=i == 0, stop=False, skip_group_check=True)
                nc.tensor.matmul(bank[:, :, width - P:width], ident_b[:, :], mask_b[:, 0:nh, :],
                                 start=False, stop=True, skip_group_check=True).then_inc(max_full, 1)

            def max_transpose(n, step, slot):
                a_write(step, "max_t", slot)
                pe.wait_ge(max_parts_done, n + 1)
                for pp in range(2):
                    for t in range(T):
                        last = nc.tensor.transpose(a_bf[0:6, pp * S + t * P:pp * S + (t + 1) * P],
                                                   max_parts[:, t, 2 * pp:2 * pp + 2, :].rearrange("p h c -> p (h c)"),
                                                   ident_b[:, :])
                last.then_inc(a_full, 1)

            def exp_unit(n, g, k):
                if k == 0:
                    pe.wait_ge(max_rows_in, 32 * (n + 1))
                wait_from(pe, exp_done, EXP_UNITS * n + k - 1)
                for h, j, col in exp_place(k):
                    last = nc.tensor.matmul(sc_ps[:, k % 2, col:col + S - j * P], k_t[:, g, h % 2, j * P:(j + 1) * P],
                                            q_t[:, g, h // 2, j * P:S], start=True, stop=True)
                last.then_inc(sc_full, 1)

            def weigh_values(n, b, g, k):
                j = (0, 1, 3, 2)[k]
                if k == 0:
                    wait_from(pe, o_copied, n)
                    pe.wait_ge(v_done, 2 * b + (2 if g == G - 1 else 1))
                pe.wait_ge(masked, 4 * n + k + 1)
                for h in range(HG):
                    unit, col = next((u, c) for u in range(EXP_UNITS) for hh, jj, c in exp_place(u) if (hh, jj) == (h, j))
                    last = nc.tensor.matmul(pv_ps[32 * h:32 * h + 32, j * P:S], v_aug[:, j, g, :],
                                            probs[:, g % 2, unit, col:col + S - j * P], start=k == 0, stop=k == 3,
                                            skip_group_check=True)
                if k == 3:
                    last.then_inc(pv_full, 1)

            def out_transpose(n, step, slot):
                a_write(step, "out_t", slot)
                pe.wait_ge(o_copied, n + 1)
                for t in range(T):
                    last = nc.tensor.transpose(a_ps[:, t * P:(t + 1) * P], o_sb[:, t * P:(t + 1) * P], ident_f[:, :])
                last.then_inc(a_full, 1)

            def f_write(b, name):
                bank, _ = f_use(b, name)
                pe.wait_ge(*f_previous(b, name))
                return bank

            def f_transpose(b, name, src, ready, value):
                bank = f_write(b, name)
                pe.wait_ge(ready, value)
                for t in range(T):
                    last = nc.tensor.transpose(f_ps[:, bank, t * P:(t + 1) * P], src(t), ident_f[:, :])
                last.then_inc(f_full[bank], 1)

            def token_major(b, name, lhs, rhs, width, ready, value):
                bank = f_write(b, name)
                pe.wait_ge(ready, value)
                for t in range(T):
                    last = nc.tensor.matmul(f_ps[:, bank, t * width:(t + 1) * width], lhs[:, t * P:(t + 1) * P], rhs,
                                            start=True, stop=True)
                last.then_inc(f_full[bank], 1)

            def first_expert(b, c):
                bank = f_write(b, f"c{c}")
                nc.tensor.matmul(f_ps[:, bank, :], wi_t[:, c, :], xn2_t[:, :], start=True, stop=False, skip_group_check=True)
                pe.wait_ge(ut_done, 2 * b + 1)
                nc.tensor.matmul(f_ps[:, bank, :], lb_t[:, c, :], u1_t[:, :], start=False, stop=False,
                                 skip_group_check=True).then_inc(f_full[bank], 1)

            def second_expert(b, c):
                bank = f_write(b, f"c{c}+")
                pe.wait_ge(ut_done, 2 * b + 2)
                nc.tensor.matmul(f_ps[:, bank, :], lb_t[:, c, :], ud_t[:, :], start=False, stop=True,
                                 skip_group_check=True).then_inc(f_full[bank], 1)

            def down(b, t):
                if t == 0:
                    f_write(b, "ffn")
                    pe.wait_ge(hid_done, FC * (b + 2))
                bank, _ = f_use(b, "ffn")
                for c in range(FC):
                    last = nc.tensor.matmul(f_ps[:, bank, t * P:(t + 1) * P], hid[:, c, t * P:(t + 1) * P],
                                            wo_t[:, c, :], start=c == 0, stop=c == FC - 1)
                if t == T - 1:
                    last.then_inc(f_full[bank], 1)

            def ffn_task(b, g, p):
                if (g, p) == (0, 7):
                    f_transpose(b, "att_t", lambda t: att[:, t, :, :].rearrange("p h d -> p (h d)"), att_done, 4 * (b + 1))
                if (g, p) == (0, 9):
                    token_major(b, "x1", att_t, wout, P, att_t_done, b + 1)
                if (g, p) == (1, 2):
                    f_transpose(b, "xn2_t", lambda t: xn2[:, t, :], xn2_done, b + 1)
                if (g, p) == (1, 4):
                    token_major(b, "logit", xn2_t, gate_t, NE, xn2t_done, b + 1)
                    token_major(b, "u", xn2_t, la_t, P, xn2t_done, b + 1)
                if (g, p) == (1, 9):
                    f_transpose(b, "u1_t", lambda t: u1[:, t, :, :].rearrange("p e r -> p (e r)"), u_done, b + 1)
                if (g, p) == (1, 10):
                    f_transpose(b, "ud_t", lambda t: ud[:, t, :, :].rearrange("p e r -> p (e r)"), u_done, b + 1)
                if (g, p) in RELU_AT:
                    first_expert(b, RELU_AT.index((g, p)))
                if (g, p) in HIDDEN_AT:
                    second_expert(b, HIDDEN_AT.index((g, p)))
                if g == 3 and 3 <= p < 3 + T:
                    down(b, p - 3)

            def step(b, first=False, last=False):
                for g in range(G):
                    n = 4 * b + g
                    for p in range(NPOS):
                        if not (last and g == 3):
                            for k in MAX_AT[p]:
                                max_unit(n + 1, (g + 1) % G, k)
                        if p < EXP_UNITS:
                            exp_unit(n, g, p)
                        if p < T and not (first and g == 0):
                            weigh_values(n - 1, b if g else b - 1, (g - 1) % G, p)
                        if not (last and g >= 2):
                            if p == 0:
                                q_transpose(b + (g >= 2), b, g, (g + 2) % G)
                            if p == 1:
                                k_transpose(b + (g >= 2), b, g, (g + 2) % G)
                        if g == 0 and not last:
                            if p == 6:
                                xn1_transpose(b + 1, b)
                            if p == 7:
                                project(b + 1, b, 0)
                        if p == 5 and not (first and g == 0):
                            out_transpose(n - 1, b, g)
                        if p == 8 and not (last and g == 3):
                            max_transpose(n + 1, b, g)
                        if p == 9 and g == 0 and not last:
                            project(b + 1, b, 1)
                        if not first:
                            ffn_task(b - 1, g, p)

            pe.wait_ge(small_in, 32)
            nc.tensor.matmul(f_ps[:, 0, 0:P], wq_in[:, 0:P], wq_in[:, P:2 * P], start=True, stop=True)
            nc.tensor.matmul(f_ps[:, 0, P:QKV], wkv_in[:, 0:P], wkv_in[:, P:P + QKV - P], start=True, stop=True)\
              .then_inc(wqkv_ps, 1)
            pe.wait_ge(setup, SETUP)
            pe.wait_ge(big_in, 48)
            for c in range(FC):
                last = nc.tensor.matmul(f_ps[:, 1, 0:E], bi[:, c:c + 1].to_broadcast([P, P]), wo_t[:, c, :],
                                        start=c == 0, stop=c == FC - 1)
            last.then_inc(const_ps, 1)
            xn1_transpose(0, -1)
            pe.wait_ge(wqkv_done, 1)
            project(0, -1, 0)
            project(0, -1, 1)
            for g in range(2):
                q_transpose(0, -1, g, g)
                k_transpose(0, -1, g, g)
            for k in range(MAX_UNITS):
                max_unit(0, 0, k)
            max_transpose(0, -1, 0)
            pe.wait_ge(const_done, 1)
            step(0, first=True)
            with pe.Fori(1, B - 1) as b:
                step(b)
            step(B - 1, last=True)
            for k in range(T):
                weigh_values(4 * B - 1, B - 1, G - 1, k)
            out_transpose(4 * B - 1, B, 0)
            for g in range(G):
                for p in range(NPOS):
                    ffn_task(B - 1, g, p)


def kernel(**inputs):
    import numpy as np
    import concourse.bacc as bacc
    from concourse.bass_utils import run_bass_kernel_spmd

    w = {k: np.asarray(v) for k, v in inputs.items()}
    x = w["L0_attn_x"]
    B, S, E = x.shape
    T = S // P
    G, D = 4, 8
    H = E // D
    NE, R, _ = w["L0_ffn_lora_A"].shape
    F = w["L0_ffn_wi"].shape[0]
    FC = F // P

    halves = np.array([2 * i + c for c in range(2) for i in range(D // 2)])
    q_cols = np.concatenate([h * D + halves for h in range(H)])
    k_cols = np.concatenate([(g * D + halves) * 2 for g in range(G)])
    v_cols = np.arange(G * D) * 2 + 1
    kv_cols = np.concatenate([k_cols, v_cols])

    inv_freq = (1.0 / np.float32(10000.0) ** (np.arange(0, D, 2, dtype=np.float32) / np.float32(D))).astype(np.float32)
    angle = np.outer(np.arange(S, dtype=np.float32), inv_freq).astype(np.float32)
    cos, sin = np.cos(angle).astype(np.float32), np.sin(angle).astype(np.float32)

    def by_token(a):
        return a.reshape(T, P, D).transpose(1, 0, 2).reshape(P, T * D)

    rank = np.tile(np.arange(NE, 0, -1, dtype=np.float32), (P, 1))
    arrays = {
        "x": x.reshape(B, T, P, E).transpose(0, 2, 1, 3),
        "w_q": np.concatenate([w["L0_attn_Wqa"].T, w["L0_attn_Wqb"][:, q_cols]], axis=1),
        "w_kv": np.concatenate([w["L0_attn_Wkva"].T, w["L0_attn_Wkvb"][:, kv_cols]], axis=1),
        "w_big": np.concatenate([
            w["L0_ffn_wi"].T,
            w["L0_ffn_lora_B"].transpose(0, 2, 1).reshape(NE * R, F),
            w["L0_ffn_wo"].T.reshape(FC, P, E).transpose(1, 0, 2).reshape(P, FC * E),
            w["L0_ffn_lora_A"].reshape(NE * R, E).T,
            w["L0_ffn_gate_w"].T,
            w["L0_attn_Wout"],
            w["L0_ffn_bi"].reshape(FC, P).T], axis=1),
        "rows": np.concatenate([w["L0_attn_bout"], w["L0_ffn_bo"], w["L0_ffn_gate_b"]])[None, :],
        "tables": np.concatenate([by_token(np.concatenate([cos, cos], axis=1)),
                                  by_token(np.concatenate([-sin, sin], axis=1)), rank], axis=1),
    }
    arrays = {k: np.ascontiguousarray(v) for k, v in arrays.items()}
    nc = bacc.Bacc("TRN2", target_bir_lowering=False, num_devices=1)
    args = [nc.dram_tensor(k, v.shape, mybir.dt.from_np(v.dtype), kind="ExternalInput").ap() for k, v in arrays.items()]
    y = nc.dram_tensor("y", (B, P, T, E), F32, kind="ExternalOutput").ap()
    bass_preln_attention_moe_lora(nc, *args, y)
    out = run_bass_kernel_spmd(nc, [arrays], core_ids=[0]).results[0]["y"]
    return out.reshape(B, P, T, E).transpose(0, 2, 1, 3).reshape(B, S, E)
```

```python
from contextlib import ExitStack

import concourse.bass as bass
from concourse import mybir

ALU = mybir.AluOpType
ACT = mybir.ActivationFunctionType
AX = mybir.AxisListType
F32 = mybir.dt.float32
BF16 = mybir.dt.bfloat16

P = 128
LN_EPS = 1e-5
MASKED = -1e30

SLOTS = 8
MAX_ROW = 48

NPOS = 11
MAX_UNITS = 11
EXP_UNITS = 10
MAX_LEAD = 6
BASE_AT = [(1, 8), (1, 9), (2, 9), (2, 10)]
FIRST_AT = [(2, 4), (2, 5), (2, 9), (2, 10)]
RELU_AT = [(2, 5), (2, 6), (2, 10), (3, 0)]
SECOND_AT = [(2, 7), (2, 7), (3, 0), (3, 1)]
HIDDEN_AT = [(2, 8), (2, 9), (3, 1), (3, 2)]
DOWN_AT = [(3, 3), (3, 4), (3, 5), (3, 6)]
SETUP_IDENT = 3
SETUP = 9


def max_at(n, g, p):
    if p < MAX_UNITS - MAX_LEAD:
        return n + 1, (g + 1) % 4, p + MAX_LEAD
    return n + 2, (g + 2) % 4, p - (MAX_UNITS - MAX_LEAD)


def max_place(k):
    if k == 0:
        return 0, 0, 4, P
    if k < 3:
        return 1, 2 * (k - 1), 2, 2 * P
    if k < 7:
        return 2, k - 3, 1, 3 * P
    return 3, k - 7, 1, 4 * P


def exp_place(k):
    if k < 4:
        return [(k, 0, 0)]
    if k < 8:
        return [(k - 4, 1, 0), (k - 4, 3, 3 * P)]
    return [(2 * (k - 8), 2, 0), (2 * (k - 8) + 1, 2, 2 * P)]


def bass_preln_attention_moe_lora(nc: bass.Bass, x, w_q, w_kv, w_big, rows, tables, y):
    B, _, T, E = x.shape
    S = T * P
    D = 8
    H = E // D
    G = 4
    HG = H // G
    HK = H + G
    QL = w_q.shape[0]
    KVL = w_kv.shape[0]
    NE = 8
    R = P // NE
    FC = 4
    QKV = (HK + G) * D
    SCALE = float(D) ** -0.5
    assert S == 512 and E == P and HG == 4 and T == 4

    with ExitStack() as ctx:
        def sb(name, shape, dt=F32):
            return ctx.enter_context(nc.sbuf_tensor(name, shape, dt))

        def sem(name):
            return ctx.enter_context(nc.semaphore(name))

        wq_in = sb("wq_in", [QL, 2 * P])
        wkv_in = sb("wkv_in", [KVL, P + 2 * G * D])
        wbig = sb("wbig", [P, w_big.shape[1]])
        o = 0
        wi_t = wbig[:, o:o + FC * P].rearrange("p (c f) -> p c f", c=FC); o += FC * P
        lb_t = wbig[:, o:o + FC * P].rearrange("p (c f) -> p c f", c=FC); o += FC * P
        wo_t = wbig[:, o:o + FC * P].rearrange("p (c d) -> p c d", c=FC); o += FC * P
        la_t = wbig[:, o:o + P]; o += P
        gate_t = wbig[:, o:o + NE]; o += NE
        wout = wbig[:, o:o + P]; o += P
        bi = wbig[:, o:o + FC]; o += FC
        row_sb = sb("row_sb", [P, 2 * E + NE])
        bout_row, bo_row, gate_b_row = row_sb[:, 0:E], row_sb[:, E:2 * E], row_sb[:, 2 * E:2 * E + NE]
        tab_sb = sb("tab_sb", [P, 2 * T * D + NE])
        cos_t = tab_sb[:, 0:T * D].rearrange("p (t o d) -> p t o d", t=T, o=1)
        sin_t = tab_sb[:, T * D:2 * T * D].rearrange("p (t o d) -> p t o d", t=T, o=1)
        rank_row = tab_sb[:, 2 * T * D:2 * T * D + NE]
        wqkv = sb("wqkv", [P, QKV])
        neg_bi = sb("neg_bi", [P, FC])
        out_const = sb("out_const", [P, E])
        ident_f = sb("ident_f", [P, P])
        ident_b = sb("ident_b", [P, P], BF16)
        mask_b = sb("mask_b", [P, HG, P], BF16)
        neg_half = sb("neg_half", [P, T])

        x_sb = sb("x_sb", [P, T, E])
        st1 = sb("st1", [P, T, 6])
        mv1 = sb("mv1", [P, T, 2])
        ve1 = sb("ve1", [P, T])
        rstd1 = sb("rstd1", [P, T])
        xn1 = sb("xn1", [P, T, E])
        xn1_t = sb("xn1_t", [P, S])
        raw = sb("raw", [P, T, QKV])
        rot_a = sb("rot_a", [P, T, HK, D])
        rot_b = sb("rot_b", [P, T, HK, D])
        rq = sb("rq", [P, T * H, D])
        rk = sb("rk", [P, T * G, D])
        rest_q = sb("rest_q", [P, T * H, D])
        rest_k = sb("rest_k", [P, T * G, D])
        q_parts = sb("q_parts", [P, T * H, SLOTS * D], BF16)
        k_parts = sb("k_parts", [P, T * G, 2, SLOTS * D], BF16)

        q_t = sb("q_t", [P, G, 2, S], BF16)
        k_t = sb("k_t", [P, G, 2, S], BF16)
        v_aug = sb("v_aug", [P, T, G, 32])
        neg_max = sb("neg_max", [P, T, HG])
        max_rest = sb("max_rest", [P, T, HG])
        max_parts = sb("max_parts", [P, T, HG, 3], BF16)
        max_t = sb("max_t", [6, 2, S], BF16)
        probs = sb("probs", [P, 2, EXP_UNITS, S])
        o_sb = sb("o_sb", [P, S])
        rcp = sb("rcp", [P, T, HG])
        att = sb("att", [P, T, H, D])

        x_res = sb("x_res", [P, T, E])
        x_bias = sb("x_bias", [P, T, E])
        att_t = sb("att_t", [P, S])
        x1 = sb("x1", [P, T, E])
        st2 = sb("st2", [P, T, 6])
        mv2 = sb("mv2", [P, T, 2])
        ve2 = sb("ve2", [P, T])
        rstd2 = sb("rstd2", [P, T])
        xn2 = sb("xn2", [P, T, E])
        xn2_t = sb("xn2_t", [P, S])
        logit = sb("logit", [P, T, NE])
        lmax = sb("lmax", [P, T])
        ex = sb("ex", [P, T, NE])
        esum = sb("esum", [P, T])
        ersum = sb("ersum", [P, T])
        top1 = sb("top1", [P, T])
        top2 = sb("top2", [P, T])
        tsum = sb("tsum", [P, T])
        gate = sb("gate", [P, T])
        tie = sb("tie", [P, T, NE])
        tmax = sb("tmax", [P, T])
        hot1 = sb("hot1", [P, T, NE])
        hot2 = sb("hot2", [P, T, NE])
        hot_d = sb("hot_d", [P, T, NE])
        u = sb("u", [P, S])
        u1 = sb("u1", [P, T, NE, R])
        ud = sb("ud", [P, T, NE, R])
        u1_t = sb("u1_t", [P, S])
        ud_t = sb("ud_t", [P, S])
        relu1 = sb("relu1", [P, FC, S])
        hid = sb("hid", [P, FC, S])
        ffn = sb("ffn", [P, T, E])
        gated = sb("gated", [P, T, E])
        y_sb = sb("y_sb", [P, T, E])

        max_ps = ctx.enter_context(nc.psum_tensor("max_ps", [P, 2, S], F32))
        sc_ps = ctx.enter_context(nc.psum_tensor("sc_ps", [P, 2, S], F32))
        pv_ps = ctx.enter_context(nc.psum_tensor("pv_ps", [P, S], F32))
        a_ps = ctx.enter_context(nc.psum_tensor("a_ps", [P, S], F32))
        f_ps = ctx.enter_context(nc.psum_tensor("f_ps", [P, 2, S], F32))
        a_bf = a_ps[:, :].bitcast(BF16)

        q_slots = q_parts[:, :, :].rearrange("p r (s d) -> p r s d", d=D)
        k_slots = k_parts[:, :, :, :].rearrange("p r e (s d) -> p r e s d", d=D)

        small_in = sem("small_in")
        tab_in = sem("tab_in")
        big_in = sem("big_in")
        x_in = sem("x_in")
        xres_in = sem("xres_in")
        y_out = sem("y_out")
        setup = sem("setup")
        cleared = sem("cleared")
        wqkv_ps = sem("wqkv_ps")
        wqkv_done = sem("wqkv_done")
        const_ps = sem("const_ps")
        const_done = sem("const_done")
        a_full = sem("a_full")
        f_full = [sem("f_full0"), sem("f_full1")]
        passed = sem("passed")
        x1_done = sem("x1_done")
        logit_read = sem("logit_read")
        u_copied = sem("u_copied")
        max_full = sem("max_full")
        max_done = sem("max_done")
        sc_full = sem("sc_full")
        exp_done = sem("exp_done")
        masked = sem("masked")
        pv_full = sem("pv_full")
        o_copied = sem("o_copied")
        att_done = sem("att_done")
        stats1 = sem("stats1")
        rstd1_done = sem("rstd1_done")
        xn1_done = sem("xn1_done")
        xn1t_done = sem("xn1t_done")
        raw_done = sem("raw_done")
        rope_done = sem("rope_done")
        v_done = sem("v_done")
        parts_done = sem("parts_done")
        qt_done = sem("qt_done")
        kt_done = sem("kt_done")
        max_parts_done = sem("max_parts_done")
        maxt_done = sem("maxt_done")
        max_rows_in = sem("max_rows_in")
        bias_added = sem("bias_added")
        att_t_done = sem("att_t_done")
        stats2 = sem("stats2")
        rstd2_done = sem("rstd2_done")
        xn2_done = sem("xn2_done")
        xn2t_done = sem("xn2t_done")
        logit_done = sem("logit_done")
        ex_done = sem("ex_done")
        hot_done = sem("hot_done")
        u_done = sem("u_done")
        ut_done = sem("ut_done")
        relu_done = sem("relu_done")
        hid_done = sem("hid_done")
        ffn_done = sem("ffn_done")
        y_done = sem("y_done")
        high_done = sem("high_done")
        rest_done = sem("rest_done")
        mid_done = sem("mid_done")
        c_prep = sem("c_prep")
        c_rotate = sem("c_rotate")
        c_max = sem("c_max")
        c_att = sem("c_att")
        c_ffn = sem("c_ffn")
        c_pool = sem("c_pool")
        c_pool2 = sem("c_pool2")

        HEAD_START = [(stats2, 1), (hid_done, FC), (ffn_done, 1), (y_done, 1), (y_out, 16)]

        block = ctx.enter_context(nc.Block())

        def a_jobs(first, last):
            jobs = []
            for g in range(G):
                if not (last and g >= 2):
                    jobs += [("q_t", g), ("k_t", g)]
                if g == 2 and not first:
                    jobs += [("u1_t", 0), ("ud_t", 0)]
                if g > 0 and not (last and g == 3):
                    jobs.append(("max_t", g))
                if not (first and g == 0):
                    jobs.append(("out_t", g))
                if g == 0:
                    jobs.append(("max_t", g))
            return jobs

        PRO_JOBS = [("q_t", 0), ("k_t", 0), ("q_t", 1), ("k_t", 1), ("max_t", 0)]
        LAST_JOBS = [("out_t", 0), ("u1_t", 0), ("ud_t", 0)]

        def a_index(b, name, g=0):
            if isinstance(b, int) and b < 0:
                return PRO_JOBS.index((name, g))
            if isinstance(b, int) and b == B:
                return a_index(B - 1, "out_t", 3) + 1 + LAST_JOBS.index((name, g))
            first, last = isinstance(b, int) and b == 0, isinstance(b, int) and b == B - 1
            k = a_jobs(first, last).index((name, g))
            if first:
                return len(PRO_JOBS) + k
            return (b - 1) * len(a_jobs(False, False)) + (len(PRO_JOBS) + len(a_jobs(True, False)) + k)

        def a_previous(b, name, g=0):
            if isinstance(b, int) and b < 0:
                k = PRO_JOBS.index((name, g))
                if k == 0:
                    return qt_done, 0
                return a_reader(*PRO_JOBS[k - 1])
            if isinstance(b, int) and b == B:
                k = LAST_JOBS.index((name, g))
                return [a_reader("out_t", 4 * B - 2), a_reader("out_t", 4 * B - 1), (ut_done, 2 * B - 1)][k]
            jobs = a_jobs(isinstance(b, int) and b == 0, isinstance(b, int) and b == B - 1)
            k = jobs.index((name, g))
            if k == 0:
                return a_reader("out_t", 4 * b - 2) if not isinstance(b, int) or b else a_reader("max_t", 0)
            before, at = jobs[k - 1]
            if before in ("u1_t", "ud_t"):
                return ut_done, 2 * b - 1 if before == "u1_t" else 2 * b
            return a_reader(before, 4 * b + at + {"q_t": 2, "k_t": 2, "out_t": -1, "max_t": 1}[before])

        def a_reader(name, group):
            return {"q_t": qt_done, "k_t": kt_done, "out_t": att_done, "max_t": maxt_done}[name], group + 1

        F_PREP = [["xn1_t", "qkv1"], ["qkv0"]]
        F_FFN = [["x1", "xn2_t", "logit", "c0", "c0+", "c2", "c2+"],
                 ["att_t", "u", "c1", "c1+", "c3", "c3+", "ffn"]]

        def f_bank(name):
            return 0 if name in F_PREP[0] + F_FFN[0] else 1

        def f_use(b, name):
            bank = f_bank(name)
            if name in F_PREP[bank]:
                ffns = 0 if isinstance(b, int) and b < 2 else b - 2
                preps, k = b, F_PREP[bank].index(name)
            else:
                ffns, k = b, F_FFN[bank].index(name)
                preps = min(b + 3, B) if isinstance(b, int) else b + 3
            return bank, len(F_FFN[bank]) * ffns + (len(F_PREP[bank]) * preps + k)

        def f_previous(b, name):
            bank = f_bank(name)
            if name in F_PREP[bank]:
                k = F_PREP[bank].index(name)
                if k > 0:
                    return [f_reader(b, F_PREP[bank][k - 1])]
                if isinstance(b, int) and b == 0:
                    return []
                if isinstance(b, int) and b == 1:
                    return [f_reader(0, F_PREP[bank][-1])]
                return [f_reader(b - 1, F_PREP[bank][-1]), f_reader(b - 3, F_FFN[bank][-1])]
            k = F_FFN[bank].index(name)
            if k > 0:
                return [f_reader(b, F_FFN[bank][k - 1])]
            if isinstance(b, int) and b + 2 >= B:
                return [f_reader(b - 1, F_FFN[bank][-1])]
            return [f_reader(b + 2, F_PREP[bank][-1])]

        def f_reader(b, name):
            if name[0] == "c":
                if name[-1] == "+":
                    return hid_done, FC * (b + 1) + int(name[1]) + 1
                return relu_done, FC * b + int(name[1]) + 1
            return {"xn1_t": (xn1t_done, b + 1), "qkv0": (raw_done, 2 * b + 1), "qkv1": (raw_done, 2 * b + 2),
                    "att_t": (att_t_done, b + 1), "x1": (x1_done, b + 1), "xn2_t": (xn2t_done, b + 1),
                    "u": (u_copied, b + 1), "logit": (logit_read, b + 1), "ffn": (ffn_done, b + 2)}[name]

        def wait_from(eng, semaphore, value):
            if not (isinstance(value, int) and value <= 0):
                eng.wait_ge(semaphore, value)

        def wait_apart(eng, semaphore, value):
            eng.wait_ge(semaphore, value)
            if not isinstance(value, int):
                eng.sem_inc(passed, 1)

        def rotation(t0, t1):
            both = raw[:, t0:t1, 0:HK * D].rearrange("p t (h d) -> p t h d", d=D)
            a, b, cos, sin = (v[:, t0:t1] for v in (rot_a, rot_b, cos_t, sin_t))
            n, h = t1 - t0, D // 2
            return [(a, both, cos.to_broadcast([P, n, HK, D])),
                    (b[:, :, :, 0:h], both[:, :, :, h:D], sin[:, :, :, 0:h].to_broadcast([P, n, HK, h])),
                    (b[:, :, :, h:D], both[:, :, :, 0:h], sin[:, :, :, h:D].to_broadcast([P, n, HK, h]))]

        def rotation_sums(t0, t1):
            return [(rq[:, t0 * H:t1 * H, :].rearrange("p (t h) d -> p t h d", h=H),
                     rot_a[:, t0:t1, 0:H, :], rot_b[:, t0:t1, 0:H, :]),
                    (rk[:, t0 * G:t1 * G, :].rearrange("p (t h) d -> p t h d", h=G),
                     rot_a[:, t0:t1, H:HK, :], rot_b[:, t0:t1, H:HK, :])]

        @block.sync
        def _(sp):
            sp.dma_start(x_sb[:, :, :], x[0]).then_inc(x_in, 16)
            sp.dma_start(wq_in[:, :], w_q).then_inc(small_in, 16)
            sp.dma_start(wkv_in[:, :], w_kv).then_inc(small_in, 16)
            sp.dma_start(tab_sb[:, :], tables).then_inc(tab_in, 16)
            sp.dma_start(wbig[:, :], w_big).then_inc(big_in, 16)
            sp.dma_start(row_sb[:, :], rows.to_broadcast([P, 2 * E + NE])).then_inc(big_in, 16)

            def load_x(b):
                wait_from(sp, xn1_done, b)
                sp.dma_start(x_sb[:, :, :], x[b]).then_inc(x_in, 16)

            def load_residual(b):
                wait_from(sp, bias_added, b)
                sp.dma_start(x_res[:, :, :], x[b]).then_inc(xres_in, 16)

            def max_rows(n, g):
                sp.wait_ge(maxt_done, n + 1)
                for c in range(2):
                    r = 64 * c + MAX_ROW
                    sp.dma_start(q_t[r:r + 3, g, :, :], max_t[3 * c:3 * c + 3, :, :]).then_inc(max_rows_in, 16)

            def store(b):
                sp.wait_ge(y_done, b + 2)
                sp.dma_start(y[b], y_sb[:, :, :]).then_inc(y_out, 16)

            def step(b, first=False, last=False, load=True):
                for g in range(G):
                    if g == 1:
                        load_residual(b)
                        if load:
                            load_x(b + 2)
                    if not (last and g == 3):
                        max_rows(4 * b + g + 1, (g + 1) % G)
                    if g == 3 and not first:
                        store(b - 1)

            load_x(1)
            max_rows(0, 0)
            step(0, first=True)
            with sp.Fori(1, B - 2) as b:
                step(b)
            step(B - 2, load=False)
            step(B - 1, last=True, load=False)
            store(B - 1)
            sp.wait_ge(y_out, 16 * (B + 1))

        @block.gpsimd
        def _(pool):
            n_setup = 0
            for semaphore, count in HEAD_START:
                pool.sem_inc(semaphore, count)

            def done(ins):
                nonlocal n_setup
                ins.then_inc(setup, 1)
                n_setup += 1

            done(nc.gpsimd.memset(ident_f[:, :], 0.0))
            done(nc.gpsimd.memset(neg_half[:, :], -0.5))
            pool.wait_ge(setup, 2)
            done(nc.gpsimd.affine_select(out=ident_f[:, :], in_=ident_f[:, :], compare_op=ALU.not_equal, fill=1.0,
                                         base=0, pattern=[[-1, P]], channel_multiplier=1))
            assert n_setup == SETUP_IDENT

            def setup_others():
                for m in (ident_b, mask_b):
                    done(nc.gpsimd.memset(m[:], 0.0))
                pool.wait_ge(setup, SETUP_IDENT + 2)
                done(nc.gpsimd.affine_select(out=ident_b[:, :], in_=ident_b[:, :], compare_op=ALU.not_equal, fill=1.0,
                                             base=0, pattern=[[-1, P]], channel_multiplier=1))
                done(nc.gpsimd.affine_select(out=mask_b[:, :, :], in_=mask_b[:, :, :], compare_op=ALU.is_ge, fill=MASKED,
                                             base=0, pattern=[[0, HG], [-1, P]], channel_multiplier=1))
                done(nc.gpsimd.memset(v_aug[:, :, :, D + 1:32], 0.0))
                done(nc.gpsimd.memset(v_aug[:, :, :, D:D + 1], 1.0))
                assert n_setup == SETUP

            def rstd(stats, n, var, ve, out, chain, k, ready):
                wait_apart(pool, stats, n)
                nc.gpsimd.tensor_scalar(ve[:, :], var[:, :, 1], LN_EPS, None, ALU.add).then_inc(chain, 1)
                pool.wait_ge(chain, k)
                nc.gpsimd.tensor_tensor(out[:, :], ve[:, :], neg_half[:, :], ALU.pow).then_inc(ready, 1)

            def rstd1_of(b):
                rstd(stats1, b + 1, mv1, ve1, rstd1, c_pool, 2 * b if not isinstance(b, int) or b else 1, rstd1_done)

            def rotate_products(b):
                pool.wait_ge(raw_done, 2 * b + 2)
                for out, in0, in1 in rotation(0, T):
                    last = nc.gpsimd.tensor_tensor(out, in0, in1, ALU.mult)
                last.then_inc(c_pool, 1)

            def rotate_sums(b):
                pool.wait_ge(c_pool, 2 * b + 1)
                pool.wait_ge(parts_done, 2 * b)
                for out, in0, in1 in rotation_sums(0, T):
                    last = nc.gpsimd.tensor_tensor(out, in0, in1, ALU.add)
                last.then_inc(rope_done, 1)

            def split_rests(b):
                pool.wait_ge(high_done, 2 * b + 1)
                nc.gpsimd.tensor_tensor(rest_q[:, :, :], rq[:, :, :], q_slots[:, :, 0, :], ALU.subtract)\
                  .then_inc(rest_done, 1)
                pool.wait_ge(high_done, 2 * b + 2)
                nc.gpsimd.tensor_tensor(rest_k[:, :, :], rk[:, :, :], k_slots[:, :, 0, 2, :], ALU.subtract)\
                  .then_inc(rest_done, 1)

            def values(b, g0, g1):
                wait_from(pool, pv_full, 4 * b + g1 - 4)
                wait_apart(pool, raw_done, 2 * b + 2)
                v = raw[:, :, HK * D:QKV].rearrange("p t (g d) -> p t g d", d=D)
                nc.gpsimd.tensor_copy(v_aug[:, :, g0:g1, 0:D], v[:, :, g0:g1, :]).then_inc(v_done, 1)

            def clear_later_keys(n, g, k):
                pr = probs[:, g % 2]
                units = [(4, 0, 4, 0), (8, 4, 8, 0), (8, 4, 8, 384), (10, 8, 10, None)]
                after, u0, u1_, col = units[k]
                wait_apart(pool, exp_done, EXP_UNITS * n + after)
                if col is None:
                    v = pr[:, u0:u1_, :].rearrange("p u (i q) -> p (u i) q", i=2)[:, :, 0:P]
                else:
                    v = pr[:, u0:u1_, col:col + P]
                nc.gpsimd.affine_select(out=v, in_=v, compare_op=ALU.is_ge, fill=0.0, base=0,
                                        pattern=[[0, 4], [1, P]], channel_multiplier=-1).then_inc(masked, 1)

            def add_out_bias(b):
                pool.wait_ge(xres_in, 16 * (b + 1))
                pool.wait_ge(big_in, 32)
                pool.wait_ge(stats2, b + 1)
                nc.gpsimd.tensor_tensor(x_bias[:, :, :], x_res[:, :, :],
                                        bout_row.rearrange("p (o d) -> p o d", o=1).to_broadcast([P, T, E]),
                                        ALU.add).then_inc(bias_added, 1)

            def rstd2_of(b):
                rstd(stats2, b + 2, mv2, ve2, rstd2, c_pool2, b + 1, rstd2_done)

            def step(b, first=False, last=False):
                for g in range(G):
                    n = 4 * b + g
                    if g == 0 and not last:
                        rstd1_of(b + 1)
                    if g == 1 and not first:
                        rstd2_of(b - 1)
                    if g == 1 and not last:
                        rotate_sums(b + 1)
                    clear_later_keys(n, g, 0)
                    if g == 0 and not first:
                        values(b, 3, 4)
                        add_out_bias(b - 1)
                    if g == 1 and not last:
                        split_rests(b + 1)
                    clear_later_keys(n, g, 1)
                    clear_later_keys(n, g, 2)
                    if g == 0 and not last:
                        rotate_products(b + 1)
                    clear_later_keys(n, g, 3)
                    if g == 3 and not last:
                        values(b + 1, 0, 3)

            rstd1_of(0)
            setup_others()
            pool.wait_ge(tab_in, 16)
            values(0, 0, 3)
            values(0, 3, 4)
            step(0, first=True)
            with pool.Fori(1, B - 1) as b:
                step(b)
            step(B - 1, last=True)
            add_out_bias(B - 1)
            rstd2_of(B - 1)

        @block.scalar
        def _(act):
            def a_read(b, name, g=0):
                act.wait_ge(a_full, a_index(b, name, g) + 1)

            def raw_copy(b, j):
                bank, k = f_use(b, f"qkv{j}")
                act.wait_ge(f_full[bank], k + 1)
                if j == 0:
                    wait_from(act, rope_done, b)
                    wait_from(act, v_done, 2 * b)
                nc.scalar.activation(raw[:, 2 * j:2 * j + 2, :],
                                     f_ps[:, bank, 0:2 * QKV].rearrange("p (t c) -> p t c", t=2), ACT.Copy)\
                  .then_inc(raw_done, 1)

            def k_t_copy(n, step, slot, g):
                a_read(step, "k_t", slot)
                wait_from(act, sc_full, EXP_UNITS * (n - 3))
                nc.scalar.activation(k_t[0:64, g, 0, :], a_bf[0:64, 0:S], ACT.Copy)
                nc.scalar.activation(k_t[64:P, g, 1, :], a_bf[64:P, 0:S], ACT.Copy).then_inc(kt_done, 1)

            def max_t_copy(n, step, slot):
                a_read(step, "max_t", slot)
                wait_from(act, max_rows_in, 32 * n)
                nc.scalar.activation(max_t[:, :, :], a_bf[0:6, :].rearrange("p (a q) -> p a q", a=2), ACT.Copy)\
                  .then_inc(maxt_done, 1)

            def exp_unit(n, g, k):
                if k == 0:
                    wait_from(act, pv_full, n - 1)
                act.wait_ge(sc_full, EXP_UNITS * n + k + 1)
                nc.scalar.activation(probs[:, g % 2, k, :], sc_ps[:, k % 2, :], ACT.Exp, scale=SCALE)\
                  .then_inc(exp_done, 1)

            def o_copy(n):
                act.wait_ge(pv_full, n + 1)
                wait_from(act, att_done, n)
                nc.scalar.activation(o_sb[:, :], pv_ps[:, :], ACT.Copy).then_inc(o_copied, 1)

            def f_copy(b, name, out, ready):
                bank, k = f_use(b, name)
                act.wait_ge(f_full[bank], k + 1)
                nc.scalar.activation(out[:, :], f_ps[:, bank, :], ACT.Copy).then_inc(ready, 1)

            def a_copy(b, name, out):
                a_read(b + 1, name)
                nc.scalar.activation(out[:, :], a_ps[:, :], ACT.Copy).then_inc(ut_done, 1)

            def router_exp(b):
                act.wait_ge(logit_done, b + 1)
                nc.scalar.activation(ex[:, :, :], logit[:, :, :], ACT.Exp).then_inc(ex_done, 1)

            def relu(b, c):
                bank, k = f_use(b, f"c{c}")
                act.wait_ge(f_full[bank], k + 1)
                act.wait_ge(hid_done, FC * (b + 1))
                nc.scalar.activation(relu1[:, c, :], f_ps[:, bank, :], ACT.Relu, bias=bi[:, c:c + 1])\
                  .then_inc(relu_done, 1)

            def ffn_task(b, g, p):
                if (g, p) == (1, 4):
                    f_copy(b, "xn2_t", xn2_t, xn2t_done)
                if (g, p) == (1, 7):
                    router_exp(b)
                if (g, p) == (1, 6):
                    f_copy(b, "u", u, u_copied)
                if (g, p) == (2, 3):
                    a_copy(b, "u1_t", u1_t)
                if (g, p) == (2, 5):
                    a_copy(b, "ud_t", ud_t)
                if (g, p) in RELU_AT:
                    relu(b, RELU_AT.index((g, p)))

            def step(b, first=False, last=False):
                for g in range(G):
                    n = 4 * b + g
                    for p in range(NPOS):
                        if p == (7 if g or first else 8) and not (last and g == 3):
                            max_t_copy(n + 1, b, g)
                        if p == 2 and not (last and g >= 2):
                            k_t_copy(n + 2, b, g, (g + 2) % G)
                        if p < EXP_UNITS:
                            exp_unit(n, g, p)
                        if g == 0 and p == 5 and not last:
                            f_copy(b + 1, "xn1_t", xn1_t, xn1t_done)
                        if p == 4 and not (first and g == 0):
                            o_copy(n - 1)
                        if g == 0 and not last:
                            if p == 7:
                                raw_copy(b + 1, 0)
                            if p == 8:
                                raw_copy(b + 1, 1)
                        if not first:
                            ffn_task(b - 1, g, p)

            act.wait_ge(wqkv_ps, 1)
            nc.scalar.activation(wqkv[:, :], max_ps[:, 0, 0:QKV], ACT.Copy).then_inc(wqkv_done, 1)
            f_copy(0, "xn1_t", xn1_t, xn1t_done)
            raw_copy(0, 0)
            raw_copy(0, 1)
            act.wait_ge(cleared, 1)
            k_t_copy(0, -1, 0, 0)
            k_t_copy(1, -1, 1, 1)
            max_t_copy(0, -1, 0)
            act.wait_ge(big_in, 32)
            step(0, first=True)
            with act.Fori(1, B - 1) as b:
                step(b)
            step(B - 1, last=True)
            o_copy(4 * B - 1)
            for g in range(G):
                for p in range(NPOS):
                    ffn_task(B - 1, g, p)

        @block.vector
        def _(dve):
            def norm_stats(xs, st, mv, chain, k, ready):
                for t in range(T):
                    last = nc.vector.bn_stats(st[:, t, :], xs[:, t, :])
                last.then_inc(chain, 1)
                wait_apart(dve, chain, k)
                for t in range(T):
                    last = nc.vector.bn_aggr(mv[:, t, :], st[:, t, :])
                last.then_inc(ready, 1)

            def normalise(xs, mv, rs, out, tiles, ready):
                for t in tiles:
                    last = nc.vector.tensor_scalar(out[:, t, :], xs[:, t, :], mv[:, t, 0:1], rs[:, t:t + 1],
                                                   ALU.subtract, ALU.mult)
                if t == T - 1:
                    last.then_inc(ready, 1)

            def stats1_of(b):
                dve.wait_ge(x_in, 16 * (b + 1))
                norm_stats(x_sb, st1, mv1, c_prep, b + 1, stats1)

            def normalise1(b, half):
                dve.wait_ge(rstd1_done, b + 1)
                wait_from(dve, xn1t_done, b)
                normalise(x_sb, mv1, rstd1, xn1, range(2 * half, 2 * half + 2), xn1_done)

            def rotate_first(j):
                dve.wait_ge(raw_done, j + 1)
                dve.wait_ge(tab_in, 16)
                for out, in0, in1 in rotation(2 * j, 2 * j + 2):
                    last = nc.vector.tensor_tensor(out, in0, in1, ALU.mult)
                last.then_inc(c_rotate, 1)
                dve.wait_ge(c_rotate, j + 1)
                for out, in0, in1 in rotation_sums(2 * j, 2 * j + 2):
                    last = nc.vector.tensor_tensor(out, in0, in1, ALU.add)
                if j == 1:
                    last.then_inc(rope_done, 1)

            def high_q(b):
                dve.wait_ge(rope_done, b + 1)
                wait_from(dve, qt_done, 4 * b)
                nc.vector.tensor_copy(q_slots[:, :, 0:3, :], rq[:, :, :].rearrange("p r (o d) -> p r o d", o=1)
                                      .to_broadcast([P, T * H, 3, D])).then_inc(high_done, 1)

            def high_k(b):
                wait_from(dve, kt_done, 4 * b)
                for e in range(2):
                    last = nc.vector.tensor_copy(k_slots[:, :, e, 2:5, :], rk[:, :, :].rearrange("p r (o d) -> p r o d", o=1)
                                                 .to_broadcast([P, T * G, 3, D]))
                last.then_inc(high_done, 1)

            def rests_first():
                dve.wait_ge(high_done, 1)
                nc.vector.tensor_tensor(rest_q[:, :, :], rq[:, :, :], q_slots[:, :, 0, :], ALU.subtract).then_inc(rest_done, 1)
                dve.wait_ge(high_done, 2)
                nc.vector.tensor_tensor(rest_k[:, :, :], rk[:, :, :], k_slots[:, :, 0, 2, :], ALU.subtract).then_inc(rest_done, 1)

            def mid_q(b):
                dve.wait_ge(rest_done, 2 * b + 1)
                nc.vector.tensor_copy(q_slots[:, :, 3:6:2, :], rest_q[:, :, :].rearrange("p r (o d) -> p r o d", o=1)
                                      .to_broadcast([P, T * H, 2, D])).then_inc(mid_done, 1)

            def mid_k(b):
                dve.wait_ge(rest_done, 2 * b + 2)
                for e in range(2):
                    last = nc.vector.tensor_copy(k_slots[:, :, e, 0:6:5, :], rest_k[:, :, :].rearrange("p r (o d) -> p r o d", o=1)
                                                 .to_broadcast([P, T * G, 2, D]))
                last.then_inc(mid_done, 1)

            def low_q(b):
                dve.wait_ge(mid_done, 2 * b + 1)
                nc.vector.tensor_tensor(q_slots[:, :, 4, :], rest_q[:, :, :], q_slots[:, :, 3, :], ALU.subtract)\
                  .then_inc(parts_done, 1)

            def low_k(b):
                dve.wait_ge(mid_done, 2 * b + 2)
                for e in range(2):
                    last = nc.vector.tensor_tensor(k_slots[:, :, e, 1, :], rest_k[:, :, :], k_slots[:, :, e, 0, :], ALU.subtract)
                last.then_inc(parts_done, 1)

            def q_t_copy(n, step, slot, g):
                dve.wait_ge(a_full, a_index(step, "q_t", slot) + 1)
                wait_from(dve, sc_full, EXP_UNITS * (n - 3))
                nc.vector.tensor_copy(q_t[:, g, :, :].rearrange("p a q -> p (a q)"), a_bf[:, :])\
                  .then_inc(qt_done, 1)

            def max_unit(n, g, k):
                t, h0, nh, width = max_place(k)
                dve.wait_ge(max_full, MAX_UNITS * n + k + 1)
                if k == 0:
                    wait_from(dve, max_parts_done, n)
                src = max_ps[:, (g + k) % 2, 0:nh * width].rearrange("p (h k) -> p h k", h=nh)
                nc.vector.tensor_reduce(neg_max[:, t, h0:h0 + nh], src, AX.X, ALU.max, negate=True)\
                  .then_inc(max_done, 1)

            def split_max(n):
                dve.wait_ge(max_done, MAX_UNITS * (n + 1))
                wait_from(dve, maxt_done, n)
                nc.vector.tensor_copy(max_parts[:, :, :, 0], neg_max[:, :, :]).then_inc(c_max, 1)
                dve.wait_ge(c_max, 3 * n + 1)
                nc.vector.tensor_tensor(max_rest[:, :, :], neg_max[:, :, :], max_parts[:, :, :, 0], ALU.subtract)\
                  .then_inc(c_max, 1)
                dve.wait_ge(c_max, 3 * n + 2)
                nc.vector.tensor_copy(max_parts[:, :, :, 1], max_rest[:, :, :]).then_inc(c_max, 1)
                dve.wait_ge(c_max, 3 * n + 3)
                nc.vector.tensor_tensor(max_parts[:, :, :, 2], max_rest[:, :, :], max_parts[:, :, :, 1], ALU.subtract)\
                  .then_inc(max_parts_done, 1)

            def normalise_att(n, b, step, slot, g):
                dve.wait_ge(a_full, a_index(step, "out_t", slot) + 1)
                v = a_ps[:, :].rearrange("p (t h d) -> p t h d", t=T, h=HG)
                nc.vector.reciprocal(rcp[:, :, :], v[:, :, :, D]).then_inc(c_att, 1)
                dve.wait_ge(c_att, n + 1)
                if g == 0:
                    wait_from(dve, att_t_done, b)
                nc.vector.tensor_tensor(att[:, :, HG * g:HG * g + HG, :], v[:, :, :, 0:D],
                                        rcp[:, :, :].rearrange("p t (h o) -> p t h o", o=1)
                                        .to_broadcast([P, T, HG, D]), ALU.mult).then_inc(att_done, 1)

            def att_t_copy(b):
                bank, k = f_use(b, "att_t")
                dve.wait_ge(f_full[bank], k + 1)
                nc.vector.tensor_copy(att_t[:, :], f_ps[:, bank, :]).then_inc(att_t_done, 1)

            def residual(b):
                bank, k = f_use(b, "x1")
                dve.wait_ge(f_full[bank], k + 1)
                dve.wait_ge(bias_added, b + 1)
                dve.wait_ge(y_done, b + 1)
                nc.vector.tensor_tensor(x1[:, :, :], f_ps[:, bank, :].rearrange("p (t d) -> p t d", t=T),
                                        x_bias[:, :, :], ALU.add).then_inc(x1_done, 1)

            def stats2_of(b):
                dve.wait_ge(x1_done, b + 1)
                norm_stats(x1, st2, mv2, c_ffn, (ROUTER_CHAIN + 1) * b + 1, stats2)

            def normalise2(b, half):
                dve.wait_ge(rstd2_done, b + 1)
                normalise(x1, mv2, rstd2, xn2, range(2 * half, 2 * half + 2), xn2_done)

            def over(a):
                return a[:, :].rearrange("p (t o) -> p t o", o=1).to_broadcast([P, T, NE])

            ROUTER_CHAIN = 13

            def linked(b, i):
                dve.wait_ge(c_ffn, (ROUTER_CHAIN + 1) * b + (i + 1))

            def link(ins):
                ins.then_inc(c_ffn, 1)

            rank = rank_row.rearrange("p (o e) -> p o e", o=1).to_broadcast([P, T, NE])

            def router_logits(b):
                bank, k = f_use(b, "logit")
                dve.wait_ge(f_full[bank], k + 1)
                nc.vector.tensor_tensor(logit[:, :, :], f_ps[:, bank, 0:T * NE].rearrange("p (t e) -> p t e", t=T),
                                        gate_b_row.rearrange("p (o e) -> p o e", o=1).to_broadcast([P, T, NE]),
                                        ALU.add).then_inc(logit_read, 1)
                dve.wait_ge(logit_read, b + 1)
                link(nc.vector.tensor_reduce(lmax[:, :], logit[:, :, :], AX.X, ALU.max))
                linked(b, 1)
                nc.vector.tensor_tensor(logit[:, :, :], logit[:, :, :], over(lmax), ALU.subtract)\
                  .then_inc(logit_done, 1)

            def router_best(b):
                dve.wait_ge(ex_done, b + 1)
                link(nc.vector.tensor_reduce(top1[:, :], ex[:, :, :], AX.X, ALU.max))
                nc.vector.tensor_reduce(esum[:, :], ex[:, :, :], AX.X, ALU.add)
                linked(b, 2)
                link(nc.vector.tensor_tensor(tie[:, :, :], ex[:, :, :], over(top1), ALU.is_equal))

            def router_ties(b, i):
                linked(b, i)
                link(nc.vector.tensor_tensor(tie[:, :, :], tie[:, :, :], rank, ALU.mult))
                linked(b, i + 1)
                link(nc.vector.tensor_reduce(tmax[:, :], tie[:, :, :], AX.X, ALU.max))

            def router_first(b):
                linked(b, 5)
                link(nc.vector.tensor_tensor(hot1[:, :, :], tie[:, :, :], over(tmax), ALU.is_equal))
                nc.vector.reciprocal(ersum[:, :], esum[:, :])

            def router_others(b):
                linked(b, 6)
                link(nc.vector.scalar_tensor_tensor(out=ex[:, :, :], in0=hot1[:, :, :], scalar=-2.0,
                                                    in1=ex[:, :, :], op0=ALU.mult, op1=ALU.add))
                linked(b, 7)
                link(nc.vector.tensor_reduce(top2[:, :], ex[:, :, :], AX.X, ALU.max))

            def router_next(b):
                linked(b, 8)
                link(nc.vector.tensor_tensor(tie[:, :, :], ex[:, :, :], over(top2), ALU.is_equal))
                link(nc.vector.tensor_tensor(tsum[:, :], top1[:, :], top2[:, :], ALU.add))

            def router_second(b):
                linked(b, 12)
                link(nc.vector.tensor_tensor(hot2[:, :, :], tie[:, :, :], over(tmax), ALU.is_equal))
                nc.vector.tensor_tensor(gate[:, :], tsum[:, :], ersum[:, :], ALU.mult)
                linked(b, 13)
                nc.vector.tensor_tensor(hot_d[:, :, :], hot2[:, :, :], hot1[:, :, :], ALU.subtract).then_inc(hot_done, 1)

            def low_rank(b, expert):
                dve.wait_ge(u_copied, b + 1)
                if expert == 0:
                    linked(b, 6)
                else:
                    dve.wait_ge(hot_done, b + 1)
                out, hot = ((u1, hot1), (ud, hot_d))[expert]
                nc.vector.tensor_tensor(out[:, :, :, :], u[:, :].rearrange("p (t e r) -> p t e r", t=T, e=NE),
                                        hot[:, :, :].rearrange("p t (e o) -> p t e o", o=1)
                                        .to_broadcast([P, T, NE, R]), ALU.mult).then_inc(u_done, 1)

            def hidden(b, c):
                bank, k = f_use(b, f"c{c}+")
                dve.wait_ge(f_full[bank], k + 1)
                nc.vector.scalar_tensor_tensor(out=hid[:, c, :], in0=f_ps[:, bank, :], scalar=neg_bi[:, c:c + 1],
                                               in1=relu1[:, c, :], op0=ALU.max, op1=ALU.add).then_inc(hid_done, 1)

            def add_out_const(b):
                bank, k = f_use(b, "ffn")
                dve.wait_ge(f_full[bank], k + 1)
                nc.vector.tensor_tensor(ffn[:, :, :], f_ps[:, bank, :].rearrange("p (t d) -> p t d", t=T),
                                        out_const[:, :].rearrange("p (o d) -> p o d", o=1).to_broadcast([P, T, E]),
                                        ALU.add).then_inc(ffn_done, 1)

            def output(b):
                dve.wait_ge(ffn_done, b + 2)
                dve.wait_ge(y_out, 16 * (b + 1))
                for t in range(T):
                    last = nc.vector.scalar_tensor_tensor(out=y_sb[:, t, :], in0=ffn[:, t, :], scalar=gate[:, t:t + 1],
                                                          in1=x1[:, t, :], op0=ALU.mult, op1=ALU.add)
                last.then_inc(y_done, 1)

            def ffn_task(b, g, p):
                if (g, p) == (0, 8):
                    att_t_copy(b)
                if (g, p) == (0, 10):
                    residual(b)
                if (g, p) == (1, 0):
                    stats2_of(b)
                if (g, p) == (1, 2):
                    normalise2(b, 0)
                if (g, p) == (1, 3):
                    normalise2(b, 1)
                if (g, p) in ROUTER_AT:
                    task, *args = ROUTER_AT[g, p]
                    task(b, *args)
                if (g, p) in HIDDEN_AT:
                    hidden(b, HIDDEN_AT.index((g, p)))
                if (g, p) == (3, 8):
                    add_out_const(b)
                if (g, p) == (3, 9):
                    output(b)

            def step(b, first=False, last=False):
                for g in range(G):
                    n = 4 * b + g
                    for p in range(NPOS):
                        if p == 5 and not (last and g == 3):
                            split_max(n + 1)
                        if (g, p) == (0, 0) and not last:
                            stats1_of(b + 1)
                        m, place, k = max_at(n, g, p)
                        if not (last and (g == 3 or g == 2 and k < MAX_LEAD)):
                            max_unit(m, place, k)
                        if p == 0 and not (last and g >= 2):
                            q_t_copy(n + 2, b, g, (g + 2) % G)
                        if p == (9 if g else 5) and not (first and g == 0):
                            normalise_att(n - 1, b if g else b - 1, b, g, (g - 1) % G)
                        if not last and (g, p) in PREP_AT:
                            task, *args = PREP_AT[g, p]
                            task(b + 1, *args)
                        if not first:
                            ffn_task(b - 1, g, p)

            ROUTER_AT = {(1, 7): [router_logits], (1, 8): [router_best], (1, 9): [router_ties, 3], (1, 10): [router_first],
                         (2, 0): [low_rank, 0], (2, 1): [router_others], (2, 2): [router_next],
                         (2, 3): [router_ties, 10], (2, 4): [router_second], (2, 5): [low_rank, 1]}
            PREP_AT = {(0, 2): [normalise1, 0], (0, 3): [normalise1, 1], (1, 4): [high_q], (1, 6): [high_k],
                       (1, 7): [mid_q], (1, 8): [mid_k], (1, 9): [low_q], (1, 10): [low_k]}
            stats1_of(0)
            nc.vector.memset(q_parts[:, :, MAX_ROW:], 0.0)
            nc.vector.memset(k_parts[:, :, :, MAX_ROW:MAX_ROW + 3], 1.0)
            nc.vector.memset(k_parts[:, :, :, MAX_ROW + 3:], 0.0)
            normalise1(0, 0)
            normalise1(0, 1)
            nc.vector.memset(k_t[64:P, :, 0, :].bitcast(F32), 0.0)
            nc.vector.memset(k_t[0:64, :, 1, :].bitcast(F32), 0.0).then_inc(cleared, 1)
            rotate_first(0)
            rotate_first(1)
            high_q(0)
            high_k(0)
            rests_first()
            for task in (mid_q, mid_k, low_q, low_k):
                task(0)
            q_t_copy(0, -1, 0, 0)
            dve.wait_ge(big_in, 32)
            nc.vector.tensor_scalar(neg_bi[:, :], bi, -1.0, None, ALU.mult)
            dve.wait_ge(const_ps, 1)
            nc.vector.scalar_tensor_tensor(out=out_const[:, :], in0=bo_row, scalar=2.0, in1=max_ps[:, 1, 0:E],
                                           op0=ALU.mult, op1=ALU.add).then_inc(const_done, 1)
            for k in range(MAX_UNITS):
                max_unit(0, 0, k)
                if k == 1:
                    q_t_copy(1, -1, 1, 1)
            split_max(0)
            for k in range(MAX_LEAD):
                max_unit(1, 1, k)
            step(0, first=True)
            with dve.Fori(1, B - 1) as b:
                step(b)
            step(B - 1, last=True)
            normalise_att(4 * B - 1, B - 1, B, 0, 3)
            for g in range(G):
                for p in range(NPOS):
                    ffn_task(B - 1, g, p)

        @block.tensor
        def _(pe):
            def a_write(step, name, g=0):
                wait_from(pe, *a_previous(step, name, g))

            def f_write(b, name):
                for semaphore, value in f_previous(b, name):
                    pe.wait_ge(semaphore, value)
                return f_bank(name)

            def project(b, j):
                bank = f_write(b, f"qkv{j}")
                pe.wait_ge(xn1t_done, b + 1)
                for i in range(2):
                    t = 2 * j + i
                    last = nc.tensor.matmul(f_ps[:, bank, i * QKV:(i + 1) * QKV], xn1_t[:, t * P:(t + 1) * P], wqkv[:, :],
                                            start=True, stop=True)
                last.then_inc(f_full[bank], 1)

            def xn1_transpose(b):
                f_transpose(b, "xn1_t", lambda t: xn1[:, t, :], xn1_done, b + 1)

            def q_transpose(b, step, slot, g):
                a_write(step, "q_t", slot)
                pe.wait_ge(parts_done, 2 * b + 1)
                for pp in range(2):
                    for t in range(T):
                        h = t * H + HG * g + 2 * pp
                        last = nc.tensor.transpose(a_bf[:, pp * S + t * P:pp * S + (t + 1) * P],
                                                   q_parts[:, h:h + 2, :].rearrange("p h r -> p (h r)"), ident_b[:, :])
                last.then_inc(a_full, 1)

            def k_transpose(b, step, slot, g):
                a_write(step, "k_t", slot)
                pe.wait_ge(parts_done, 2 * b + 2)
                for t in range(T):
                    last = nc.tensor.transpose(a_bf[:, t * P:(t + 1) * P],
                                               k_parts[:, t * G + g, :, :].rearrange("p e r -> p (e r)"), ident_b[:, :])
                last.then_inc(a_full, 1)

            def max_unit(n, g, k):
                t, h0, nh, width = max_place(k)
                if k == 0:
                    pe.wait_ge(qt_done, n + 1)
                    pe.wait_ge(kt_done, n + 1)
                wait_from(pe, max_done, MAX_UNITS * n + k - 1)
                bank = max_ps[:, (g + k) % 2, 0:nh * width].rearrange("p (h k) -> p h k", h=nh)
                for i in range(nh):
                    h = h0 + i
                    nc.tensor.matmul(bank[:, i, :], q_t[:, g, h // 2, t * P:(t + 1) * P], k_t[:, g, h % 2, 0:width],
                                     start=i == 0, stop=False, skip_group_check=True)
                nc.tensor.matmul(bank[:, :, width - P:width], ident_b[:, :], mask_b[:, 0:nh, :],
                                 start=False, stop=True, skip_group_check=True).then_inc(max_full, 1)

            def max_transpose(n, step, slot):
                a_write(step, "max_t", slot)
                pe.wait_ge(max_parts_done, n + 1)
                for pp in range(2):
                    for t in range(T):
                        last = nc.tensor.transpose(a_bf[0:6, pp * S + t * P:pp * S + (t + 1) * P],
                                                   max_parts[:, t, 2 * pp:2 * pp + 2, :].rearrange("p h c -> p (h c)"),
                                                   ident_b[:, :])
                last.then_inc(a_full, 1)

            def exp_unit(n, g, k):
                if k == 0:
                    pe.wait_ge(max_rows_in, 32 * (n + 1))
                wait_from(pe, exp_done, EXP_UNITS * n + k - 1)
                for h, j, col in exp_place(k):
                    last = nc.tensor.matmul(sc_ps[:, k % 2, col:col + S - j * P], k_t[:, g, h % 2, j * P:(j + 1) * P],
                                            q_t[:, g, h // 2, j * P:S], start=True, stop=True)
                last.then_inc(sc_full, 1)

            def weigh_values(n, b, g, k):
                j = (0, 1, 3, 2)[k]
                if k == 0:
                    wait_from(pe, o_copied, n)
                    pe.wait_ge(v_done, 2 * b + (2 if g == G - 1 else 1))
                pe.wait_ge(masked, 4 * n + k + 1)
                for h in range(HG):
                    unit, col = next((u, c) for u in range(EXP_UNITS) for hh, jj, c in exp_place(u) if (hh, jj) == (h, j))
                    last = nc.tensor.matmul(pv_ps[32 * h:32 * h + 32, j * P:S], v_aug[:, j, g, :],
                                            probs[:, g % 2, unit, col:col + S - j * P], start=k == 0, stop=k == 3,
                                            skip_group_check=True)
                if k == 3:
                    last.then_inc(pv_full, 1)

            def out_transpose(n, step, slot):
                a_write(step, "out_t", slot)
                pe.wait_ge(o_copied, n + 1)
                for t in range(T):
                    last = nc.tensor.transpose(a_ps[:, t * P:(t + 1) * P], o_sb[:, t * P:(t + 1) * P], ident_f[:, :])
                last.then_inc(a_full, 1)

            def f_transpose(b, name, src, ready, value):
                bank = f_write(b, name)
                pe.wait_ge(ready, value)
                for t in range(T):
                    last = nc.tensor.transpose(f_ps[:, bank, t * P:(t + 1) * P], src(t), ident_f[:, :])
                last.then_inc(f_full[bank], 1)

            def token_major(b, name, lhs, rhs, width, ready, value):
                bank = f_write(b, name)
                pe.wait_ge(ready, value)
                for t in range(T):
                    last = nc.tensor.matmul(f_ps[:, bank, t * width:(t + 1) * width], lhs[:, t * P:(t + 1) * P], rhs,
                                            start=True, stop=True)
                last.then_inc(f_full[bank], 1)

            def u_transpose(b, name, src, ready):
                a_write(b + 1, name)
                pe.wait_ge(u_done, ready)
                for t in range(T):
                    last = nc.tensor.transpose(a_ps[:, t * P:(t + 1) * P],
                                               src[:, t, :, :].rearrange("p e r -> p (e r)"), ident_f[:, :])
                last.then_inc(a_full, 1)

            def base(b, c):
                bank = f_write(b, f"c{c}")
                nc.tensor.matmul(f_ps[:, bank, :], wi_t[:, c, :], xn2_t[:, :], start=True, stop=False, skip_group_check=True)

            def first_expert(b, c):
                bank = f_bank(f"c{c}")
                pe.wait_ge(ut_done, 2 * b + 1)
                nc.tensor.matmul(f_ps[:, bank, :], lb_t[:, c, :], u1_t[:, :], start=False, stop=False,
                                 skip_group_check=True).then_inc(f_full[bank], 1)

            def second_expert(b, c):
                bank = f_write(b, f"c{c}+")
                pe.wait_ge(ut_done, 2 * b + 2)
                nc.tensor.matmul(f_ps[:, bank, :], lb_t[:, c, :], ud_t[:, :], start=False, stop=True,
                                 skip_group_check=True).then_inc(f_full[bank], 1)

            def down(b, t):
                if t == 0:
                    f_write(b, "ffn")
                    pe.wait_ge(hid_done, FC * (b + 2))
                bank, _ = f_use(b, "ffn")
                for c in range(FC):
                    last = nc.tensor.matmul(f_ps[:, bank, t * P:(t + 1) * P], hid[:, c, t * P:(t + 1) * P],
                                            wo_t[:, c, :], start=c == 0, stop=c == FC - 1)
                if t == T - 1:
                    last.then_inc(f_full[bank], 1)

            def ffn_task(b, g, p):
                if (g, p) == (0, 8):
                    f_transpose(b, "att_t", lambda t: att[:, t, :, :].rearrange("p h d -> p (h d)"), att_done, 4 * (b + 1))
                if (g, p) == (0, 9):
                    token_major(b, "x1", att_t, wout, P, att_t_done, b + 1)
                if (g, p) == (1, 4):
                    f_transpose(b, "xn2_t", lambda t: xn2[:, t, :], xn2_done, b + 1)
                if (g, p) == (1, 5):
                    token_major(b, "logit", xn2_t, gate_t, NE, xn2t_done, b + 1)
                    token_major(b, "u", xn2_t, la_t, P, xn2t_done, b + 1)
                if (g, p) == (2, 2):
                    u_transpose(b, "u1_t", u1, 2 * b + 1)
                if (g, p) == (2, 5):
                    u_transpose(b, "ud_t", ud, 2 * b + 2)
                for c in range(FC):
                    if (g, p) == BASE_AT[c]:
                        base(b, c)
                    if (g, p) == FIRST_AT[c]:
                        first_expert(b, c)
                    if (g, p) == SECOND_AT[c]:
                        second_expert(b, c)
                if (g, p) in DOWN_AT:
                    down(b, DOWN_AT.index((g, p)))

            def step(b, first=False, last=False):
                for g in range(G):
                    n = 4 * b + g
                    for p in range(NPOS):
                        if p == (9 if g else 5) and not (first and g == 0):
                            out_transpose(n - 1, b, g)
                        m, place, k = max_at(n, g, p)
                        if not (last and (g == 3 or g == 2 and k < MAX_LEAD)):
                            max_unit(m, place, k)
                        if p < EXP_UNITS:
                            exp_unit(n, g, p)
                        if p < T and not (first and g == 0):
                            weigh_values(n - 1, b if g else b - 1, (g - 1) % G, p)
                        if not (last and g >= 2):
                            if p == 0:
                                q_transpose(b + (g >= 2), b, g, (g + 2) % G)
                            if p == 1:
                                k_transpose(b + (g >= 2), b, g, (g + 2) % G)
                        if p == (6 if g or first else 7) and not (last and g == 3):
                            max_transpose(n + 1, b, g)
                        if g == 0 and not last:
                            if p == 4:
                                xn1_transpose(b + 1)
                            if p == 6:
                                project(b + 1, 0)
                            if p == 7:
                                project(b + 1, 1)
                        if not first:
                            ffn_task(b - 1, g, p)

            pe.wait_ge(small_in, 32)
            nc.tensor.matmul(max_ps[:, 0, 0:P], wq_in[:, 0:P], wq_in[:, P:2 * P], start=True, stop=True)
            nc.tensor.matmul(max_ps[:, 0, P:QKV], wkv_in[:, 0:P], wkv_in[:, P:P + QKV - P], start=True, stop=True)\
              .then_inc(wqkv_ps, 1)
            pe.wait_ge(setup, SETUP_IDENT)
            xn1_transpose(0)
            pe.wait_ge(wqkv_done, 1)
            project(0, 0)
            project(0, 1)
            pe.wait_ge(big_in, 32)
            for c in range(FC):
                last = nc.tensor.matmul(max_ps[:, 1, 0:E], bi[:, c:c + 1].to_broadcast([P, P]), wo_t[:, c, :],
                                        start=c == 0, stop=c == FC - 1)
            last.then_inc(const_ps, 1)
            pe.wait_ge(setup, SETUP)
            pe.wait_ge(cleared, 1)
            q_transpose(0, -1, 0, 0)
            k_transpose(0, -1, 0, 0)
            for k in range(MAX_UNITS):
                if k == 1:
                    pe.wait_ge(const_done, 1)
                max_unit(0, 0, k)
                if k == 1:
                    q_transpose(0, -1, 1, 1)
                if k == 4:
                    k_transpose(0, -1, 1, 1)
            max_transpose(0, -1, 0)
            for k in range(MAX_LEAD):
                max_unit(1, 1, k)
            step(0, first=True)
            with pe.Fori(1, B - 1) as b:
                step(b)
            step(B - 1, last=True)
            for k in range(T):
                weigh_values(4 * B - 1, B - 1, G - 1, k)
            out_transpose(4 * B - 1, B, 0)
            for g in range(G):
                for p in range(NPOS):
                    ffn_task(B - 1, g, p)


def kernel(**inputs):
    import numpy as np
    import concourse.bacc as bacc
    from concourse.bass_utils import run_bass_kernel_spmd

    w = {k: np.asarray(v) for k, v in inputs.items()}
    x = w["L0_attn_x"]
    B, S, E = x.shape
    T = S // P
    G, D = 4, 8
    H = E // D
    NE, R, _ = w["L0_ffn_lora_A"].shape
    F = w["L0_ffn_wi"].shape[0]
    FC = F // P

    halves = np.array([2 * i + c for c in range(2) for i in range(D // 2)])
    q_cols = np.concatenate([h * D + halves for h in range(H)])
    k_cols = np.concatenate([(g * D + halves) * 2 for g in range(G)])
    v_cols = np.arange(G * D) * 2 + 1
    kv_cols = np.concatenate([k_cols, v_cols])

    inv_freq = (1.0 / np.float32(10000.0) ** (np.arange(0, D, 2, dtype=np.float32) / np.float32(D))).astype(np.float32)
    angle = np.outer(np.arange(S, dtype=np.float32), inv_freq).astype(np.float32)
    cos, sin = np.cos(angle).astype(np.float32), np.sin(angle).astype(np.float32)

    def by_token(a):
        return a.reshape(T, P, D).transpose(1, 0, 2).reshape(P, T * D)

    rank = np.tile(np.arange(NE, 0, -1, dtype=np.float32), (P, 1))
    arrays = {
        "x": x.reshape(B, T, P, E).transpose(0, 2, 1, 3),
        "w_q": np.concatenate([w["L0_attn_Wqa"].T, w["L0_attn_Wqb"][:, q_cols]], axis=1),
        "w_kv": np.concatenate([w["L0_attn_Wkva"].T, w["L0_attn_Wkvb"][:, kv_cols]], axis=1),
        "w_big": np.concatenate([
            w["L0_ffn_wi"].T,
            w["L0_ffn_lora_B"].transpose(0, 2, 1).reshape(NE * R, F),
            w["L0_ffn_wo"].T.reshape(FC, P, E).transpose(1, 0, 2).reshape(P, FC * E),
            w["L0_ffn_lora_A"].reshape(NE * R, E).T,
            w["L0_ffn_gate_w"].T,
            w["L0_attn_Wout"],
            w["L0_ffn_bi"].reshape(FC, P).T], axis=1),
        "rows": np.concatenate([w["L0_attn_bout"], w["L0_ffn_bo"], w["L0_ffn_gate_b"]])[None, :],
        "tables": np.concatenate([by_token(np.concatenate([cos, cos], axis=1)),
                                  by_token(np.concatenate([-sin, sin], axis=1)), rank], axis=1),
    }
    arrays = {k: np.ascontiguousarray(v) for k, v in arrays.items()}
    nc = bacc.Bacc("TRN2", target_bir_lowering=False, num_devices=1)
    args = [nc.dram_tensor(k, v.shape, mybir.dt.from_np(v.dtype), kind="ExternalInput").ap() for k, v in arrays.items()]
    y = nc.dram_tensor("y", (B, P, T, E), F32, kind="ExternalOutput").ap()
    bass_preln_attention_moe_lora(nc, *args, y)
    out = run_bass_kernel_spmd(nc, [arrays], core_ids=[0]).results[0]["y"]
    return out.reshape(B, P, T, E).transpose(0, 2, 1, 3).reshape(B, S, E)
```

```python
from contextlib import ExitStack

import concourse.bass as bass
from concourse import mybir

ALU = mybir.AluOpType
ACT = mybir.ActivationFunctionType
AX = mybir.AxisListType
F32 = mybir.dt.float32
BF16 = mybir.dt.bfloat16

P = 128
LN_EPS = 1e-5
MASKED = -1e30

SLOTS = 8
MAX_ROW = 48

NPOS = 11
MAX_UNITS = 11
EXP_UNITS = 10
MAX_LEAD = 6
PE_AT = {
    "xn1_t": (0, 5), "qkv0": (0, 6), "qkv1": (0, 9),
    "att_t": (0, 7), "x1": (0, 9), "xn2_t": (1, 3), "router": (1, 5), "u1_t": (2, 2), "ud_t": (2, 4),
    "base": [(1, 9), (1, 8), (2, 9), (2, 10)],
    "first": [(2, 4), (2, 5), (2, 9), (2, 10)],
    "second": [(2, 7), (2, 7), (3, 1), (3, 1)],
    "down": [(3, 3), (3, 4), (3, 6), (3, 7)],
}
ACT_AT = {
    "xn1_t": (0, 5), "qkv0": (0, 6), "qkv1": (0, 10),
    "high_q": (1, 5), "mid_q": (1, 9), "k": (1, 9),
    "xn2_t": (1, 3), "exp": (1, 7), "u": (1, 6), "u1_t": (2, 2), "ud_t": (2, 4),
    "relu": [(2, 5), (2, 6), (3, 0), (3, 1)],
}
DVE_AT = {
    "normalise1": [(0, 1), (0, 3)],
    "high_q": (1, 4), "high_k": (1, 7), "mid_q": (1, 7), "mid_k": (1, 8), "low_k": (1, 9),
    "att_t": (0, 7), "x1": (0, 9), "stats2": (0, 10), "normalise2": [(1, 1), (1, 1)],
    "logits": (1, 5), "best": (1, 7), "ties": (1, 8), "first": (1, 9), "u1": (1, 10),
    "others": (2, 0), "second": (2, 0), "ud": (2, 2), "output_rest": [(2, 4), (2, 5)],
    "hidden": [(2, 7), (2, 9), (3, 0), (3, 1)],
    "output": [(3, 8), (3, 10)],
}
PE_SLOT = {"weigh": [(0, 0), (1, 1), (2, 2), (2, 2)], "q_t": (0, 0), "k_t": (1, 1), "max_t": (6, 6), "out_t": (5, 9)}
ACT_SLOT = {"k_t": (2, 2), "max_t": (6, 7), "o": (2, 2)}
DVE_SLOT = {"q_t": (0, 0), "att": (4, 9)}
SETUP_IDENT = 3
SETUP = 12


def max_at(n, g, p):
    if p < MAX_UNITS - MAX_LEAD:
        return n + 1, (g + 1) % 4, p + MAX_LEAD
    return n + 2, (g + 2) % 4, p - (MAX_UNITS - MAX_LEAD)


def max_place(k):
    if k == 0:
        return 0, 0, 4, P
    if k < 3:
        return 1, 2 * (k - 1), 2, 2 * P
    if k < 7:
        return 2, k - 3, 1, 3 * P
    return 3, k - 7, 1, 4 * P


def exp_place(k):
    if k < 4:
        return [(k, 0, 0)]
    if k < 8:
        return [(k - 4, 1, 0), (k - 4, 3, 3 * P)]
    return [(2 * (k - 8), 2, 0), (2 * (k - 8) + 1, 2, 2 * P)]


def bass_preln_attention_moe_lora(nc: bass.Bass, x, w_q, w_kv, w_big, rows, tables, y):
    B, _, T, E = x.shape
    S = T * P
    D = 8
    H = E // D
    G = 4
    HG = H // G
    HK = H + G
    QL = w_q.shape[0]
    KVL = w_kv.shape[0]
    NE = 8
    R = P // NE
    FC = 4
    QKV = (HK + G) * D
    SCALE = float(D) ** -0.5
    assert S == 512 and E == P and HG == 4 and T == 4

    with ExitStack() as ctx:
        def sb(name, shape, dt=F32):
            return ctx.enter_context(nc.sbuf_tensor(name, shape, dt))

        def sem(name):
            return ctx.enter_context(nc.semaphore(name))

        wq_in = sb("wq_in", [QL, 2 * P])
        wkv_in = sb("wkv_in", [KVL, P + 2 * G * D])
        wbig = sb("wbig", [P, w_big.shape[1]])
        o = 0
        wi_t = wbig[:, o:o + FC * P].rearrange("p (c f) -> p c f", c=FC); o += FC * P
        lb_t = wbig[:, o:o + FC * P].rearrange("p (c f) -> p c f", c=FC); o += FC * P
        wo_t = wbig[:, o:o + FC * P].rearrange("p (c d) -> p c d", c=FC); o += FC * P
        la_gate_t = wbig[:, o:o + P + NE]; o += P + NE
        wout = wbig[:, o:o + P]; o += P
        bi = wbig[:, o:o + FC]; o += FC
        row_sb = sb("row_sb", [P, 2 * E + NE])
        bout_row, bo_row, gate_b_row = row_sb[:, 0:E], row_sb[:, E:2 * E], row_sb[:, 2 * E:2 * E + NE]
        tab_sb = sb("tab_sb", [P, 2 * T * D + NE])
        cos_t = tab_sb[:, 0:T * D].rearrange("p (t o d) -> p t o d", t=T, o=1)
        sin_t = tab_sb[:, T * D:2 * T * D].rearrange("p (t o d) -> p t o d", t=T, o=1)
        rank_row = tab_sb[:, 2 * T * D:2 * T * D + NE]
        wqkv = sb("wqkv", [P, QKV])
        neg_bi = sb("neg_bi", [P, FC])
        out_const = sb("out_const", [P, E])
        ident_f = sb("ident_f", [P, P])
        ident_b = sb("ident_b", [P, P], BF16)
        mask_b = sb("mask_b", [P, HG, P], BF16)
        neg_half = sb("neg_half", [P, T])

        x_sb = sb("x_sb", [P, T, E])
        st1 = sb("st1", [P, T, 6])
        mv1 = sb("mv1", [P, T, 2])
        ve1 = sb("ve1", [P, T])
        rstd1 = sb("rstd1", [P, T])
        xn1 = sb("xn1", [P, T, E])
        xn1_t = sb("xn1_t", [P, S])
        raw = sb("raw", [P, T, QKV])
        rot_a = sb("rot_a", [P, T, HK, D])
        rot_b = sb("rot_b", [P, T, HK, D])
        rq = sb("rq", [P, T * H, D])
        rk = sb("rk", [P, T * G, D])
        rest_q = sb("rest_q", [P, T * H, D])
        rest_k = sb("rest_k", [P, T * G, D])
        q_parts = sb("q_parts", [P, T * H, SLOTS * D], BF16)
        k_parts = sb("k_parts", [P, T * G, 2, SLOTS * D], BF16)

        q_t = sb("q_t", [P, G, 2, S], BF16)
        k_t = sb("k_t", [P, G, 2, S], BF16)
        v_aug = sb("v_aug", [P, T, G, 32])
        neg_max = sb("neg_max", [P, T, HG])
        max_rest = sb("max_rest", [P, T, HG])
        max_parts = sb("max_parts", [P, T, HG, 3], BF16)
        max_t = sb("max_t", [3 * HG, S], BF16)
        probs = sb("probs", [P, 2, EXP_UNITS, S])
        o_sb = sb("o_sb", [P, S])
        rcp = sb("rcp", [P, T, HG])
        att = sb("att", [P, T, H, D])

        x_res = sb("x_res", [P, T, E])
        x_bias = sb("x_bias", [P, T, E])
        att_t = sb("att_t", [P, S])
        x1 = sb("x1", [P, T, E])
        st2 = sb("st2", [P, T, 6])
        mv2 = sb("mv2", [P, T, 2])
        ve2 = sb("ve2", [P, T])
        rstd2 = sb("rstd2", [P, T])
        xn2 = sb("xn2", [P, T, E])
        xn2_t = sb("xn2_t", [P, S])
        logit = sb("logit", [P, T, NE])
        lmax = sb("lmax", [P, T])
        ex = sb("ex", [P, T, NE])
        esum = sb("esum", [P, T])
        ersum = sb("ersum", [P, T])
        best = sb("best", [P, T, NE])
        tsum = sb("tsum", [P, T])
        gate = sb("gate", [P, T])
        tie = sb("tie", [P, T, 2, NE])
        tmax = sb("tmax", [P, T])
        hot1 = sb("hot1", [P, T, NE])
        hot2 = sb("hot2", [P, T, NE])
        hot_d = sb("hot_d", [P, T, NE])
        u = sb("u", [P, S])
        u1 = sb("u1", [P, T, NE, R])
        ud = sb("ud", [P, T, NE, R])
        u1_t = sb("u1_t", [P, S])
        ud_t = sb("ud_t", [P, S])
        relu1 = sb("relu1", [P, FC, S])
        hid = sb("hid", [P, FC, S])
        y_rest = sb("y_rest", [P, T, E])
        y_sb = sb("y_sb", [P, T, E])

        max_ps = ctx.enter_context(nc.psum_tensor("max_ps", [P, 2, S], F32))
        sc_ps = ctx.enter_context(nc.psum_tensor("sc_ps", [P, 2, S], F32))
        pv_ps = ctx.enter_context(nc.psum_tensor("pv_ps", [P, S], F32))
        a_ps = ctx.enter_context(nc.psum_tensor("a_ps", [P, S], F32))
        f_ps = ctx.enter_context(nc.psum_tensor("f_ps", [P, 2, S], F32))
        a_bf = a_ps[:, :].bitcast(BF16)
        first_xn1_t, first_qkv = [sc_ps[:, 0, :], max_ps[:, 1, :]], [sc_ps[:, 1, :], pv_ps[:, :]]
        first_q_t = [a_bf, f_ps[:, 0, :].bitcast(BF16)]
        first_k_t = [sc_ps[:, 0, :].bitcast(BF16), sc_ps[:, 1, :].bitcast(BF16)]
        first_max_t = f_ps[:, 1, :].bitcast(BF16)
        last_out_ps = [a_ps, max_ps[:, 0, :]]
        last_att_t_ps = [f_ps[:, 1, :], max_ps[:, 1, :]]
        last_x1_ps = [sc_ps[:, 0, :], sc_ps[:, 1, :]]
        last_xn2_t_ps = [f_ps[:, 0, :], pv_ps]
        last_hidden = [max_ps[:, 0, :], max_ps[:, 1, :], sc_ps[:, 0, :], sc_ps[:, 1, :]]
        last_down = [f_ps[:, 0, 0:P], f_ps[:, 1, 0:P], pv_ps[:, 0:P], a_ps[:, 0:P]]

        router_ps = f_ps[:, :, 0:2 * (P + NE)].rearrange("p k (t c) -> p k t c", t=2)

        q_slots = q_parts[:, :, :].rearrange("p r (s d) -> p r s d", d=D)
        k_slots = k_parts[:, :, :, :].rearrange("p r e (s d) -> p r e s d", d=D)

        small_in = sem("small_in")
        tab_in = sem("tab_in")
        big_in = sem("big_in")
        x_in = sem("x_in")
        xres_in = sem("xres_in")
        y_out = sem("y_out")
        setup = sem("setup")
        cleared = sem("cleared")
        wqkv_ps = sem("wqkv_ps")
        wqkv_done = sem("wqkv_done")
        const_ps = sem("const_ps")
        const_done = sem("const_done")
        first_full = sem("first_full")
        first_xn1 = sem("first_xn1")
        first_xn1t_done = sem("first_xn1t_done")
        a_full = sem("a_full")
        f_full = [sem("f_full0"), sem("f_full1")]
        passed = sem("passed")
        x1_done = sem("x1_done")
        logit_read = sem("logit_read")
        u_copied = sem("u_copied")
        max_full = sem("max_full")
        max_done = sem("max_done")
        sc_full = sem("sc_full")
        exp_done = sem("exp_done")
        masked = sem("masked")
        pv_full = sem("pv_full")
        o_copied = sem("o_copied")
        att_done = sem("att_done")
        stats1 = sem("stats1")
        rstd1_done = sem("rstd1_done")
        xn1_done = sem("xn1_done")
        xn1t_done = sem("xn1t_done")
        raw_done = sem("raw_done")
        rope_done = sem("rope_done")
        v_done = sem("v_done")
        low_q_done = sem("low_q_done")
        parts_done = sem("parts_done")
        qt_done = sem("qt_done")
        kt_done = sem("kt_done")
        max_parts_done = sem("max_parts_done")
        maxt_done = sem("maxt_done")
        max_rows_in = sem("max_rows_in")
        bias_added = sem("bias_added")
        att_t_done = sem("att_t_done")
        stats2 = sem("stats2")
        rstd2_done = sem("rstd2_done")
        xn2_done = sem("xn2_done")
        xn2t_done = sem("xn2t_done")
        logit_done = sem("logit_done")
        ex_done = sem("ex_done")
        hot_done = sem("hot_done")
        u_done = sem("u_done")
        ut_done = sem("ut_done")
        relu_done = sem("relu_done")
        hid_done = sem("hid_done")
        rest_y_done = sem("rest_y_done")
        y_done = sem("y_done")
        last_full = sem("last_full")
        last_y = sem("last_y")
        last_o = sem("last_o")
        last_out_t = sem("last_out_t")
        last_att = sem("last_att")
        last_att_t = sem("last_att_t")
        last_att_t_done = sem("last_att_t_done")
        last_x1 = sem("last_x1")
        last_x1_done = sem("last_x1_done")
        last_xn2 = sem("last_xn2")
        last_xn2_t = sem("last_xn2_t")
        last_xn2t_done = sem("last_xn2t_done")
        high_done = sem("high_done")
        rest_done = sem("rest_done")
        mid_done = sem("mid_done")
        repeated = sem("repeated")
        c_prep = sem("c_prep")
        c_rotate = sem("c_rotate")
        c_max = sem("c_max")
        c_att = sem("c_att")
        c_ffn = sem("c_ffn")
        c_pool = sem("c_pool")
        c_pool2 = sem("c_pool2")

        HEAD_START = [(stats2, 1), (hid_done, FC), (y_done, 1), (y_out, 16)]

        block = ctx.enter_context(nc.Block())

        def a_jobs(first, last):
            jobs = []
            for g in range(G):
                if not (last and g >= 2):
                    jobs += [("q_t", g), ("k_t", g)]
                if g == 2 and not first:
                    jobs += [("u1_t", 0), ("ud_t", 0)]
                if g > 0 and not (last and g == 3):
                    jobs.append(("max_t", g))
                if not (first and g == 0):
                    jobs.append(("out_t", g))
                if g == 0:
                    jobs.append(("max_t", g))
            return jobs

        HALF = [slice(0, S // 2), slice(S // 2, S)]
        LAST_STORES = [(0, T - 1), (T - 1, T)]
        LAST_JOBS = [("out_t", 0), ("u1_t", 0), ("ud_t", 0)]

        def a_index(b, name, g=0):
            if isinstance(b, int) and b == B:
                return a_index(B - 1, "out_t", 3) + 1 + LAST_JOBS.index((name, g))
            first, last = isinstance(b, int) and b == 0, isinstance(b, int) and b == B - 1
            k = a_jobs(first, last).index((name, g))
            if first:
                return k
            return (b - 1) * len(a_jobs(False, False)) + (len(a_jobs(True, False)) + k)

        def a_previous(b, name, g=0):
            if isinstance(b, int) and b == B:
                k = LAST_JOBS.index((name, g))
                return [a_reader("out_t", 4 * B - 2), a_reader("out_t", 4 * B - 1), (ut_done, 2 * B - 1)][k]
            jobs = a_jobs(isinstance(b, int) and b == 0, isinstance(b, int) and b == B - 1)
            k = jobs.index((name, g))
            if k == 0:
                return (a_reader("out_t", 4 * b - 2) if not isinstance(b, int) or b else (qt_done, 0))
            before, at = jobs[k - 1]
            if before in ("u1_t", "ud_t"):
                return ut_done, 2 * b - 1 if before == "u1_t" else 2 * b
            return a_reader(before, 4 * b + at + {"q_t": 2, "k_t": 2, "out_t": -1, "max_t": 1}[before])

        def a_reader(name, group):
            return {"q_t": qt_done, "k_t": kt_done, "out_t": att_done, "max_t": maxt_done}[name], group + 1

        F_PREP = [["xn1_t", "qkv0", "qkv1"], []]
        F_FFN = [["xn2_t", "router0", "c0", "c0+", "c2", "c2+"],
                 ["att_t", "x1", "router1", "c1", "c1+", "c3", "c3+", "ffn"]]

        def f_bank(name):
            return 0 if name in F_PREP[0] + F_FFN[0] else 1

        def f_use(b, name):
            bank = f_bank(name)
            if name in F_PREP[bank]:
                ffns = 0 if isinstance(b, int) and b < 2 else b - 2
                preps, k = b - 1, F_PREP[bank].index(name)
            else:
                ffns, k = b, F_FFN[bank].index(name)
                preps = min(b + 3, B) - 1 if isinstance(b, int) else b + 2
            return bank, len(F_FFN[bank]) * ffns + (len(F_PREP[bank]) * preps + k)

        def f_previous(b, name):
            bank = f_bank(name)
            if name in F_PREP[bank]:
                k = F_PREP[bank].index(name)
                if k > 0:
                    return [f_reader(b, F_PREP[bank][k - 1])]
                if isinstance(b, int) and b == 1:
                    return []
                return [f_reader(b - 1, F_PREP[bank][-1]), f_reader(b - 3, F_FFN[bank][-1])]
            k = F_FFN[bank].index(name)
            if k > 0 and F_FFN[bank][k - 1][0] == "r":
                return [(u_copied, b + 1)]
            if k > 0:
                return [f_reader(b, F_FFN[bank][k - 1])]
            if not F_PREP[bank] or isinstance(b, int) and b + 2 >= B:
                return [f_reader(b - 1, F_FFN[bank][-1])]
            return [f_reader(b + 2, F_PREP[bank][-1])]

        def f_reader(b, name):
            if name[0] == "c":
                if name[-1] == "+":
                    return hid_done, FC * (b + 1) + int(name[1]) + 1
                return relu_done, FC * b + int(name[1]) + 1
            return {"xn1_t": (xn1t_done, b + 1), "qkv0": (raw_done, 2 * b + 1), "qkv1": (raw_done, 2 * b + 2),
                    "att_t": (att_t_done, b + 1), "x1": (x1_done, b + 1), "xn2_t": (xn2t_done, b + 1),
                    "ffn": (y_done, b + 2)}[name]

        def wait_from(eng, semaphore, value):
            if not (isinstance(value, int) and value <= 0):
                eng.wait_ge(semaphore, value)

        def wait_apart(eng, semaphore, value):
            eng.wait_ge(semaphore, value)
            if not isinstance(value, int):
                eng.sem_inc(passed, 1)

        def rotation(t0, t1):
            both = raw[:, t0:t1, 0:HK * D].rearrange("p t (h d) -> p t h d", d=D)
            a, b, cos, sin = (v[:, t0:t1] for v in (rot_a, rot_b, cos_t, sin_t))
            n, h = t1 - t0, D // 2
            return [(a, both, cos.to_broadcast([P, n, HK, D])),
                    (b[:, :, :, 0:h], both[:, :, :, h:D], sin[:, :, :, 0:h].to_broadcast([P, n, HK, h])),
                    (b[:, :, :, h:D], both[:, :, :, 0:h], sin[:, :, :, h:D].to_broadcast([P, n, HK, h]))]

        def rotation_sums(t0, t1):
            return [(rq[:, t0 * H:t1 * H, :].rearrange("p (t h) d -> p t h d", h=H),
                     rot_a[:, t0:t1, 0:H, :], rot_b[:, t0:t1, 0:H, :]),
                    (rk[:, t0 * G:t1 * G, :].rearrange("p (t h) d -> p t h d", h=G),
                     rot_a[:, t0:t1, H:HK, :], rot_b[:, t0:t1, H:HK, :])]

        @block.sync
        def _(sp):
            sp.dma_start(x_sb[:, :, :], x[0]).then_inc(x_in, 16)
            sp.dma_start(wq_in[:, :], w_q).then_inc(small_in, 16)
            sp.dma_start(wkv_in[:, :], w_kv).then_inc(small_in, 16)
            sp.dma_start(tab_sb[:, :], tables).then_inc(tab_in, 16)
            sp.dma_start(wbig[:, :], w_big).then_inc(big_in, 16)
            sp.dma_start(row_sb[:, :], rows.to_broadcast([P, 2 * E + NE])).then_inc(big_in, 16)

            def load_x(b):
                wait_from(sp, xn1_done, b)
                sp.dma_start(x_sb[:, :, :], x[b]).then_inc(x_in, 16)

            def load_residual(b):
                wait_from(sp, bias_added, b)
                sp.dma_start(x_res[:, :, :], x[b]).then_inc(xres_in, 16)

            def max_rows(n, g):
                sp.wait_ge(maxt_done, n + 1)
                for pp in range(2):
                    sp.dma_start(q_t[MAX_ROW:MAX_ROW + 6, g, pp, :], max_t[6 * pp:6 * pp + 6, :]).then_inc(max_rows_in, 16)

            def store(b):
                sp.wait_ge(y_done, b + 2)
                sp.dma_start(y[b], y_sb[:, :, :]).then_inc(y_out, 16)

            def step(b, first=False, last=False, load=True):
                for g in range(G):
                    if g == 1:
                        load_residual(b)
                        if load:
                            load_x(b + 2)
                    if not (last and g == 3):
                        max_rows(4 * b + g + 1, (g + 1) % G)
                    if g == 3 and not first:
                        store(b - 1)

            load_x(1)
            max_rows(0, 0)
            step(0, first=True)
            with sp.Fori(1, B - 2) as b:
                step(b)
            step(B - 2, load=False)
            step(B - 1, last=True, load=False)
            for t0, t1 in LAST_STORES:
                sp.wait_ge(last_y, t1)
                sp.dma_start(y[B - 1][:, t0:t1, :], y_sb[:, t0:t1, :]).then_inc(y_out, 16)
            sp.wait_ge(y_out, 16 * (B + len(LAST_STORES)))

        @block.gpsimd
        def _(pool):
            n_setup = 0
            for semaphore, count in HEAD_START:
                pool.sem_inc(semaphore, count)

            def done(ins):
                nonlocal n_setup
                ins.then_inc(setup, 1)
                n_setup += 1

            done(nc.gpsimd.memset(ident_f[:, :], 0.0))
            done(nc.gpsimd.memset(neg_half[:, :], -0.5))
            pool.wait_ge(setup, 2)
            done(nc.gpsimd.affine_select(out=ident_f[:, :], in_=ident_f[:, :], compare_op=ALU.not_equal, fill=1.0,
                                         base=0, pattern=[[-1, P]], channel_multiplier=1))
            assert n_setup == SETUP_IDENT

            def setup_others():
                for m in (ident_b, mask_b):
                    done(nc.gpsimd.memset(m[:], 0.0))
                pool.wait_ge(setup, SETUP_IDENT + 2)
                done(nc.gpsimd.affine_select(out=ident_b[:, :], in_=ident_b[:, :], compare_op=ALU.not_equal, fill=1.0,
                                             base=0, pattern=[[-1, P]], channel_multiplier=1))
                done(nc.gpsimd.affine_select(out=mask_b[:, :, :], in_=mask_b[:, :, :], compare_op=ALU.is_ge, fill=MASKED,
                                             base=0, pattern=[[0, HG], [-1, P]], channel_multiplier=1))
                lower = k_t[0:64, :, 1, :]
                done(nc.gpsimd.memset(lower, 1.0))
                for base, step in ((-(MAX_ROW + 3), 1), (MAX_ROW + 5, -1)):
                    pool.wait_ge(setup, n_setup)
                    done(nc.gpsimd.affine_select(out=lower, in_=lower, compare_op=ALU.is_ge, fill=0.0, base=base,
                                                 pattern=[[0, G], [0, S]], channel_multiplier=step))
                done(nc.gpsimd.memset(v_aug[:, :, :, D + 1:32], 0.0))
                done(nc.gpsimd.memset(v_aug[:, :, :, D:D + 1], 1.0))
                assert n_setup == SETUP

            def rstd(stats, n, var, ve, out, chain, k, ready):
                wait_apart(pool, stats, n)
                nc.gpsimd.tensor_scalar(ve[:, :], var[:, :, 1], LN_EPS, None, ALU.add).then_inc(chain, 1)
                pool.wait_ge(chain, k)
                nc.gpsimd.tensor_tensor(out[:, :], ve[:, :], neg_half[:, :], ALU.pow).then_inc(ready, 1)

            def rstd1_of(b):
                rstd(stats1, b + 1, mv1, ve1, rstd1, c_pool, 2 * b if not isinstance(b, int) or b else 1, rstd1_done)

            def rotate_products(b, k0, k1):
                pool.wait_ge(raw_done, 2 * b + 2)
                for out, in0, in1 in rotation(0, T)[k0:k1]:
                    last = nc.gpsimd.tensor_tensor(out, in0, in1, ALU.mult)
                if k1 == 3:
                    last.then_inc(c_pool, 1)

            def rotate_sums(b):
                pool.wait_ge(c_pool, 2 * b + 1)
                pool.wait_ge(low_q_done, b)
                pool.wait_ge(parts_done, b)
                for out, in0, in1 in rotation_sums(0, T):
                    last = nc.gpsimd.tensor_tensor(out, in0, in1, ALU.add)
                last.then_inc(rope_done, 1)

            def split_rests(b):
                pool.wait_ge(high_done, 2 * b + 1)
                nc.gpsimd.tensor_tensor(rest_q[:, :, :], rq[:, :, :], q_slots[:, :, 0, :], ALU.subtract)\
                  .then_inc(rest_done, 1)
                pool.wait_ge(high_done, 2 * b + 2)
                nc.gpsimd.tensor_tensor(rest_k[:, :, :], rk[:, :, :], k_slots[:, :, 0, 2, :], ALU.subtract)\
                  .then_inc(rest_done, 1)

            def low_q(b):
                pool.wait_ge(mid_done, 2 * b + 1)
                nc.gpsimd.tensor_tensor(q_slots[:, :, 4, :], rest_q[:, :, :], q_slots[:, :, 3, :], ALU.subtract)\
                  .then_inc(low_q_done, 1)

            def values(b, g0, g1):
                wait_from(pool, pv_full, 4 * b + g1 - 4)
                wait_apart(pool, raw_done, 2 * b + 2)
                v = raw[:, :, HK * D:QKV].rearrange("p t (g d) -> p t g d", d=D)
                nc.gpsimd.tensor_copy(v_aug[:, :, g0:g1, 0:D], v[:, :, g0:g1, :]).then_inc(v_done, 1)

            def clear_later_keys(n, g, k):
                pr = probs[:, g % 2]
                units = [(4, 0, 4, 0), (8, 4, 8, 0), (8, 4, 8, 384), (10, 8, 10, None)]
                after, u0, u1_, col = units[k]
                wait_apart(pool, exp_done, EXP_UNITS * n + after)
                if col is None:
                    v = pr[:, u0:u1_, :].rearrange("p u (i q) -> p (u i) q", i=2)[:, :, 0:P]
                else:
                    v = pr[:, u0:u1_, col:col + P]
                nc.gpsimd.affine_select(out=v, in_=v, compare_op=ALU.is_ge, fill=0.0, base=0,
                                        pattern=[[0, 4], [1, P]], channel_multiplier=-1).then_inc(masked, 1)

            def add_out_bias(b):
                pool.wait_ge(xres_in, 16 * (b + 1))
                pool.wait_ge(big_in, 32)
                pool.wait_ge(stats2, b + 1)
                nc.gpsimd.tensor_tensor(x_bias[:, :, :], x_res[:, :, :],
                                        bout_row.rearrange("p (o d) -> p o d", o=1).to_broadcast([P, T, E]),
                                        ALU.add).then_inc(bias_added, 1)

            def rstd2_of(b):
                rstd(stats2, b + 2, mv2, ve2, rstd2, c_pool2, b + 1, rstd2_done)

            def step(b, first=False, last=False):
                for g in range(G):
                    n = 4 * b + g
                    if g == 0 and not last:
                        rstd1_of(b + 1)
                    if g == 1 and not last:
                        rotate_sums(b + 1)
                    clear_later_keys(n, g, 0)
                    if g == 0 and not first:
                        values(b, 3, 4)
                        add_out_bias(b - 1)
                    if g == 1 and not last:
                        split_rests(b + 1)
                        low_q(b + 1)
                    clear_later_keys(n, g, 1)
                    clear_later_keys(n, g, 2)
                    if g == 0 and not last:
                        rotate_products(b + 1, 0, 1)
                    clear_later_keys(n, g, 3)
                    if g == 0 and not first:
                        rstd2_of(b - 1)
                    if g == 0 and not last:
                        rotate_products(b + 1, 1, 3)
                    if g == 3 and not last:
                        values(b + 1, 0, 3)

            rstd1_of(0)
            setup_others()
            pool.wait_ge(tab_in, 16)
            values(0, 0, 3)
            values(0, 3, 4)
            step(0, first=True)
            with pool.Fori(1, B - 1) as b:
                step(b)
            step(B - 1, last=True)
            add_out_bias(B - 1)
            rstd2_of(B - 1)

        @block.scalar
        def _(act):
            def a_read(b, name, g=0):
                act.wait_ge(a_full, a_index(b, name, g) + 1)

            def raw_copy(b, j):
                if isinstance(b, int) and b == 0:
                    act.wait_ge(first_full, 3 + j)
                    src = first_qkv[j]
                else:
                    bank, k = f_use(b, f"qkv{j}")
                    act.wait_ge(f_full[bank], k + 1)
                    src = f_ps[:, bank, :]
                if j == 0:
                    wait_from(act, rope_done, b)
                    wait_from(act, v_done, 2 * b)
                nc.scalar.activation(raw[:, 2 * j:2 * j + 2, :],
                                     src[:, 0:2 * QKV].rearrange("p (t c) -> p t c", t=2), ACT.Copy)\
                  .then_inc(raw_done, 1)

            def k_t_copy(n, step, slot, g):
                if slot is None:
                    act.wait_ge(first_full, (6, 8)[n])
                    src = first_k_t[n]
                else:
                    a_read(step, "k_t", slot)
                    src = a_bf
                wait_from(act, sc_full, EXP_UNITS * (n - 3))
                nc.scalar.activation(k_t[0:64, g, 0, :], src[0:64, 0:S], ACT.Copy)
                nc.scalar.activation(k_t[64:P, g, 1, :], src[64:P, 0:S], ACT.Copy).then_inc(kt_done, 1)

            def max_t_copy(n, step, slot):
                if slot is None:
                    act.wait_ge(first_full, 9)
                    src = first_max_t
                else:
                    a_read(step, "max_t", slot)
                    src = a_bf
                wait_from(act, max_rows_in, 32 * n)
                nc.scalar.activation(max_t[:, :], src[0:3 * HG, 0:S], ACT.Copy)\
                  .then_inc(maxt_done, 1)

            def exp_unit(n, g, k):
                if k == 0:
                    wait_from(act, pv_full, n - 1)
                act.wait_ge(sc_full, EXP_UNITS * n + k + 1)
                nc.scalar.activation(probs[:, g % 2, k, :], sc_ps[:, k % 2, :], ACT.Exp, scale=SCALE)\
                  .then_inc(exp_done, 1)

            def o_copy(n):
                act.wait_ge(pv_full, n + 1)
                wait_from(act, att_done, n)
                nc.scalar.activation(o_sb[:, :], pv_ps[:, :], ACT.Copy).then_inc(o_copied, 1)

            def u_copy(b):
                act.wait_ge(logit_read, b + 1)
                nc.scalar.activation(u[:, :].rearrange("p (k t r) -> p k t r", k=2, t=2), router_ps[:, :, :, 0:P], ACT.Copy)\
                  .then_inc(u_copied, 1)

            def repeat_high_q(b):
                act.wait_ge(high_done, 2 * b + 1)
                nc.scalar.activation(q_slots[:, :, 1:3, :], q_slots[:, :, 0:1, :].to_broadcast([P, T * H, 2, D]), ACT.Copy)

            def repeat_mid_q(b):
                act.wait_ge(mid_done, 2 * b + 1)
                nc.scalar.activation(q_slots[:, :, 5, :], q_slots[:, :, 3, :], ACT.Copy).then_inc(repeated, 1)

            def repeat_k(b):
                act.wait_ge(parts_done, b + 1)
                nc.scalar.activation(k_slots[:, :, 1, 0:6, :], k_slots[:, :, 0, 0:6, :], ACT.Copy).then_inc(repeated, 1)

            def f_copy(b, name, out, ready):
                bank, k = f_use(b, name)
                act.wait_ge(f_full[bank], k + 1)
                nc.scalar.activation(out[:, :], f_ps[:, bank, :], ACT.Copy).then_inc(ready, 1)

            def a_copy(b, name, out):
                a_read(b + 1, name)
                nc.scalar.activation(out[:, :], a_ps[:, :], ACT.Copy).then_inc(ut_done, 1)

            def router_exp(b):
                act.wait_ge(logit_done, b + 1)
                nc.scalar.activation(ex[:, :, :], logit[:, :, :], ACT.Exp).then_inc(ex_done, 1)

            def relu(b, c, last=False):
                if last:
                    act.wait_ge(last_full, c + 1)
                    src = last_hidden[c]
                else:
                    bank, k = f_use(b, f"c{c}")
                    act.wait_ge(f_full[bank], k + 1)
                    src = f_ps[:, bank, :]
                act.wait_ge(hid_done, FC * (b + 1))
                nc.scalar.activation(relu1[:, c, :], src, ACT.Relu, bias=bi[:, c:c + 1])\
                  .then_inc(relu_done, 1)

            def ffn_task(b, g, p):
                if (g, p) == ACT_AT["xn2_t"]:
                    f_copy(b, "xn2_t", xn2_t, xn2t_done)
                if (g, p) == ACT_AT["exp"]:
                    router_exp(b)
                if (g, p) == ACT_AT["u"]:
                    u_copy(b)
                if (g, p) == ACT_AT["u1_t"]:
                    a_copy(b, "u1_t", u1_t)
                if (g, p) == ACT_AT["ud_t"]:
                    a_copy(b, "ud_t", ud_t)
                if (g, p) in ACT_AT["relu"]:
                    relu(b, ACT_AT["relu"].index((g, p)))

            def step(b, first=False, last=False):
                for g in range(G):
                    n = 4 * b + g
                    for p in range(NPOS):
                        if p == ACT_SLOT["max_t"][g > 0] and not (last and g == 3):
                            max_t_copy(n + 1, b, g)
                        if p == ACT_SLOT["k_t"][g > 0] and not (last and g >= 2):
                            k_t_copy(n + 2, b, g, (g + 2) % G)
                        if p < EXP_UNITS:
                            exp_unit(n, g, p)
                        if (g, p) == ACT_AT["xn1_t"] and not last:
                            f_copy(b + 1, "xn1_t", xn1_t, xn1t_done)
                        if p == ACT_SLOT["o"][g > 0] and not (first and g == 0):
                            o_copy(n - 1)
                        for j in range(2):
                            if (g, p) == ACT_AT[f"qkv{j}"] and not last:
                                raw_copy(b + 1, j)
                        for name, task in (("high_q", repeat_high_q), ("mid_q", repeat_mid_q), ("k", repeat_k)):
                            if (g, p) == ACT_AT[name] and not last:
                                task(b + 1)
                        if not first:
                            ffn_task(b - 1, g, p)

            act.wait_ge(wqkv_ps, 1)
            nc.scalar.activation(wqkv[:, :], max_ps[:, 0, 0:QKV], ACT.Copy).then_inc(wqkv_done, 1)
            for h, ready in enumerate((first_xn1t_done, xn1t_done)):
                act.wait_ge(first_full, h + 1)
                nc.scalar.activation(xn1_t[:, HALF[h]], first_xn1_t[h][:, HALF[h]], ACT.Copy).then_inc(ready, 1)
            raw_copy(0, 0)
            raw_copy(0, 1)
            repeat_high_q(0)
            repeat_mid_q(0)
            repeat_k(0)
            act.wait_ge(cleared, 1)
            k_t_copy(0, -1, None, 0)
            act.wait_ge(first_full, 7)
            nc.scalar.activation(q_t[:, 1, :, :].rearrange("p a q -> p (a q)"), first_q_t[1], ACT.Copy)\
              .then_inc(qt_done, 1)
            k_t_copy(1, -1, None, 1)
            max_t_copy(0, -1, None)
            act.wait_ge(big_in, 32)
            step(0, first=True)
            with act.Fori(1, B - 1) as b:
                step(b)
            step(B - 1, last=True)
            act.wait_ge(pv_full, 4 * B)
            act.wait_ge(att_done, 4 * B - 1)
            for h, ready in enumerate((last_o, o_copied)):
                nc.scalar.activation(o_sb[:, HALF[h]], pv_ps[:, HALF[h]], ACT.Copy).then_inc(ready, 1)
            act.wait_ge(f_full[0], f_use(B - 1, "xn2_t")[1] + 1)
            nc.scalar.activation(xn2_t[:, HALF[0]], last_xn2_t_ps[0][:, HALF[0]], ACT.Copy).then_inc(last_xn2t_done, 1)
            act.wait_ge(last_xn2_t, 1)
            nc.scalar.activation(xn2_t[:, HALF[1]], last_xn2_t_ps[1][:, HALF[1]], ACT.Copy).then_inc(xn2t_done, 1)
            router_exp(B - 1)
            u_copy(B - 1)
            a_copy(B - 1, "u1_t", u1_t)
            relu(B - 1, 0, last=True)
            relu(B - 1, 1, last=True)
            a_copy(B - 1, "ud_t", ud_t)
            relu(B - 1, 2, last=True)
            relu(B - 1, 3, last=True)

        @block.vector
        def _(dve):
            def norm_stats(xs, st, mv, chain, k, ready):
                for t in range(T):
                    last = nc.vector.bn_stats(st[:, t, :], xs[:, t, :])
                last.then_inc(chain, 1)
                wait_apart(dve, chain, k)
                for t in range(T):
                    last = nc.vector.bn_aggr(mv[:, t, :], st[:, t, :])
                last.then_inc(ready, 1)

            def normalise(xs, mv, rs, out, tiles, ready, first_ready=None):
                for t in tiles:
                    last = nc.vector.tensor_scalar(out[:, t, :], xs[:, t, :], mv[:, t, 0:1], rs[:, t:t + 1],
                                                   ALU.subtract, ALU.mult)
                if t == T - 1:
                    last.then_inc(ready, 1)
                elif first_ready is not None:
                    last.then_inc(first_ready, 1)

            def stats1_of(b):
                dve.wait_ge(x_in, 16 * (b + 1))
                norm_stats(x_sb, st1, mv1, c_prep, b + 1, stats1)

            def normalise1(b, half, first_ready=None):
                dve.wait_ge(rstd1_done, b + 1)
                wait_from(dve, xn1t_done, b)
                normalise(x_sb, mv1, rstd1, xn1, range(2 * half, 2 * half + 2), xn1_done, first_ready)

            def rotate_first(j):
                dve.wait_ge(raw_done, j + 1)
                dve.wait_ge(tab_in, 16)
                for out, in0, in1 in rotation(2 * j, 2 * j + 2):
                    last = nc.vector.tensor_tensor(out, in0, in1, ALU.mult)
                last.then_inc(c_rotate, 1)
                dve.wait_ge(c_rotate, j + 1)
                for out, in0, in1 in rotation_sums(2 * j, 2 * j + 2):
                    last = nc.vector.tensor_tensor(out, in0, in1, ALU.add)
                if j == 1:
                    last.then_inc(rope_done, 1)

            def high_q(b):
                dve.wait_ge(rope_done, b + 1)
                wait_from(dve, qt_done, 4 * b)
                nc.vector.tensor_copy(q_slots[:, :, 0, :], rq[:, :, :]).then_inc(high_done, 1)

            def high_k(b):
                wait_from(dve, kt_done, 4 * b)
                nc.vector.tensor_copy(k_slots[:, :, 0, 2:5, :], rk[:, :, :].rearrange("p r (o d) -> p r o d", o=1)
                                      .to_broadcast([P, T * G, 3, D])).then_inc(high_done, 1)

            def rests_first():
                dve.wait_ge(high_done, 1)
                nc.vector.tensor_tensor(rest_q[:, :, :], rq[:, :, :], q_slots[:, :, 0, :], ALU.subtract).then_inc(rest_done, 1)
                dve.wait_ge(high_done, 2)
                nc.vector.tensor_tensor(rest_k[:, :, :], rk[:, :, :], k_slots[:, :, 0, 2, :], ALU.subtract).then_inc(rest_done, 1)

            def mid_q(b):
                dve.wait_ge(rest_done, 2 * b + 1)
                nc.vector.tensor_copy(q_slots[:, :, 3, :], rest_q[:, :, :]).then_inc(mid_done, 1)

            def mid_k(b):
                dve.wait_ge(rest_done, 2 * b + 2)
                nc.vector.tensor_copy(k_slots[:, :, 0, 0:6:5, :], rest_k[:, :, :].rearrange("p r (o d) -> p r o d", o=1)
                                      .to_broadcast([P, T * G, 2, D])).then_inc(mid_done, 1)

            def low_q(b):
                dve.wait_ge(mid_done, 2 * b + 1)
                nc.vector.tensor_tensor(q_slots[:, :, 4, :], rest_q[:, :, :], q_slots[:, :, 3, :], ALU.subtract)\
                  .then_inc(low_q_done, 1)

            def low_k(b):
                dve.wait_ge(mid_done, 2 * b + 2)
                nc.vector.tensor_tensor(k_slots[:, :, 0, 1, :], rest_k[:, :, :], k_slots[:, :, 0, 0, :], ALU.subtract)\
                  .then_inc(parts_done, 1)

            def q_t_copy(n, step, slot, g):
                if slot is None:
                    dve.wait_ge(first_full, 5)
                    src = first_q_t[0]
                else:
                    dve.wait_ge(a_full, a_index(step, "q_t", slot) + 1)
                    src = a_bf[:, :]
                wait_from(dve, sc_full, EXP_UNITS * (n - 3))
                nc.vector.tensor_copy(q_t[:, g, :, :].rearrange("p a q -> p (a q)"), src)\
                  .then_inc(qt_done, 1)

            def max_unit(n, g, k):
                t, h0, nh, width = max_place(k)
                dve.wait_ge(max_full, MAX_UNITS * n + k + 1)
                if k == 0:
                    wait_from(dve, max_parts_done, n)
                src = max_ps[:, (g + k) % 2, 0:nh * width].rearrange("p (h k) -> p h k", h=nh)
                nc.vector.tensor_reduce(neg_max[:, t, h0:h0 + nh], src, AX.X, ALU.max, negate=True)\
                  .then_inc(max_done, 1)

            def split_max(n):
                dve.wait_ge(max_done, MAX_UNITS * (n + 1))
                wait_from(dve, maxt_done, n)
                nc.vector.tensor_copy(max_parts[:, :, :, 0], neg_max[:, :, :]).then_inc(c_max, 1)
                dve.wait_ge(c_max, 3 * n + 1)
                nc.vector.tensor_tensor(max_rest[:, :, :], neg_max[:, :, :], max_parts[:, :, :, 0], ALU.subtract)\
                  .then_inc(c_max, 1)
                dve.wait_ge(c_max, 3 * n + 2)
                nc.vector.tensor_copy(max_parts[:, :, :, 1], max_rest[:, :, :]).then_inc(c_max, 1)
                dve.wait_ge(c_max, 3 * n + 3)
                nc.vector.tensor_tensor(max_parts[:, :, :, 2], max_rest[:, :, :], max_parts[:, :, :, 1], ALU.subtract)\
                  .then_inc(max_parts_done, 1)

            def normalise_att(n, b, step, slot, g):
                dve.wait_ge(a_full, a_index(step, "out_t", slot) + 1)
                v = a_ps[:, :].rearrange("p (t h d) -> p t h d", t=T, h=HG)
                nc.vector.reciprocal(rcp[:, :, :], v[:, :, :, D]).then_inc(c_att, 1)
                dve.wait_ge(c_att, n + 1)
                if g == 0:
                    wait_from(dve, att_t_done, b)
                nc.vector.tensor_tensor(att[:, :, HG * g:HG * g + HG, :], v[:, :, :, 0:D],
                                        rcp[:, :, :].rearrange("p t (h o) -> p t h o", o=1)
                                        .to_broadcast([P, T, HG, D]), ALU.mult).then_inc(att_done, 1)

            def att_t_copy(b):
                bank, k = f_use(b, "att_t")
                dve.wait_ge(f_full[bank], k + 1)
                nc.vector.tensor_copy(att_t[:, :], f_ps[:, bank, :]).then_inc(att_t_done, 1)

            def residual(b):
                bank, k = f_use(b, "x1")
                dve.wait_ge(f_full[bank], k + 1)
                dve.wait_ge(bias_added, b + 1)
                dve.wait_ge(y_done, b + 1)
                nc.vector.tensor_tensor(x1[:, :, :], f_ps[:, bank, :].rearrange("p (t d) -> p t d", t=T),
                                        x_bias[:, :, :], ALU.add).then_inc(x1_done, 1)

            def stats2_of(b):
                dve.wait_ge(x1_done, b + 1)
                norm_stats(x1, st2, mv2, c_ffn, (ROUTER_CHAIN + 1) * b + 1, stats2)

            def normalise2(b, half, first_ready=None):
                dve.wait_ge(rstd2_done, b + 1)
                normalise(x1, mv2, rstd2, xn2, range(2 * half, 2 * half + 2), xn2_done, first_ready)

            def over(a):
                return a[:, :].rearrange("p (t o) -> p t o", o=1).to_broadcast([P, T, NE])

            ROUTER_CHAIN = 9

            def linked(b, i):
                dve.wait_ge(c_ffn, (ROUTER_CHAIN + 1) * b + (i + 1))

            def link(ins):
                ins.then_inc(c_ffn, 1)

            rank = rank_row.rearrange("p (o e) -> p o e", o=1).to_broadcast([P, 2 * T, NE])
            tie1, tie2 = tie[:, :, 0, :], tie[:, :, 1, :]

            def router_logits(b):
                for name in ("router0", "router1"):
                    bank, k = f_use(b, name)
                    dve.wait_ge(f_full[bank], k + 1)
                nc.vector.tensor_tensor(logit[:, :, :].rearrange("p (k t) e -> p k t e", k=2), router_ps[:, :, :, P:P + NE],
                                        gate_b_row.rearrange("p (k t e) -> p k t e", k=1, t=1).to_broadcast([P, 2, 2, NE]),
                                        ALU.add).then_inc(logit_read, 1)
                dve.wait_ge(logit_read, b + 1)
                link(nc.vector.tensor_reduce(lmax[:, :], logit[:, :, :], AX.X, ALU.max))
                linked(b, 1)
                nc.vector.tensor_tensor(logit[:, :, :], logit[:, :, :], over(lmax), ALU.subtract)\
                  .then_inc(logit_done, 1)

            def router_best(b):
                dve.wait_ge(ex_done, b + 1)
                nc.vector.tensor_reduce(esum[:, :], ex[:, :, :], AX.X, ALU.add)
                for t in range(T):
                    last = nc.vector.max(out=best[:, t, :], in_=ex[:, t, :])
                link(last)

            def router_ties(b):
                linked(b, 2)
                link(nc.vector.tensor_tensor(tie[:, :, :, :],
                                             ex[:, :, :].rearrange("p t (o e) -> p t o e", o=1).to_broadcast([P, T, 2, NE]),
                                             best[:, :, 0:2].rearrange("p t (k o) -> p t k o", o=1)
                                             .to_broadcast([P, T, 2, NE]), ALU.is_equal))
                nc.vector.tensor_tensor(tsum[:, :], best[:, :, 0], best[:, :, 1], ALU.add)
                linked(b, 3)
                both = tie[:, :, :, :].rearrange("p t k e -> p (t k) e")
                link(nc.vector.tensor_tensor(both, both, rank, ALU.mult))

            def router_first(b):
                linked(b, 4)
                link(nc.vector.tensor_reduce(tmax[:, :], tie1, AX.X, ALU.max))
                nc.vector.reciprocal(ersum[:, :], esum[:, :])
                linked(b, 5)
                link(nc.vector.tensor_tensor(hot1[:, :, :], tie1, over(tmax), ALU.is_equal))

            def router_others(b):
                linked(b, 6)
                link(nc.vector.scalar_tensor_tensor(out=tie2, in0=hot1[:, :, :], scalar=-2.0 * NE, in1=tie2,
                                                    op0=ALU.mult, op1=ALU.add))
                nc.vector.tensor_tensor(gate[:, :], tsum[:, :], ersum[:, :], ALU.mult)
                linked(b, 7)
                link(nc.vector.tensor_reduce(tmax[:, :], tie2, AX.X, ALU.max))

            def router_second(b):
                linked(b, 8)
                link(nc.vector.tensor_tensor(hot2[:, :, :], tie2, over(tmax), ALU.is_equal))
                linked(b, 9)
                nc.vector.tensor_tensor(hot_d[:, :, :], hot2[:, :, :], hot1[:, :, :], ALU.subtract).then_inc(hot_done, 1)

            def low_rank(b, expert):
                dve.wait_ge(u_copied, b + 1)
                if expert == 0:
                    linked(b, 6)
                else:
                    dve.wait_ge(hot_done, b + 1)
                out, hot = ((u1, hot1), (ud, hot_d))[expert]
                nc.vector.tensor_tensor(out[:, :, :, :], u[:, :].rearrange("p (t e r) -> p t e r", t=T, e=NE),
                                        hot[:, :, :].rearrange("p t (e o) -> p t e o", o=1)
                                        .to_broadcast([P, T, NE, R]), ALU.mult).then_inc(u_done, 1)

            def hidden(b, c, last=False):
                if last:
                    dve.wait_ge(last_full, FC + c + 1)
                    src = last_hidden[c]
                else:
                    bank, k = f_use(b, f"c{c}+")
                    dve.wait_ge(f_full[bank], k + 1)
                    src = f_ps[:, bank, :]
                nc.vector.scalar_tensor_tensor(out=hid[:, c, :], in0=src, scalar=neg_bi[:, c:c + 1],
                                               in1=relu1[:, c, :], op0=ALU.max, op1=ALU.add).then_inc(hid_done, 1)

            def output_rest(b, half):
                dve.wait_ge(hot_done, b + 1)
                for t in range(2 * half, 2 * half + 2):
                    last = nc.vector.scalar_tensor_tensor(out=y_rest[:, t, :], in0=out_const[:, :], scalar=gate[:, t:t + 1],
                                                          in1=x1[:, t, :], op0=ALU.mult, op1=ALU.add)
                if half == 1:
                    last.then_inc(rest_y_done, 1)

            def output_tile(b, t, src):
                return nc.vector.scalar_tensor_tensor(out=y_sb[:, t, :], in0=src,
                                                      scalar=gate[:, t:t + 1], in1=y_rest[:, t, :],
                                                      op0=ALU.mult, op1=ALU.add)

            def output(b, half):
                bank, k = f_use(b, "ffn")
                dve.wait_ge(f_full[bank], k + 1)
                dve.wait_ge(rest_y_done, b + 1)
                dve.wait_ge(y_out, 16 * (b + 1))
                for t in range(2 * half, 2 * half + 2):
                    last = output_tile(b, t, f_ps[:, bank, t * P:(t + 1) * P])
                if half == 1:
                    last.then_inc(y_done, 1)

            def tasks_at(table, b, g, p):
                for name, tasks in table:
                    places = DVE_AT[name] if isinstance(DVE_AT[name], list) else [DVE_AT[name]]
                    for k, task in enumerate(tasks):
                        if (g, p) == places[k]:
                            task(b)

            def halves(task):
                return [lambda b: task(b, 0), lambda b: task(b, 1)]

            FFN_TASKS = [
                ("att_t", [att_t_copy]), ("x1", [residual]), ("stats2", [stats2_of]), ("normalise2", halves(normalise2)),
                ("logits", [router_logits]), ("best", [router_best]), ("ties", [router_ties]), ("first", [router_first]),
                ("u1", [lambda b: low_rank(b, 0)]), ("others", [router_others]), ("second", [router_second]),
                ("ud", [lambda b: low_rank(b, 1)]), ("output_rest", halves(output_rest)),
                ("hidden", [lambda b, c=c: hidden(b, c) for c in range(FC)]), ("output", halves(output))]
            PREP_TASKS = [("normalise1", halves(normalise1)), ("high_q", [high_q]), ("high_k", [high_k]),
                          ("mid_q", [mid_q]), ("mid_k", [mid_k]), ("low_k", [low_k])]

            def step(b, first=False, last=False):
                for g in range(G):
                    n = 4 * b + g
                    for p in range(NPOS):
                        if p == MAX_UNITS - MAX_LEAD and not (last and g == 3):
                            split_max(n + 1)
                        if (g, p) == (0, 0) and not last:
                            stats1_of(b + 1)
                        m, place, k = max_at(n, g, p)
                        if not (last and (g == 3 or g == 2 and k < MAX_LEAD)):
                            max_unit(m, place, k)
                        if p == DVE_SLOT["q_t"][g > 0] and not (last and g >= 2):
                            q_t_copy(n + 2, b, g, (g + 2) % G)
                        if p == DVE_SLOT["att"][g > 0] and not (first and g == 0):
                            normalise_att(n - 1, b if g else b - 1, b, g, (g - 1) % G)
                        if not last:
                            tasks_at(PREP_TASKS, b + 1, g, p)
                        if not first:
                            tasks_at(FFN_TASKS, b - 1, g, p)

            stats1_of(0)
            nc.vector.memset(q_parts[:, :, MAX_ROW:], 0.0)
            nc.vector.memset(k_parts[:, :, 0, MAX_ROW:MAX_ROW + 3], 1.0)
            nc.vector.memset(k_parts[:, :, 0, MAX_ROW + 3:], 0.0)
            nc.vector.memset(k_parts[:, :, 1, MAX_ROW:], 0.0)
            normalise1(0, 0, first_xn1)
            normalise1(0, 1)
            nc.vector.memset(k_t[64:P, :, 0, :].bitcast(F32), 0.0).then_inc(cleared, 1)
            rotate_first(0)
            rotate_first(1)
            high_q(0)
            high_k(0)
            rests_first()
            for task in (mid_q, mid_k, low_q, low_k):
                task(0)
            q_t_copy(0, -1, None, 0)
            dve.wait_ge(big_in, 32)
            nc.vector.tensor_scalar(neg_bi[:, :], bi, -1.0, None, ALU.mult)
            dve.wait_ge(const_ps, 1)
            nc.vector.scalar_tensor_tensor(out=out_const[:, :], in0=bo_row, scalar=2.0, in1=max_ps[:, 1, 0:E],
                                           op0=ALU.mult, op1=ALU.add).then_inc(const_done, 1)
            for k in range(MAX_UNITS):
                max_unit(0, 0, k)
            split_max(0)
            for k in range(MAX_LEAD):
                max_unit(1, 1, k)
            step(0, first=True)
            with dve.Fori(1, B - 1) as b:
                step(b)
            step(B - 1, last=True)
            b = B - 1
            for h, (full, value, ready) in enumerate(((a_full, a_index(B, "out_t") + 1, last_att), (last_out_t, 1, att_done))):
                dve.wait_ge(full, value)
                v = last_out_ps[h][:, HALF[h]].rearrange("p (t h d) -> p t h d", t=2, h=HG)
                tiles = slice(2 * h, 2 * h + 2)
                nc.vector.reciprocal(rcp[:, tiles, :], v[:, :, :, D]).then_inc(c_att, 1)
                dve.wait_ge(c_att, 4 * B + h)
                nc.vector.tensor_tensor(att[:, tiles, HG * 3:H, :], v[:, :, :, 0:D],
                                        rcp[:, tiles, :].rearrange("p t (h o) -> p t h o", o=1)
                                        .to_broadcast([P, 2, HG, D]), ALU.mult).then_inc(ready, 1)
            for h, (full, value, ready) in enumerate(((f_full[1], f_use(b, "att_t")[1] + 1, last_att_t_done),
                                                      (last_att_t, 1, att_t_done))):
                dve.wait_ge(full, value)
                nc.vector.tensor_copy(att_t[:, HALF[h]], last_att_t_ps[h][:, HALF[h]]).then_inc(ready, 1)
            dve.wait_ge(bias_added, B)
            dve.wait_ge(y_done, B)
            for h, (full, value, ready) in enumerate(((last_x1, 1, last_x1_done), (f_full[1], f_use(b, "x1")[1] + 1, x1_done))):
                dve.wait_ge(full, value)
                nc.vector.tensor_tensor(x1[:, 2 * h:2 * h + 2, :],
                                        last_x1_ps[h][:, HALF[h]].rearrange("p (t d) -> p t d", t=2),
                                        x_bias[:, 2 * h:2 * h + 2, :], ALU.add).then_inc(ready, 1)
            dve.wait_ge(last_x1_done, 1)
            stats2_of(b)
            normalise2(b, 0, last_xn2)
            normalise2(b, 1)
            router_logits(b)
            router_best(b)
            router_ties(b)
            router_first(b)
            low_rank(b, 0)
            router_others(b)
            router_second(b)
            low_rank(b, 1)
            output_rest(b, 0)
            output_rest(b, 1)
            for c in range(FC):
                hidden(b, c, last=True)
            dve.wait_ge(rest_y_done, b + 1)
            dve.wait_ge(y_out, 16 * (b + 1))
            for t in range(T):
                dve.wait_ge(last_full, 2 * FC + t + 1)
                output_tile(b, t, last_down[t]).then_inc(last_y, 1)

        @block.tensor
        def _(pe):
            def a_write(step, name, g=0):
                wait_from(pe, *a_previous(step, name, g))

            def f_write(b, name):
                for semaphore, value in f_previous(b, name):
                    pe.wait_ge(semaphore, value)
                return f_bank(name)

            def project(b, j):
                if isinstance(b, int) and b == 0:
                    out, ready = first_qkv[j], first_full
                else:
                    bank = f_write(b, f"qkv{j}")
                    out, ready = f_ps[:, bank, :], f_full[bank]
                if isinstance(b, int) and b == 0 and j == 0:
                    pe.wait_ge(first_xn1t_done, 1)
                else:
                    pe.wait_ge(xn1t_done, b + 1)
                for i in range(2):
                    t = 2 * j + i
                    last = nc.tensor.matmul(out[:, i * QKV:(i + 1) * QKV], xn1_t[:, t * P:(t + 1) * P], wqkv[:, :],
                                            start=True, stop=True)
                last.then_inc(ready, 1)

            def xn1_transpose(b):
                f_transpose(b, "xn1_t", lambda t: xn1[:, t, :], xn1_done, b + 1)

            def q_transpose(b, step, slot, g):
                if slot is None:
                    out, ready = first_q_t[g], first_full
                else:
                    a_write(step, "q_t", slot)
                    out, ready = a_bf, a_full
                pe.wait_ge(low_q_done, b + 1)
                pe.wait_ge(repeated, 2 * b + 1)
                for pp in range(2):
                    for t in range(T):
                        h = t * H + HG * g + 2 * pp
                        last = nc.tensor.transpose(out[:, pp * S + t * P:pp * S + (t + 1) * P],
                                                   q_parts[:, h:h + 2, :].rearrange("p h r -> p (h r)"), ident_b[:, :])
                last.then_inc(ready, 1)

            def k_transpose(b, step, slot, g):
                if slot is None:
                    out, ready = first_k_t[g], first_full
                else:
                    a_write(step, "k_t", slot)
                    out, ready = a_bf, a_full
                pe.wait_ge(repeated, 2 * b + 2)
                for t in range(T):
                    last = nc.tensor.transpose(out[:, t * P:(t + 1) * P],
                                               k_parts[:, t * G + g, :, :].rearrange("p e r -> p (e r)"), ident_b[:, :])
                last.then_inc(ready, 1)

            def max_unit(n, g, k):
                t, h0, nh, width = max_place(k)
                if k == 0:
                    pe.wait_ge(qt_done, n + 1)
                    pe.wait_ge(kt_done, n + 1)
                wait_from(pe, max_done, MAX_UNITS * n + k - 1)
                bank = max_ps[:, (g + k) % 2, 0:nh * width].rearrange("p (h k) -> p h k", h=nh)
                for i in range(nh):
                    h = h0 + i
                    nc.tensor.matmul(bank[:, i, :], q_t[:, g, h // 2, t * P:(t + 1) * P], k_t[:, g, h % 2, 0:width],
                                     start=i == 0, stop=False, skip_group_check=True)
                nc.tensor.matmul(bank[:, :, width - P:width], ident_b[:, :], mask_b[:, 0:nh, :],
                                 start=False, stop=True, skip_group_check=True).then_inc(max_full, 1)

            def max_transpose(n, step, slot):
                if slot is None:
                    out, ready = first_max_t, first_full
                else:
                    a_write(step, "max_t", slot)
                    out, ready = a_bf, a_full
                pe.wait_ge(max_parts_done, n + 1)
                for t in range(T):
                    last = nc.tensor.transpose(out[0:3 * HG, t * P:(t + 1) * P],
                                               max_parts[:, t, :, :].rearrange("p h c -> p (h c)"), ident_b[:, :])
                last.then_inc(ready, 1)

            def exp_unit(n, g, k):
                if k == 0:
                    pe.wait_ge(max_rows_in, 32 * (n + 1))
                wait_from(pe, exp_done, EXP_UNITS * n + k - 1)
                for h, j, col in exp_place(k):
                    last = nc.tensor.matmul(sc_ps[:, k % 2, col:col + S - j * P], k_t[:, g, h % 2, j * P:(j + 1) * P],
                                            q_t[:, g, h // 2, j * P:S], start=True, stop=True)
                last.then_inc(sc_full, 1)

            def weigh_values(n, b, g, k):
                j = (0, 1, 3, 2)[k]
                if k == 0:
                    wait_from(pe, o_copied, n)
                    pe.wait_ge(v_done, 2 * b + (2 if g == G - 1 else 1))
                pe.wait_ge(masked, 4 * n + k + 1)
                for h in range(HG):
                    unit, col = next((u, c) for u in range(EXP_UNITS) for hh, jj, c in exp_place(u) if (hh, jj) == (h, j))
                    last = nc.tensor.matmul(pv_ps[32 * h:32 * h + 32, j * P:S], v_aug[:, j, g, :],
                                            probs[:, g % 2, unit, col:col + S - j * P], start=k == 0, stop=k == 3,
                                            skip_group_check=True)
                if k == 3:
                    last.then_inc(pv_full, 1)

            def out_transpose(n, step, slot):
                a_write(step, "out_t", slot)
                pe.wait_ge(o_copied, n + 1)
                for t in range(T):
                    last = nc.tensor.transpose(a_ps[:, t * P:(t + 1) * P], o_sb[:, t * P:(t + 1) * P], ident_f[:, :])
                last.then_inc(a_full, 1)

            def f_transpose(b, name, src, ready, value):
                bank = f_write(b, name)
                pe.wait_ge(ready, value)
                for t in range(T):
                    last = nc.tensor.transpose(f_ps[:, bank, t * P:(t + 1) * P], src(t), ident_f[:, :])
                last.then_inc(f_full[bank], 1)

            def token_major(b, name, lhs, rhs, tiles, ready, value):
                bank = f_write(b, name)
                pe.wait_ge(ready, value)
                width = rhs.shape[1]
                for i, t in enumerate(tiles):
                    last = nc.tensor.matmul(f_ps[:, bank, i * width:(i + 1) * width], lhs[:, t * P:(t + 1) * P], rhs,
                                            start=True, stop=True)
                last.then_inc(f_full[bank], 1)

            def u_transpose(b, name, src, ready):
                a_write(b + 1, name)
                pe.wait_ge(u_done, ready)
                for t in range(T):
                    last = nc.tensor.transpose(a_ps[:, t * P:(t + 1) * P],
                                               src[:, t, :, :].rearrange("p e r -> p (e r)"), ident_f[:, :])
                last.then_inc(a_full, 1)

            def base(b, c, last=False):
                out = last_hidden[c] if last else f_ps[:, f_write(b, f"c{c}"), :]
                nc.tensor.matmul(out, wi_t[:, c, :], xn2_t[:, :], start=True, stop=False, skip_group_check=True)

            def first_expert(b, c, last=False):
                bank = f_bank(f"c{c}")
                out, ready = (last_hidden[c], last_full) if last else (f_ps[:, bank, :], f_full[bank])
                pe.wait_ge(ut_done, 2 * b + 1)
                nc.tensor.matmul(out, lb_t[:, c, :], u1_t[:, :], start=False, stop=False, skip_group_check=True)\
                  .then_inc(ready, 1)

            def second_expert(b, c, last=False):
                if last:
                    pe.wait_ge(relu_done, FC * b + c + 1)
                    out, ready = last_hidden[c], last_full
                else:
                    bank = f_write(b, f"c{c}+")
                    out, ready = f_ps[:, bank, :], f_full[bank]
                pe.wait_ge(ut_done, 2 * b + 2)
                nc.tensor.matmul(out, lb_t[:, c, :], ud_t[:, :], start=False, stop=True, skip_group_check=True)\
                  .then_inc(ready, 1)

            def down(b, t):
                if t == 0:
                    f_write(b, "ffn")
                    pe.wait_ge(hid_done, FC * (b + 2))
                bank, _ = f_use(b, "ffn")
                for c in range(FC):
                    last = nc.tensor.matmul(f_ps[:, bank, t * P:(t + 1) * P], hid[:, c, t * P:(t + 1) * P],
                                            wo_t[:, c, :], start=c == 0, stop=c == FC - 1)
                if t == T - 1:
                    last.then_inc(f_full[bank], 1)

            def att_transpose(b):
                f_transpose(b, "att_t", lambda t: att[:, t, :, :].rearrange("p h d -> p (h d)"), att_done, 4 * (b + 1))

            def xn2_transpose(b):
                f_transpose(b, "xn2_t", lambda t: xn2[:, t, :], xn2_done, b + 1)

            def router_products(b):
                token_major(b, "router0", xn2_t, la_gate_t, range(0, 2), xn2t_done, b + 1)
                token_major(b, "router1", xn2_t, la_gate_t, range(2, T), xn2t_done, b + 1)

            def ffn_task(b, g, p):
                if (g, p) == PE_AT["att_t"]:
                    att_transpose(b)
                if (g, p) == PE_AT["x1"]:
                    token_major(b, "x1", att_t, wout, range(T), att_t_done, b + 1)
                if (g, p) == PE_AT["xn2_t"]:
                    xn2_transpose(b)
                if (g, p) == PE_AT["router"]:
                    router_products(b)
                if (g, p) == PE_AT["u1_t"]:
                    u_transpose(b, "u1_t", u1, 2 * b + 1)
                if (g, p) == PE_AT["ud_t"]:
                    u_transpose(b, "ud_t", ud, 2 * b + 2)
                for c in range(FC):
                    if (g, p) == PE_AT["base"][c]:
                        base(b, c)
                    if (g, p) == PE_AT["first"][c]:
                        first_expert(b, c)
                    if (g, p) == PE_AT["second"][c]:
                        second_expert(b, c)
                if (g, p) in PE_AT["down"]:
                    down(b, PE_AT["down"].index((g, p)))

            def step(b, first=False, last=False):
                for g in range(G):
                    n = 4 * b + g
                    for p in range(NPOS):
                        if p == PE_SLOT["out_t"][g > 0] and not (first and g == 0):
                            out_transpose(n - 1, b, g)
                        m, place, k = max_at(n, g, p)
                        if not (last and (g == 3 or g == 2 and k < MAX_LEAD)):
                            max_unit(m, place, k)
                        if p < EXP_UNITS:
                            exp_unit(n, g, p)
                        for k in range(T):
                            if p == PE_SLOT["weigh"][k][g > 0] and not (first and g == 0):
                                weigh_values(n - 1, b if g else b - 1, (g - 1) % G, k)
                        if not (last and g >= 2):
                            if p == PE_SLOT["q_t"][g > 0]:
                                q_transpose(b + (g >= 2), b, g, (g + 2) % G)
                            if p == PE_SLOT["k_t"][g > 0]:
                                k_transpose(b + (g >= 2), b, g, (g + 2) % G)
                        if p == PE_SLOT["max_t"][g > 0] and not (last and g == 3):
                            max_transpose(n + 1, b, g)
                        if (g, p) == PE_AT["xn1_t"] and not last:
                            xn1_transpose(b + 1)
                        for j in range(2):
                            if (g, p) == PE_AT[f"qkv{j}"] and not last:
                                project(b + 1, j)
                        if not first:
                            ffn_task(b - 1, g, p)

            pe.wait_ge(small_in, 32)
            nc.tensor.matmul(max_ps[:, 0, 0:P], wq_in[:, 0:P], wq_in[:, P:2 * P], start=True, stop=True)
            nc.tensor.matmul(max_ps[:, 0, P:QKV], wkv_in[:, 0:P], wkv_in[:, P:P + QKV - P], start=True, stop=True)\
              .then_inc(wqkv_ps, 1)
            pe.wait_ge(setup, SETUP_IDENT)
            for h, ready in enumerate((first_xn1, xn1_done)):
                pe.wait_ge(ready, 1)
                for t in (2 * h, 2 * h + 1):
                    last = nc.tensor.transpose(first_xn1_t[h][:, t * P:(t + 1) * P], xn1[:, t, :], ident_f[:, :])
                last.then_inc(first_full, 1)
            pe.wait_ge(wqkv_done, 1)
            project(0, 0)
            project(0, 1)
            pe.wait_ge(big_in, 32)
            for c in range(FC):
                last = nc.tensor.matmul(max_ps[:, 1, 0:E], bi[:, c:c + 1].to_broadcast([P, P]), wo_t[:, c, :],
                                        start=c == 0, stop=c == FC - 1)
            last.then_inc(const_ps, 1)
            pe.wait_ge(setup, SETUP)
            pe.wait_ge(cleared, 1)
            q_transpose(0, -1, None, 0)
            k_transpose(0, -1, None, 0)
            for k in range(MAX_UNITS):
                if k == 1:
                    pe.wait_ge(const_done, 1)
                max_unit(0, 0, k)
                if k == 3:
                    q_transpose(0, -1, None, 1)
                if k == 5:
                    k_transpose(0, -1, None, 1)
            max_unit(1, 1, 0)
            max_transpose(0, -1, None)
            for k in range(1, MAX_LEAD):
                max_unit(1, 1, k)
            step(0, first=True)
            with pe.Fori(1, B - 1) as b:
                step(b)
            step(B - 1, last=True)
            b = B - 1
            for k in range(T):
                weigh_values(4 * b + 3, b, G - 1, k)
            a_write(B, "out_t")
            pe.wait_ge(max_done, 4 * B * MAX_UNITS)
            for h, (ready, value, full) in enumerate(((last_o, 1, a_full), (o_copied, 4 * B, last_out_t))):
                pe.wait_ge(ready, value)
                for t in (2 * h, 2 * h + 1):
                    last = nc.tensor.transpose(last_out_ps[h][:, t * P:(t + 1) * P], o_sb[:, t * P:(t + 1) * P], ident_f[:, :])
                last.then_inc(full, 1)
            f_write(b, "att_t")
            for h, (ready, value, full) in enumerate(((last_att, 1, f_full[1]), (att_done, 4 * B, last_att_t))):
                pe.wait_ge(ready, value)
                for t in (2 * h, 2 * h + 1):
                    last = nc.tensor.transpose(last_att_t_ps[h][:, t * P:(t + 1) * P],
                                               att[:, t, :, :].rearrange("p h d -> p (h d)"), ident_f[:, :])
                last.then_inc(full, 1)
            pe.wait_ge(exp_done, 4 * B * EXP_UNITS)
            for h, (ready, value, full) in enumerate(((last_att_t_done, 1, last_x1), (att_t_done, B, f_full[1]))):
                pe.wait_ge(ready, value)
                for t in (2 * h, 2 * h + 1):
                    last = nc.tensor.matmul(last_x1_ps[h][:, t * P:(t + 1) * P], att_t[:, t * P:(t + 1) * P], wout,
                                            start=True, stop=True)
                last.then_inc(full, 1)
            f_write(b, "xn2_t")
            for h, (ready, value, full) in enumerate(((last_xn2, 1, f_full[0]), (xn2_done, B, last_xn2_t))):
                pe.wait_ge(ready, value)
                for t in (2 * h, 2 * h + 1):
                    last = nc.tensor.transpose(last_xn2_t_ps[h][:, t * P:(t + 1) * P], xn2[:, t, :], ident_f[:, :])
                last.then_inc(full, 1)
            pe.wait_ge(last_xn2t_done, 1)
            for t in range(2):
                last = nc.tensor.matmul(f_ps[:, 0, t * (P + NE):(t + 1) * (P + NE)], xn2_t[:, t * P:(t + 1) * P],
                                        la_gate_t, start=True, stop=True)
            last.then_inc(f_full[0], 1)
            token_major(b, "router1", xn2_t, la_gate_t, range(2, T), xn2t_done, b + 1)
            pe.wait_ge(hid_done, FC * (b + 1))
            pe.wait_ge(exp_done, 4 * B * EXP_UNITS)
            for c in range(FC - 1):
                base(b, c, last=True)
            u_transpose(b, "u1_t", u1, 2 * b + 1)
            base(b, FC - 1, last=True)
            first_expert(b, 0, last=True)
            first_expert(b, 1, last=True)
            u_transpose(b, "ud_t", ud, 2 * b + 2)
            first_expert(b, 2, last=True)
            first_expert(b, 3, last=True)
            for c in range(FC):
                second_expert(b, c, last=True)
            pe.wait_ge(u_copied, b + 1)
            pe.wait_ge(o_copied, 4 * B)
            pe.wait_ge(ut_done, 2 * B)
            for c in range(FC):
                pe.wait_ge(hid_done, FC * (b + 1) + c + 1)
                for t in range(T):
                    product = nc.tensor.matmul(last_down[t], hid[:, c, t * P:(t + 1) * P], wo_t[:, c, :],
                                               start=c == 0, stop=c == FC - 1, skip_group_check=True)
                    if c == FC - 1:
                        product.then_inc(last_full, 1)


def kernel(**inputs):
    import numpy as np
    import concourse.bacc as bacc
    from concourse.bass_utils import run_bass_kernel_spmd

    w = {k: np.asarray(v) for k, v in inputs.items()}
    x = w["L0_attn_x"]
    B, S, E = x.shape
    T = S // P
    G, D = 4, 8
    H = E // D
    NE, R, _ = w["L0_ffn_lora_A"].shape
    F = w["L0_ffn_wi"].shape[0]
    FC = F // P

    halves = np.array([2 * i + c for c in range(2) for i in range(D // 2)])
    q_cols = np.concatenate([h * D + halves for h in range(H)])
    k_cols = np.concatenate([(g * D + halves) * 2 for g in range(G)])
    v_cols = np.arange(G * D) * 2 + 1
    kv_cols = np.concatenate([k_cols, v_cols])

    inv_freq = (1.0 / np.float32(10000.0) ** (np.arange(0, D, 2, dtype=np.float32) / np.float32(D))).astype(np.float32)
    angle = np.outer(np.arange(S, dtype=np.float32), inv_freq).astype(np.float32)
    cos, sin = np.cos(angle).astype(np.float32), np.sin(angle).astype(np.float32)

    def by_token(a):
        return a.reshape(T, P, D).transpose(1, 0, 2).reshape(P, T * D)

    rank = np.tile(np.arange(NE, 0, -1, dtype=np.float32), (P, 1))
    arrays = {
        "x": x.reshape(B, T, P, E).transpose(0, 2, 1, 3),
        "w_q": np.concatenate([w["L0_attn_Wqa"].T, w["L0_attn_Wqb"][:, q_cols]], axis=1),
        "w_kv": np.concatenate([w["L0_attn_Wkva"].T, w["L0_attn_Wkvb"][:, kv_cols]], axis=1),
        "w_big": np.concatenate([
            w["L0_ffn_wi"].T,
            w["L0_ffn_lora_B"].transpose(0, 2, 1).reshape(NE * R, F),
            w["L0_ffn_wo"].T.reshape(FC, P, E).transpose(1, 0, 2).reshape(P, FC * E),
            w["L0_ffn_lora_A"].reshape(NE * R, E).T,
            w["L0_ffn_gate_w"].T,
            w["L0_attn_Wout"],
            w["L0_ffn_bi"].reshape(FC, P).T], axis=1),
        "rows": np.concatenate([w["L0_attn_bout"], w["L0_ffn_bo"], w["L0_ffn_gate_b"]])[None, :],
        "tables": np.concatenate([by_token(np.concatenate([cos, cos], axis=1)),
                                  by_token(np.concatenate([-sin, sin], axis=1)), rank], axis=1),
    }
    arrays = {k: np.ascontiguousarray(v) for k, v in arrays.items()}
    nc = bacc.Bacc("TRN2", target_bir_lowering=False, num_devices=1)
    args = [nc.dram_tensor(k, v.shape, mybir.dt.from_np(v.dtype), kind="ExternalInput").ap() for k, v in arrays.items()]
    y = nc.dram_tensor("y", (B, P, T, E), F32, kind="ExternalOutput").ap()
    bass_preln_attention_moe_lora(nc, *args, y)
    out = run_bass_kernel_spmd(nc, [arrays], core_ids=[0]).results[0]["y"]
    return out.reshape(B, P, T, E).transpose(0, 2, 1, 3).reshape(B, S, E)
```
